# Optimizing a Trainium2 kernel written in Bass

```python
import numpy as np
import jax
import jax.numpy as jnp

def _softmax(x, axis=-1):
    return jax.nn.softmax(x, axis=axis)

def _gelu(x):
    return jax.nn.gelu(x, approximate=True)

def _silu(x):
    return jax.nn.silu(x)

def _sigmoid(x):
    return jax.nn.sigmoid(x)

def _layernorm(x, axis=-1, eps=1e-05):
    m = jnp.mean(x, axis=axis, keepdims=True)
    v = jnp.var(x, axis=axis, keepdims=True)
    return (x - m) / jnp.sqrt(v + eps)

def _scatter_add(tgt, idx, src, axis=0):
    return tgt.at[idx].add(src)

def _segment_sum(src, seg, n):
    return jax.ops.segment_sum(src, seg, n)
kernel_name = 'mk_early_fusion_d2_tok_img1024_r4_189e80'

def setup_inputs(seed: int=0):
    np.random.seed(seed)
    _w = jnp.asarray

    def _rec_inputs():
        import jax
        import jax.numpy as jnp
        _rk = jax.random.key(seed)
        x = -0.000348323 + 0.999952 * jax.random.normal(jax.random.fold_in(_rk, 1), (32, 3, 224, 224), jnp.float32)
        txt = 7.22391e-06 + 0.554264 * jax.random.normal(jax.random.fold_in(_rk, 2), (32, 77, 256), jnp.float32)
        return (x, txt)
    x, txt = _rec_inputs()

    def _L0_tok_setup():
        import jax, jax.numpy as jnp
        import numpy as np
        PATCH = 16
        key = jax.random.key(seed)
        k1, k2 = jax.random.split(key)
        pixel_values = jax.random.normal(k1, (32, 3, 96, 96), dtype=jnp.float32)
        W = jax.random.normal(k2, (256, 3 * PATCH * PATCH), dtype=jnp.float32) * 0.02
        return {'pixel_values': pixel_values, 'W': W}
    _L0_tok_all = _L0_tok_setup()
    _L0_tok_in = {k: v for k, v in _L0_tok_all.items() if k in ('W',)}
    del _L0_tok_all

    def _L0_attn_setup():
        import jax, jax.numpy as jnp
        import numpy as np
        SEQ_LEN = 512
        DIM_EMB = 256
        DIM_K = 256
        DIM_V = 256
        BATCH = 4
        key = jax.random.key(seed)
        kx, kq, kk, kv, ko = jax.random.split(key, 5)
        s = DIM_EMB ** (-0.5)
        return {'x': jax.random.normal(kx, (BATCH, SEQ_LEN, DIM_EMB), dtype=jnp.float32), 'Wq': jax.random.normal(kq, (DIM_EMB, DIM_K), dtype=jnp.float32) * s, 'Wk': jax.random.normal(kk, (DIM_EMB, DIM_K), dtype=jnp.float32) * s, 'Wv': jax.random.normal(kv, (DIM_EMB, DIM_V), dtype=jnp.float32) * s, 'Wo': jax.random.normal(ko, (DIM_V, DIM_V), dtype=jnp.float32) * DIM_V ** (-0.5)}
    _L0_attn_all = _L0_attn_setup()
    _L0_attn_in = {k: v for k, v in _L0_attn_all.items() if k in ('Wq', 'Wk', 'Wv', 'Wo')}
    del _L0_attn_all

    def _L0_ffn_setup():
        import jax, jax.numpy as jnp
        import numpy as np
        BLOCK = 32
        W_BITS = 4
        ACT_BITS = 16

        def act_qdq(x):
            qmax = 2.0 ** (ACT_BITS - 1) - 1.0
            scale = jnp.maximum(jnp.max(jnp.abs(x)) / qmax, 1e-12)
            return jnp.clip(jnp.round(x / scale), -qmax - 1.0, qmax) * scale

        def fixed_qdq_u16(x):
            scale = 1.0 / 65536.0
            return jnp.clip(jnp.round(x / scale), 0.0, 65535.0) * scale

        def lpbq_dequant(w):
            O, I = w.shape
            qmax = 2.0 ** (W_BITS - 1) - 1.0
            wb = w.reshape(O, I // BLOCK, BLOCK)
            s = jnp.maximum(jnp.max(jnp.abs(wb), axis=-1, keepdims=True) / qmax, 1e-12)
            wq = jnp.clip(jnp.round(wb / s), -qmax - 1.0, qmax) * s
            return wq.reshape(O, I)
        key = jax.random.key(seed)
        k1, k2, k3, k4 = jax.random.split(key, 4)
        B, S, H, I = (2, 1024, 256, 768)
        x = jax.random.normal(k1, (B, S, H), jnp.float32)
        w_gate = jax.random.normal(k2, (I, H), jnp.float32) * 0.02
        w_up = jax.random.normal(k3, (I, H), jnp.float32) * 0.02
        w_down = jax.random.normal(k4, (H, I), jnp.float32) * 0.02
        return {'x': x, 'w_gate': w_gate, 'w_up': w_up, 'w_down': w_down}
    _L0_ffn_all = _L0_ffn_setup()
    _L0_ffn_in = {k: v for k, v in _L0_ffn_all.items() if k in ('w_gate', 'w_up', 'w_down')}
    del _L0_ffn_all

    def _L1_attn_setup():
        import math
        import jax, jax.numpy as jnp
        import numpy as np
        B, T, C = (2, 512, 256)
        H, N1, N2, N3 = (16, 6, 4, 6)
        HD = C // H

        def _rotary(T_, hd, dtype):
            inv_freq = 1.0 / 10000.0 ** (jnp.arange(0, hd, 2, dtype=jnp.float32) / hd)
            freqs = jnp.outer(jnp.arange(T_, dtype=jnp.float32), inv_freq)
            return (jnp.cos(freqs)[None, :, None, :].astype(dtype), jnp.sin(freqs)[None, :, None, :].astype(dtype))

        def _apply_rot(x, cos, sin):
            x1, x2 = (x[..., :x.shape[-1] // 2], x[..., x.shape[-1] // 2:])
            return jnp.concatenate([x1 * cos + x2 * sin, -x1 * sin + x2 * cos], axis=-1).astype(x.dtype)

        def _causal_bias(L, S, dtype):
            mask = jnp.triu(jnp.ones((L, S), bool), k=1)
            return jnp.where(mask, jnp.asarray(-jnp.inf, dtype), jnp.asarray(0.0, dtype))

        def _sdpa(q, k, v, scale):
            scores = jnp.einsum('bhtd,bhsd->bhts', q, k) * scale + _causal_bias(q.shape[-2], k.shape[-2], q.dtype)
            return jnp.einsum('bhts,bhsd->bhtd', jax.nn.softmax(scores, axis=-1), v)

        def _hyp_attn(q, k, v, curv):
            eps = 1e-06
            tq = jnp.sqrt(1.0 / curv + jnp.sum(q * q, axis=-1, keepdims=True))
            tk = jnp.sqrt(1.0 / curv + jnp.sum(k * k, axis=-1, keepdims=True))
            inner = jnp.einsum('bhtd,bhsd->bhts', q, k) - tq * jnp.swapaxes(tk, -1, -2)
            arg = jnp.maximum(-curv * inner, 1.0 + 1e-07)
            dis = jnp.sqrt(1.0 / curv) * jnp.arccosh(arg)
            scores = 1.0 / (eps + dis) + _causal_bias(q.shape[-2], k.shape[-2], q.dtype)
            return jnp.einsum('bhts,bhsd->bhtd', jax.nn.softmax(scores, axis=-1), v)
        key = jax.random.key(seed)
        k1, k2, k3 = jax.random.split(key, 3)
        return {'x': jax.random.normal(k1, (B, T, C), jnp.float32), 'qkv_w': jax.random.normal(k2, (3 * C, C), jnp.float32) * C ** (-0.5), 'proj_w': jax.random.normal(k3, (C, C), jnp.float32) * C ** (-0.5), 'proj_b': jnp.zeros((C,), jnp.float32), 'curvature': jnp.ones((1, N2, 1, 1), jnp.float32)}
    _L1_attn_all = _L1_attn_setup()
    _L1_attn_in = {k: v for k, v in _L1_attn_all.items() if k in ('qkv_w', 'proj_w', 'proj_b', 'curvature')}
    del _L1_attn_all

    def _L1_ffn_setup():
        import jax, jax.numpy as jnp
        import numpy as np
        H = 16
        EPS = 1e-05

        def layernorm(x, g, b):
            m = jnp.mean(x, axis=-1, keepdims=True)
            v = jnp.mean((x - m) ** 2, axis=-1, keepdims=True)
            return (x - m) * jax.lax.rsqrt(v + EPS) * g + b
        key = jax.random.key(seed)
        B, S, D, E = (4, 512, 256, 8)
        ks = jax.random.split(key, 16)
        s = 0.02
        inp = {'x': jax.random.normal(ks[0], (B, S, D), jnp.float32), 'Wq': jax.random.normal(ks[1], (D, D), jnp.float32) * s, 'bq': jnp.zeros((D,), jnp.float32), 'Wk': jax.random.normal(ks[2], (D, D), jnp.float32) * s, 'bk': jnp.zeros((D,), jnp.float32), 'Wv': jax.random.normal(ks[3], (D, D), jnp.float32) * s, 'bv': jnp.zeros((D,), jnp.float32), 'Wo': jax.random.normal(ks[4], (D, D), jnp.float32) * s, 'bo': jnp.zeros((D,), jnp.float32), 'g1': jnp.ones((D,), jnp.float32), 'be1': jnp.zeros((D,), jnp.float32), 'g2': jnp.ones((D,), jnp.float32), 'be2': jnp.zeros((D,), jnp.float32), 'Wg': jax.random.normal(ks[5], (D, E), jnp.float32) * s, 'bg': jnp.zeros((E,), jnp.float32), 'We': jax.random.normal(ks[6], (E, D, D), jnp.float32) * s, 'bexp': jnp.zeros((E, D), jnp.float32)}
        return inp
    _L1_ffn_all = _L1_ffn_setup()
    _L1_ffn_in = {k: v for k, v in _L1_ffn_all.items() if k in ('Wq', 'bq', 'Wk', 'bk', 'Wv', 'bv', 'Wo', 'bo', 'g1', 'be1', 'g2', 'be2', 'Wg', 'bg', 'We', 'bexp')}
    del _L1_ffn_all
    return {'x': x, 'txt': txt, 'L0_tok_W': _L0_tok_in['W'], 'L0_attn_Wq': _L0_attn_in['Wq'], 'L0_attn_Wk': _L0_attn_in['Wk'], 'L0_attn_Wv': _L0_attn_in['Wv'], 'L0_attn_Wo': _L0_attn_in['Wo'], 'L0_ffn_w_gate': _L0_ffn_in['w_gate'], 'L0_ffn_w_up': _L0_ffn_in['w_up'], 'L0_ffn_w_down': _L0_ffn_in['w_down'], 'L1_attn_qkv_w': _L1_attn_in['qkv_w'], 'L1_attn_proj_w': _L1_attn_in['proj_w'], 'L1_attn_proj_b': _L1_attn_in['proj_b'], 'L1_attn_curvature': _L1_attn_in['curvature'], 'L1_ffn_Wq': _L1_ffn_in['Wq'], 'L1_ffn_bq': _L1_ffn_in['bq'], 'L1_ffn_Wk': _L1_ffn_in['Wk'], 'L1_ffn_bk': _L1_ffn_in['bk'], 'L1_ffn_Wv': _L1_ffn_in['Wv'], 'L1_ffn_bv': _L1_ffn_in['bv'], 'L1_ffn_Wo': _L1_ffn_in['Wo'], 'L1_ffn_bo': _L1_ffn_in['bo'], 'L1_ffn_g1': _L1_ffn_in['g1'], 'L1_ffn_be1': _L1_ffn_in['be1'], 'L1_ffn_g2': _L1_ffn_in['g2'], 'L1_ffn_be2': _L1_ffn_in['be2'], 'L1_ffn_Wg': _L1_ffn_in['Wg'], 'L1_ffn_bg': _L1_ffn_in['bg'], 'L1_ffn_We': _L1_ffn_in['We'], 'L1_ffn_bexp': _L1_ffn_in['bexp']}

def reference(x, txt, L0_tok_W, L0_attn_Wq, L0_attn_Wk, L0_attn_Wv, L0_attn_Wo, L0_ffn_w_gate, L0_ffn_w_up, L0_ffn_w_down, L1_attn_qkv_w, L1_attn_proj_w, L1_attn_proj_b, L1_attn_curvature, L1_ffn_Wq, L1_ffn_bq, L1_ffn_Wk, L1_ffn_bk, L1_ffn_Wv, L1_ffn_bv, L1_ffn_Wo, L1_ffn_bo, L1_ffn_g1, L1_ffn_be1, L1_ffn_g2, L1_ffn_be2, L1_ffn_Wg, L1_ffn_bg, L1_ffn_We, L1_ffn_bexp):
    import jax
    import jax.numpy as jnp

    def _L0_tok_ref(pixel_values, W):
        import jax, jax.numpy as jnp
        import numpy as np
        PATCH = 16
        B, C, H, Wd = pixel_values.shape
        p = PATCH
        Hp, Wp = (H // p, Wd // p)
        x = pixel_values.reshape(B, C, Hp, p, Wp, p)
        x = x.transpose(0, 2, 4, 1, 3, 5).reshape(B, Hp * Wp, C * p * p)
        return jnp.einsum('bnk,hk->bnh', x, W)

    def _L0_attn_ref(x, Wq, Wk, Wv, Wo):
        import jax, jax.numpy as jnp
        import numpy as np
        SEQ_LEN = 512
        DIM_EMB = 256
        DIM_K = 256
        DIM_V = 256
        BATCH = 4
        q = jnp.einsum('bse,ek->bsk', x, Wq)
        k = jnp.einsum('bse,ek->bsk', x, Wk)
        v = jnp.einsum('bse,ev->bsv', x, Wv)
        scores = jnp.einsum('bqk,bsk->bqs', q, k)
        S = scores.shape[-1]
        causal_mask = jnp.triu(jnp.ones((S, S), dtype=bool), k=1)
        scores = jnp.where(causal_mask[None], -jnp.inf, scores)
        attn = jax.nn.softmax(scores * Wq.shape[1] ** (-0.5), axis=-1)
        out = jnp.einsum('bqs,bsv->bqv', attn, v)
        return jnp.einsum('bqv,vo->bqo', out, Wo)

    def _L0_ffn_ref(x, w_gate, w_up, w_down):
        import jax, jax.numpy as jnp
        import numpy as np
        BLOCK = 32
        W_BITS = 4
        ACT_BITS = 16

        def act_qdq(x):
            qmax = 2.0 ** (ACT_BITS - 1) - 1.0
            scale = jnp.maximum(jnp.max(jnp.abs(x)) / qmax, 1e-12)
            return jnp.clip(jnp.round(x / scale), -qmax - 1.0, qmax) * scale

        def fixed_qdq_u16(x):
            scale = 1.0 / 65536.0
            return jnp.clip(jnp.round(x / scale), 0.0, 65535.0) * scale

        def lpbq_dequant(w):
            O, I = w.shape
            qmax = 2.0 ** (W_BITS - 1) - 1.0
            wb = w.reshape(O, I // BLOCK, BLOCK)
            s = jnp.maximum(jnp.max(jnp.abs(wb), axis=-1, keepdims=True) / qmax, 1e-12)
            wq = jnp.clip(jnp.round(wb / s), -qmax - 1.0, qmax) * s
            return wq.reshape(O, I)
        x = act_qdq(x)
        up = act_qdq(x @ lpbq_dequant(w_up).T)
        gate = act_qdq(x @ lpbq_dequant(w_gate).T)
        sig = fixed_qdq_u16(jax.nn.sigmoid(gate))
        gate = act_qdq(gate * sig)
        o = act_qdq(gate * up)
        return o @ lpbq_dequant(w_down).T

    def _L1_attn_ref(x, qkv_w, proj_w, proj_b, curvature):
        import math
        import jax, jax.numpy as jnp
        import numpy as np
        B, T, C = (2, 512, 256)
        H, N1, N2, N3 = (16, 6, 4, 6)
        HD = C // H

        def _rotary(T_, hd, dtype):
            inv_freq = 1.0 / 10000.0 ** (jnp.arange(0, hd, 2, dtype=jnp.float32) / hd)
            freqs = jnp.outer(jnp.arange(T_, dtype=jnp.float32), inv_freq)
            return (jnp.cos(freqs)[None, :, None, :].astype(dtype), jnp.sin(freqs)[None, :, None, :].astype(dtype))

        def _apply_rot(x, cos, sin):
            x1, x2 = (x[..., :x.shape[-1] // 2], x[..., x.shape[-1] // 2:])
            return jnp.concatenate([x1 * cos + x2 * sin, -x1 * sin + x2 * cos], axis=-1).astype(x.dtype)

        def _causal_bias(L, S, dtype):
            mask = jnp.triu(jnp.ones((L, S), bool), k=1)
            return jnp.where(mask, jnp.asarray(-jnp.inf, dtype), jnp.asarray(0.0, dtype))

        def _sdpa(q, k, v, scale):
            scores = jnp.einsum('bhtd,bhsd->bhts', q, k) * scale + _causal_bias(q.shape[-2], k.shape[-2], q.dtype)
            return jnp.einsum('bhts,bhsd->bhtd', jax.nn.softmax(scores, axis=-1), v)

        def _hyp_attn(q, k, v, curv):
            eps = 1e-06
            tq = jnp.sqrt(1.0 / curv + jnp.sum(q * q, axis=-1, keepdims=True))
            tk = jnp.sqrt(1.0 / curv + jnp.sum(k * k, axis=-1, keepdims=True))
            inner = jnp.einsum('bhtd,bhsd->bhts', q, k) - tq * jnp.swapaxes(tk, -1, -2)
            arg = jnp.maximum(-curv * inner, 1.0 + 1e-07)
            dis = jnp.sqrt(1.0 / curv) * jnp.arccosh(arg)
            scores = 1.0 / (eps + dis) + _causal_bias(q.shape[-2], k.shape[-2], q.dtype)
            return jnp.einsum('bhts,bhsd->bhtd', jax.nn.softmax(scores, axis=-1), v)
        Bx, Tx, Cx = x.shape
        qkv = x @ qkv_w.T
        q, k, v = jnp.split(qkv, 3, axis=-1)
        q = q.reshape(Bx, Tx, H, HD)
        k = k.reshape(Bx, Tx, H, HD)
        v = v.reshape(Bx, Tx, H, HD)
        cos, sin = _rotary(Tx, HD, x.dtype)
        q = _apply_rot(q, cos, sin)
        k = _apply_rot(k, cos, sin)
        q, k, v = (jnp.swapaxes(t, 1, 2) for t in (q, k, v))
        outs = []
        outs.append(_sdpa(q[:, :N1], k[:, :N1], v[:, :N1], 1.0 / math.sqrt(HD)))
        outs.append(_hyp_attn(q[:, N1:N1 + N2], k[:, N1:N1 + N2], v[:, N1:N1 + N2], curvature))
        qn = q[:, N1 + N2:] / jnp.maximum(jnp.linalg.norm(q[:, N1 + N2:], axis=-1, keepdims=True), 1e-12)
        kn = k[:, N1 + N2:] / jnp.maximum(jnp.linalg.norm(k[:, N1 + N2:], axis=-1, keepdims=True), 1e-12)
        outs.append(_sdpa(qn, kn, v[:, N1 + N2:], math.sqrt(HD)))
        y = jnp.concatenate(outs, axis=1)
        y = jnp.swapaxes(y, 1, 2).reshape(Bx, Tx, Cx)
        return y @ proj_w.T + proj_b

    def _L1_ffn_ref(x, Wq, bq, Wk, bk, Wv, bv, Wo, bo, g1, be1, g2, be2, Wg, bg, We, bexp):
        import jax, jax.numpy as jnp
        import numpy as np
        H = 16
        EPS = 1e-05

        def layernorm(x, g, b):
            m = jnp.mean(x, axis=-1, keepdims=True)
            v = jnp.mean((x - m) ** 2, axis=-1, keepdims=True)
            return (x - m) * jax.lax.rsqrt(v + EPS) * g + b
        B, S, D = x.shape
        Dh = D // H
        TOP_K = 2
        q = (x @ Wq + bq).reshape(B, S, H, Dh)
        k = (x @ Wk + bk).reshape(B, S, H, Dh)
        v = (x @ Wv + bv).reshape(B, S, H, Dh)
        scores = jnp.einsum('bqhd,bkhd->bhqk', q, k) / jnp.sqrt(jnp.float32(Dh))
        attn = jax.nn.softmax(scores, axis=-1)
        ctx = jnp.einsum('bhqk,bkhd->bqhd', attn, v).reshape(B, S, D)
        attn_out = ctx @ Wo + bo
        x = x + layernorm(attn_out, g1, be1)
        gate_probs = jax.nn.softmax(x @ Wg + bg, axis=-1)
        top_vals, top_idx = jax.lax.top_k(gate_probs, TOP_K)
        all_out = jnp.einsum('bsd,edf->bsef', x, We) + bexp
        picked = jnp.take_along_axis(all_out, top_idx[..., None], axis=2)
        moe_out = jnp.sum(top_vals[..., None] * picked, axis=2)
        return x + layernorm(moe_out, g2, be2)
    h = _L0_tok_ref(x, L0_tok_W)
    h = jnp.concatenate([h, txt], axis=1)
    h = h + _L0_attn_ref(_layernorm(h, axis=-1), L0_attn_Wq, L0_attn_Wk, L0_attn_Wv, L0_attn_Wo)
    h = h + _L0_ffn_ref(_layernorm(h, axis=-1), L0_ffn_w_gate, L0_ffn_w_up, L0_ffn_w_down)
    h = h + _L1_attn_ref(_layernorm(h, axis=-1), L1_attn_qkv_w, L1_attn_proj_w, L1_attn_proj_b, L1_attn_curvature)
    h = h + _L1_ffn_ref(_layernorm(h, axis=-1), L1_ffn_Wq, L1_ffn_bq, L1_ffn_Wk, L1_ffn_bk, L1_ffn_Wv, L1_ffn_bv, L1_ffn_Wo, L1_ffn_bo, L1_ffn_g1, L1_ffn_be1, L1_ffn_g2, L1_ffn_be2, L1_ffn_Wg, L1_ffn_bg, L1_ffn_We, L1_ffn_bexp)
    return h

_drawn_inputs = setup_inputs


def setup_inputs(seed=0):
    import zlib

    import numpy as np

    out = dict(_drawn_inputs(seed))
    spreads = {'L1_attn_proj_b': (0.0, 0.1),
     'L1_attn_curvature': (1.0, 0.6),
     'L1_ffn_bq': (0.0, 0.398),
     'L1_ffn_bk': (0.0, 0.8),
     'L1_ffn_bv': (0.0, 0.1),
     'L1_ffn_bo': (0.0, 0.1),
     'L1_ffn_g1': (1.0, 0.2),
     'L1_ffn_be1': (0.0, 0.1),
     'L1_ffn_g2': (1.0, 0.2),
     'L1_ffn_be2': (0.0, 0.1),
     'L1_ffn_bg': (0.0, 0.1),
     'L1_ffn_bexp': (0.0, 0.1)}
    factors = {}
    for name, (base, spread) in spreads.items():
        noise = np.random.default_rng([zlib.crc32(name.encode()), seed]).standard_normal(out[name].shape)
        drawn = base * np.exp(spread * noise) if base else spread * noise
        out[name] = jnp.asarray(drawn.astype(out[name].dtype))
    for name, factor in factors.items():
        out[name] = (out[name] * factor).astype(out[name].dtype)
    return out
```

```python
import numpy as np
import concourse.bass as bass
from concourse import mybir
from contextlib import ExitStack

F32 = mybir.dt.float32
BF16 = mybir.dt.bfloat16
ALU = mybir.AluOpType
ACT = mybir.ActivationFunctionType
AX = mybir.AxisListType

D = 256
CT = D // 128
PATCHES, TEXT = 196, 77
T = PATCHES + TEXT
R = 91
NT = T // R
P_LAST = PATCHES - (NT - 1) * R
KP = 768 // 128
FF = 768
FT = FF // 128
QBLOCK = 32
H, HD = 16, 16
EXPERTS = 8
EPS = 1e-5
NEG = -1e30
MAGIC = 12582912.0
QMAX = 32767.0


class Signal:

    def __init__(self, ctx, nc, name, per=1):
        self.sem, self.per = nc.alloc_semaphore(name), per

    def give(self, engine):
        engine.sem_inc(self.sem, 2 * self.per)

    def at(self, n, count=None):
        return n * self.per + 2 * self.per + (self.per if count is None else count)

    def before(self, n):
        return n * self.per + self.per


def signals(ctx, nc, prefix, **pers):
    return {k: Signal(ctx, nc, f"{prefix}_{k}", per) for k, per in pers.items()}


def setup_constants(nc, ctx, rot_dram):
    c = {}
    for name, shape, dt in (("ident", [128, 128], F32), ("identb", [128, 128], BF16),
                            ("mask_qk", [R, R], BF16), ("mask_kq", [R, R], BF16),
                            ("minus_half", [R, 64], F32), ("eps", [R, NT], F32),
                            ("cos", [R, NT, HD], F32), ("sin", [R, NT, HD], F32)):
        c[name] = ctx.enter_context(nc.sbuf_tensor("c_" + name, shape, dt))
    filled = nc.alloc_semaphore("const_filled")
    loaded = nc.alloc_semaphore("const_loaded")
    with nc.Block() as block:
        @block.gpsimd
        def _(pool):
            fills = (("ident", 0.0), ("identb", 0.0), ("mask_qk", 0.0), ("mask_kq", 0.0),
                     ("minus_half", -0.5), ("eps", EPS))
            for name, value in fills:
                nc.gpsimd.memset(c[name][:], value).then_inc(filled, 1)
            pool.wait_ge(filled, len(fills))
            for name in ("ident", "identb"):
                nc.gpsimd.affine_select(out=c[name][:], in_=c[name][:], compare_op=ALU.not_equal,
                                        fill=1.0, base=0, pattern=[[-1, 128]], channel_multiplier=1)
            nc.gpsimd.affine_select(out=c["mask_qk"][:], in_=c["mask_qk"][:], compare_op=ALU.is_ge,
                                    fill=NEG, base=0, pattern=[[-1, R]], channel_multiplier=1)
            nc.gpsimd.affine_select(out=c["mask_kq"][:], in_=c["mask_kq"][:], compare_op=ALU.is_ge,
                                    fill=NEG, base=0, pattern=[[1, R]], channel_multiplier=-1)

        @block.sync
        def _(sp):
            for k, name in enumerate(("cos", "sin")):
                sp.dma_start(c[name][:], rot_dram[k].rearrange("(t p) d -> p t d", p=R)).then_inc(loaded, 16)
            sp.wait_ge(loaded, 32)
    return c


def ln_stats(nc, dve, x, stats, mv, bn, s_mv):
    for t in range(NT):
        nc.vector.bn_stats(stats[:, t, :], x[:, t, :]).then_inc(bn[0], 1)
    dve.wait_ge(bn[0], bn[1] - 1)
    dve.sem_inc(bn[0], 1)
    for t in range(NT):
        last = nc.vector.bn_aggr(mv[:, t, :], stats[:, t, :])
    last.then_inc(s_mv.sem, 1)


def ln_apply(nc, out, x, mv, rstd, done):
    for t in range(NT):
        nc.vector.tensor_scalar(out[:, t, :], x[:, t, :], mv[:, t, 0:1], rstd[:, t:t + 1],
                                ALU.subtract, ALU.mult).then_inc(done.sem, 1)


def ln_rstd(nc, pool, c, mv, var_eps, rstd, s_mv, s_eps, s_rstd, n):
    pool.wait_ge(s_mv.sem, s_mv.at(n))
    pool.wait_ge(s_rstd.sem, s_rstd.before(n))
    nc.gpsimd.tensor_tensor(var_eps[:], mv[:, :, 1], c["eps"][:, 0:NT], ALU.add).then_inc(s_eps.sem, 1)
    pool.wait_ge(s_eps.sem, s_eps.at(n))
    nc.gpsimd.tensor_tensor(rstd[:], var_eps[:], c["minus_half"][:, 0:NT], ALU.pow).then_inc(s_rstd.sem, 1)


def transpose_tokens(nc, pe, c, x, banks):
    for ct in range(CT):
        for t in range(NT):
            last = nc.tensor.transpose(banks(ct)[:, t * R:(t + 1) * R],
                                       x[:, t, ct * 128:(ct + 1) * 128], c["ident"][0:R, 0:R])
    return last


def phase_a(nc, c, ps, NB, patches_dram, txt_dram, wtok_dram, wq_dram, wk_dram, wv_dram, wo_dram,
            h1_dram, x0_dram, amax_x):
    ctx = ExitStack()
    with ctx:
        def sb(name, shape, dt=F32):
            return ctx.enter_context(nc.sbuf_tensor("a_" + name, shape, dt))

        def sem(name):
            return nc.alloc_semaphore("a_" + name)

        wtok = sb("wtok", [128, KP, D])
        wq, wk, wv, wo = (sb(n, [128, CT, D]) for n in ("wq", "wk", "wv", "wo"))
        patches = sb("patches", [128, 2, KP, PATCHES])
        h = sb("h", [R, 2, NT, D])
        stats = sb("stats", [R, 2, NT, 6])
        mv = sb("mv", [R, 2, NT, 2])
        var_eps = sb("var_eps", [R, 2, NT])
        rstd = sb("rstd", [R, 2, NT])
        xn = sb("xn", [R, 2, NT, D])
        xT = sb("xT", [128, 2, CT, T])
        qT = sb("qT", [128, 2, CT, T])
        kT = sb("kT", [128, 2, CT, T])
        v = sb("v", [R, 2, NT, D])
        mx = sb("mx", [R, 2, NT])
        nb = sb("nb", [R, 2, NT])
        prob = sb("prob", [R, 2, NT, T])
        den = sb("den", [R, 2, NT])
        rden = sb("rden", [R, 2, NT])
        probT = sb("probT", [R, 2, 2, T])
        aT = sb("aT", [128, 2, CT, T])
        x0T = sb("x0T", [128, 2, CT, T])
        amax_new = sb("amax_new", [R, 2, 1])

        w_loaded = sem("w_loaded")
        patches_loaded = [sem(f"patches_loaded{u}") for u in range(2)]
        txt_loaded = [sem(f"txt_loaded{u}") for u in range(2)]
        h1_stored = [sem(f"h1_stored{u}") for u in range(2)]
        x0_stored = [sem(f"x0_stored{u}") for u in range(2)]
        amax_step = sem("amax_step")
        S = signals(ctx, nc, "a", tok=1, tok_out=2, bn=NT + 1, mv=1, eps=1, rstd=1, xn=NT, xT=1, xT_out=1,
                    qk=1, qk_out=2, v=1, v_out=1, s=NT, mx=NT, nb=1, p=NT, pT=1, pT_out=1, a=1,
                    a_out=1, rden=1, y=1, h1=1, bn2=NT + 1, mv2=1, eps2=1, rstd2=1, x0=NT, x0T=1, x0T_out=1,
                    amr=1, amax=1)
        banks = [lambda k, u=u: ps[:, 4 * u + k, :] for u in range(2)]
        causal = {0: (1, 182), 1: (1, 0), 2: (0, 0)}
        scale = float(D) ** -0.5

        block = ctx.enter_context(nc.Block())

        @block.sync
        def _(sp):
            def load_patches(n, u):
                sp.dma_start(patches[:, u], patches_dram[n].rearrange("(k p) n -> p k n", p=128))\
                    .then_inc(patches_loaded[u], 16)

            def load_text(n, u):
                sp.dma_start(h[P_LAST:R, u, NT - 1, :], txt_dram[n]).then_inc(txt_loaded[u], 16)

            def pair(i, more):
                for u in range(2):
                    n = 2 * i + u
                    if more:
                        sp.wait_ge(S["tok"].sem, S["tok"].at(n))
                        load_patches(n + 2, u)
                for u in range(2):
                    n = 2 * i + u
                    sp.wait_ge(S["h1"].sem, S["h1"].at(n))
                    sp.dma_start(h1_dram[n].rearrange("(t p) d -> p t d", p=R), h[:, u])\
                        .then_inc(h1_stored[u], 16)
                for u in range(2):
                    n = 2 * i + u
                    if more:
                        sp.wait_ge(S["x0"].sem, S["x0"].at(n))
                        sp.wait_ge(h1_stored[u], 16 * i + 16)
                        load_text(n + 2, u)
                    sp.wait_ge(S["x0T_out"].sem, S["x0T_out"].at(n))
                    sp.dma_start(x0_dram[n].rearrange("(c p) t -> p c t", p=128), x0T[:, u])\
                        .then_inc(x0_stored[u], 16)

            sp.dma_start(wtok[:], wtok_dram.rearrange("(k p) n -> p k n", p=128)).then_inc(w_loaded, 16)
            for w, dram in ((wq, wq_dram), (wk, wk_dram), (wv, wv_dram), (wo, wo_dram)):
                sp.dma_start(w[:], dram.rearrange("(k p) n -> p k n", p=128)).then_inc(w_loaded, 16)
            for u in range(2):
                load_patches(u, u)
                load_text(u, u)
            with sp.Fori(0, NB // 2 - 1) as i:
                pair(i, True)
            pair(NB // 2 - 1, False)
            for u in range(2):
                sp.wait_ge(h1_stored[u], 16 * (NB // 2))
                sp.wait_ge(x0_stored[u], 16 * (NB // 2))

        @block.gpsimd
        def _(pool):
            for k in ("eps", "rstd", "eps2", "rstd2"):
                S[k].give(pool)
            with pool.Fori(0, NB // 2) as i:
                for u in range(2):
                    ln_rstd(nc, pool, c, mv[:, u], var_eps[:, u], rstd[:, u],
                            S["mv"], S["eps"], S["rstd"], 2 * i + u)
                for u in range(2):
                    ln_rstd(nc, pool, c, mv[:, u], var_eps[:, u], rstd[:, u],
                            S["mv2"], S["eps2"], S["rstd2"], 2 * i + u)

        @block.scalar
        def _(act):
            for k in ("tok_out", "xT_out", "v_out", "p", "a_out", "x0T_out"):
                S[k].give(act)
            with act.Fori(0, NB // 2) as i:
                for u in range(2):
                    n, B = 2 * i + u, banks[u]
                    act.wait_ge(S["tok"].sem, S["tok"].at(n))
                    act.wait_ge(S["x0"].sem, S["x0"].before(n))
                    act.wait_ge(h1_stored[u], 16 * i)
                    nc.scalar.copy(h[:, u, 0:2, :], B(0)[0:R, :].rearrange("p (t d) -> p t d", t=2))\
                        .then_inc(S["tok_out"].sem, 1)
                    nc.scalar.copy(h[0:P_LAST, u, 2, :], B(1)[0:P_LAST, 0:D]).then_inc(S["tok_out"].sem, 1)
                for u in range(2):
                    n, B = 2 * i + u, banks[u]
                    act.wait_ge(S["xT"].sem, S["xT"].at(n))
                    act.wait_ge(S["v"].sem, S["v"].before(n))
                    nc.scalar.copy(xT[:, u], ps[:, 4 * u + 2:4 * u + 4, 0:T]).then_inc(S["xT_out"].sem, 1)
                for u in range(2):
                    n, B = 2 * i + u, banks[u]
                    act.wait_ge(S["v"].sem, S["v"].at(n))
                    act.wait_ge(S["a"].sem, S["a"].before(n))
                    nc.scalar.copy(v[:, u, 0:2, :], B(0)[0:R, :].rearrange("p (t d) -> p t d", t=2))
                    nc.scalar.copy(v[:, u, 2, :], B(1)[0:R, 0:D]).then_inc(S["v_out"].sem, 1)
                for u in range(2):
                    n = 2 * i + u
                    act.wait_ge(S["nb"].sem, S["nb"].at(n))
                    act.wait_ge(S["pT"].sem, S["pT"].before(n))
                    act.wait_ge(S["rden"].sem, S["rden"].before(n))
                    for t in range(NT):
                        bank, col = causal[t]
                        w = (t + 1) * R
                        nc.scalar.activation(prob[:, u, t, 0:w], banks[u](bank + 2)[0:R, col:col + w], ACT.Exp,
                                             bias=nb[:, u, t:t + 1], scale=scale,
                                             accum_out=den[:, u, t:t + 1]).then_inc(S["p"].sem, 1)
                for u in range(2):
                    n = 2 * i + u
                    act.wait_ge(S["a"].sem, S["a"].at(n))
                    act.wait_ge(S["y"].sem, S["y"].before(n))
                    nc.scalar.copy(aT[:, u], ps[:, 4 * u + 2:4 * u + 4, 0:T]).then_inc(S["a_out"].sem, 1)
                for u in range(2):
                    n = 2 * i + u
                    act.wait_ge(S["x0T"].sem, S["x0T"].at(n))
                    act.wait_ge(x0_stored[u], 16 * i)
                    nc.scalar.copy(x0T[:, u], ps[:, 4 * u + 2:4 * u + 4, 0:T]).then_inc(S["x0T_out"].sem, 1)

        @block.vector
        def _(dve):
            for k in ("bn", "mv", "xn", "qk_out", "mx", "nb", "pT_out", "rden", "h1", "bn2", "mv2", "x0",
                      "amr", "amax"):
                S[k].give(dve)
            nc.vector.memset(amax_x[:], 0.0).then_inc(amax_step, 1)
            dve.wait_ge(amax_step, 1)
            with dve.Fori(0, NB // 2) as i:
                for u in range(2):
                    n = 2 * i + u
                    dve.wait_ge(S["tok_out"].sem, S["tok_out"].at(n))
                    dve.wait_ge(txt_loaded[u], 16 * i + 16)
                    dve.wait_ge(S["x0"].sem, S["x0"].before(n))
                    dve.wait_ge(S["rstd2"].sem, S["rstd2"].before(n))
                    ln_stats(nc, dve, h[:, u], stats[:, u], mv[:, u], (S["bn"].sem, S["bn"].at(n)), S["mv"])
                for u in range(2):
                    n = 2 * i + u
                    dve.wait_ge(S["rstd"].sem, S["rstd"].at(n))
                    dve.wait_ge(S["x0T"].sem, S["x0T"].before(n))
                    dve.wait_ge(S["amr"].sem, S["amr"].before(n))
                    ln_apply(nc, xn[:, u], h[:, u], mv[:, u], rstd[:, u], S["xn"])
                for u in range(2):
                    n = 2 * i + u
                    dve.wait_ge(S["qk"].sem, S["qk"].at(n))
                    dve.wait_ge(S["s"].sem, S["s"].before(n))
                    nc.vector.tensor_copy(qT[:, u], ps[:, 4 * u:4 * u + 2, 0:T]).then_inc(S["qk_out"].sem, 1)
                    nc.vector.tensor_copy(kT[:, u], ps[:, 4 * u + 2:4 * u + 4, 0:T]).then_inc(S["qk_out"].sem, 1)
                for u in range(2):
                    n = 2 * i + u
                    dve.wait_ge(S["s"].sem, S["s"].at(n))
                    dve.wait_ge(S["nb"].sem, S["nb"].before(n))
                    for t in range(NT):
                        bank, col = causal[t]
                        nc.vector.reduce_max(mx[:, u, t:t + 1], banks[u](bank + 2)[0:R, col:col + (t + 1) * R], AX.X)\
                            .then_inc(S["mx"].sem, 1)
                    dve.wait_ge(S["mx"].sem, S["mx"].at(n))
                    dve.wait_ge(S["p"].sem, S["p"].before(n))
                    nc.vector.tensor_scalar(nb[:, u], mx[:, u], -scale, None, ALU.mult).then_inc(S["nb"].sem, 1)
                for u in range(2):
                    n = 2 * i + u
                    dve.wait_ge(S["pT"].sem, S["pT"].at(n))
                    dve.wait_ge(S["a"].sem, S["a"].before(n))
                    nc.vector.tensor_copy(probT[:, u], ps[0:R, 4 * u:4 * u + 2, 0:T]).then_inc(S["pT_out"].sem, 1)
                    dve.wait_ge(S["p"].sem, S["p"].at(n))
                    nc.vector.reciprocal(rden[:, u], den[:, u]).then_inc(S["rden"].sem, 1)
                for u in range(2):
                    n, B = 2 * i + u, banks[u]
                    dve.wait_ge(S["y"].sem, S["y"].at(n))
                    dve.wait_ge(S["rden"].sem, S["rden"].at(n))
                    dve.wait_ge(S["xn"].sem, S["xn"].at(n))
                    for t in range(NT):
                        y = B(t // 2)[0:R, (t % 2) * D:(t % 2 + 1) * D]
                        last = nc.vector.scalar_tensor_tensor(out=h[:, u, t, :], in0=y, scalar=rden[:, u, t:t + 1],
                                                              in1=h[:, u, t, :], op0=ALU.mult, op1=ALU.add)
                    last.then_inc(S["h1"].sem, 1)
                for u in range(2):
                    n = 2 * i + u
                    dve.wait_ge(S["h1"].sem, S["h1"].at(n))
                    ln_stats(nc, dve, h[:, u], stats[:, u], mv[:, u], (S["bn2"].sem, S["bn2"].at(n)), S["mv2"])
                for u in range(2):
                    n = 2 * i + u
                    dve.wait_ge(S["rstd2"].sem, S["rstd2"].at(n))
                    dve.wait_ge(S["xT"].sem, S["xT"].at(n))
                    ln_apply(nc, xn[:, u], h[:, u], mv[:, u], rstd[:, u], S["x0"])
                for u in range(2):
                    n = 2 * i + u
                    dve.wait_ge(S["x0"].sem, S["x0"].at(n))
                    dve.wait_ge(S["amax"].sem, S["amax"].before(n))
                    nc.vector.tensor_reduce(amax_new[:, u], xn[:, u].rearrange("p t d -> p (t d)"), AX.X, ALU.max,
                                            apply_absolute_value=True).then_inc(S["amr"].sem, 1)
                    dve.wait_ge(S["amr"].sem, S["amr"].at(n))
                    nc.vector.tensor_tensor(amax_x[:, u:u + 1], amax_x[:, u:u + 1], amax_new[:, u], ALU.max)\
                        .then_inc(S["amax"].sem, 1)

        @block.tensor
        def _(pe):
            for k in ("tok", "xT", "qk", "v", "s", "pT", "a", "y", "x0T"):
                S[k].give(pe)
            pe.wait_ge(w_loaded, 16 * 5)
            with pe.Fori(0, NB // 2) as i:
                for u in range(2):
                    n, B = 2 * i + u, banks[u]
                    pe.wait_ge(patches_loaded[u], 16 * i + 16)
                    pe.wait_ge(S["h1"].sem, S["h1"].before(n))
                    for t in range(NT):
                        m = R if t < NT - 1 else P_LAST
                        for k in range(KP):
                            last = nc.tensor.matmul(B(t // 2)[0:m, (t % 2) * D:(t % 2 + 1) * D],
                                                    patches[:, u, k, t * R:t * R + m], wtok[:, k, :],
                                                    start=(k == 0), stop=(k == KP - 1))
                    last.then_inc(S["tok"].sem, 1)
                for u in range(2):
                    n, B = 2 * i + u, banks[u]
                    pe.wait_ge(S["xn"].sem, S["xn"].at(n))
                    pe.wait_ge(S["x0T_out"].sem, S["x0T_out"].before(n))
                    transpose_tokens(nc, pe, c, xn[:, u], lambda k: B(2 + k)).then_inc(S["xT"].sem, 1)
                for u in range(2):
                    n, B = 2 * i + u, banks[u]
                    pe.wait_ge(S["xT_out"].sem, S["xT_out"].at(n))
                    pe.wait_ge(S["tok_out"].sem, S["tok_out"].at(n))
                    for m in range(2 * CT):
                        w = (wq, wk)[m // CT]
                        for k in range(CT):
                            last = nc.tensor.matmul(B(m)[:, 0:T], w[:, k, (m % CT) * 128:(m % CT + 1) * 128],
                                                    xT[:, u, k, :], start=(k == 0), stop=(k == CT - 1))
                    last.then_inc(S["qk"].sem, 1)
                for u in range(2):
                    n, B = 2 * i + u, banks[u]
                    pe.wait_ge(S["qk_out"].sem, S["qk_out"].at(n, 1))
                    for t in range(NT):
                        for k in range(CT):
                            last = nc.tensor.matmul(B(t // 2)[0:R, (t % 2) * D:(t % 2 + 1) * D],
                                                    xT[:, u, k, t * R:(t + 1) * R], wv[:, k, :],
                                                    start=(k == 0), stop=(k == CT - 1))
                    last.then_inc(S["v"].sem, 1)
                for u in range(2):
                    n, B = 2 * i + u, banks[u]
                    pe.wait_ge(S["qk_out"].sem, S["qk_out"].at(n))
                    for t in range(NT):
                        bank, col = causal[t]
                        w = (t + 1) * R
                        for k in range(CT):
                            last = nc.tensor.matmul(B(bank + 2)[0:R, col:col + w], qT[:, u, k, t * R:(t + 1) * R],
                                                    kT[:, u, k, 0:w], start=(k == 0), stop=(k == CT - 1))
                            if k == 0:
                                nc.tensor.matmul(B(bank + 2)[0:R, col + t * R:col + w], c["identb"][0:R, 0:R],
                                                 c["mask_qk"][:], start=False, stop=False, skip_group_check=True)
                        last.then_inc(S["s"].sem, 1)
                for u in range(2):
                    n, B = 2 * i + u, banks[u]
                    pe.wait_ge(S["p"].sem, S["p"].at(n))
                    pe.wait_ge(S["v_out"].sem, S["v_out"].at(n))
                    for k in range(NT):
                        for t in range(k, NT):
                            out = B(0)[0:R, t * R:(t + 1) * R] if k == 0 else \
                                B(1)[0:R, ((k - 1) * 2 + t - k) * R:((k - 1) * 2 + t - k + 1) * R]
                            last = nc.tensor.transpose(out, prob[:, u, t, k * R:(k + 1) * R], c["ident"][0:R, 0:R])
                    last.then_inc(S["pT"].sem, 1)
                for u in range(2):
                    n, B = 2 * i + u, banks[u]
                    pe.wait_ge(S["pT_out"].sem, S["pT_out"].at(n))
                    for m in range(CT):
                        for k in range(NT):
                            moving = probT[:, u, 0, :] if k == 0 else \
                                probT[:, u, 1, (k - 1) * 2 * R:(k - 1) * 2 * R + (NT - k) * R]
                            last = nc.tensor.matmul(B(2 + m)[:, k * R:T], v[:, u, k, m * 128:(m + 1) * 128],
                                                    moving, start=(k == 0), stop=(k == NT - 1))
                    last.then_inc(S["a"].sem, 1)
                for u in range(2):
                    n, B = 2 * i + u, banks[u]
                    pe.wait_ge(S["a_out"].sem, S["a_out"].at(n))
                    for t in range(NT):
                        for k in range(CT):
                            last = nc.tensor.matmul(B(t // 2)[0:R, (t % 2) * D:(t % 2 + 1) * D],
                                                    aT[:, u, k, t * R:(t + 1) * R], wo[:, k, :],
                                                    start=(k == 0), stop=(k == CT - 1))
                    last.then_inc(S["y"].sem, 1)
                for u in range(2):
                    n, B = 2 * i + u, banks[u]
                    pe.wait_ge(S["x0"].sem, S["x0"].at(n))
                    transpose_tokens(nc, pe, c, xn[:, u], lambda k: B(2 + k)).then_inc(S["x0T"].sem, 1)


def quantise_weights(nc, c, ps, gate_dram, up_dram, down_dram, gateT, upT, downT):
    ctx = ExitStack()
    NBLK = FT * D // QBLOCK
    srcs = ((gate_dram, gateT, FT, CT), (up_dram, upT, FT, CT), (down_dram, downT, CT, FT))
    with ctx:
        w = ctx.enter_context(nc.sbuf_tensor("q_w", [128, 3, NBLK, QBLOCK], F32))
        step = ctx.enter_context(nc.sbuf_tensor("q_step", [128, 3, NBLK], F32))
        inv = ctx.enter_context(nc.sbuf_tensor("q_inv", [128, 3, NBLK], F32))
        loaded = [nc.alloc_semaphore(f"q_loaded{k}") for k in range(3)]
        chain = nc.alloc_semaphore("q_chain")
        done = nc.alloc_semaphore("q_done")
        turned = nc.alloc_semaphore("q_turned")
        out = nc.alloc_semaphore("q_out")
        block = ctx.enter_context(nc.Block())

        @block.sync
        def _(sp):
            for k, (dram, _, ot, _) in enumerate(srcs):
                sp.dma_start(w[:, k].rearrange("p b q -> p (b q)").rearrange("p (o i) -> p o i", o=ot),
                             dram.rearrange("(o p) i -> p o i", p=128)).then_inc(loaded[k], 16)

        @block.vector
        def _(dve):
            for k in range(3):
                def wide(a):
                    return a[:, k, :].unsqueeze(2).to_broadcast([128, NBLK, QBLOCK])

                dve.wait_ge(loaded[k], 16)
                nc.vector.tensor_reduce(step[:, k], w[:, k], AX.X, ALU.max, apply_absolute_value=True)\
                    .then_inc(chain, 1)
                dve.wait_ge(chain, 6 * k + 1)
                nc.vector.tensor_scalar(step[:, k], step[:, k], 1.0 / 7.0, 1e-12, ALU.mult, ALU.max)\
                    .then_inc(chain, 1)
                dve.wait_ge(chain, 6 * k + 2)
                nc.vector.reciprocal(inv[:, k], step[:, k]).then_inc(chain, 1)
                dve.wait_ge(chain, 6 * k + 3)
                nc.vector.tensor_tensor(w[:, k], w[:, k], wide(inv), ALU.mult).then_inc(chain, 1)
                dve.wait_ge(chain, 6 * k + 4)
                nc.vector.tensor_scalar(w[:, k], w[:, k], MAGIC, MAGIC, ALU.add, ALU.subtract).then_inc(chain, 1)
                dve.wait_ge(chain, 6 * k + 5)
                nc.vector.tensor_tensor(w[:, k], w[:, k], wide(step), ALU.mult).then_inc(chain, 1)
                dve.wait_ge(chain, 6 * k + 6)
                dve.sem_inc(done, 1)

        @block.tensor
        def _(pe):
            turn = 0
            for k, (_, dst, ot, it) in enumerate(srcs):
                pe.wait_ge(done, k + 1)
                src = w[:, k].rearrange("p b q -> p (b q)")
                for i in range(it):
                    for o0 in range(0, ot, 2):
                        if turn >= 8:
                            pe.wait_ge(out, turn - 7)
                        for o in (o0, o0 + 1):
                            last = nc.tensor.transpose(ps[:, turn % 8, (o - o0) * 128:(o - o0 + 1) * 128],
                                                       src[:, (o * it + i) * 128:(o * it + i + 1) * 128],
                                                       c["ident"][:])
                        last.then_inc(turned, 1)
                        turn += 1

        @block.scalar
        def _(act):
            turn = 0
            for k, (_, dst, ot, it) in enumerate(srcs):
                for i in range(it):
                    for o0 in range(0, ot, 2):
                        act.wait_ge(turned, turn + 1)
                        nc.scalar.copy(dst[:, i, o0 * 128:(o0 + 2) * 128], ps[:, turn % 8, 0:256])\
                            .then_inc(out, 1)
                        turn += 1


def set_scale(nc, name, amax, scale, inv):
    ctx = ExitStack()
    with ctx:
        k = amax.shape[1]
        every = ctx.enter_context(nc.sbuf_tensor(name + "_every", [128, k], F32))
        reduced = nc.alloc_semaphore(name + "_reduced")
        chain = nc.alloc_semaphore(name + "_chain")
        block = ctx.enter_context(nc.Block())

        @block.gpsimd
        def _(pool):
            nc.gpsimd.partition_all_reduce(every[:], amax, 128, bass.bass_isa.ReduceOp.max).then_inc(reduced, 1)

        @block.vector
        def _(dve):
            dve.wait_ge(reduced, 1)
            nc.vector.reduce_max(scale, every[:], AX.X).then_inc(chain, 1)
            dve.wait_ge(chain, 1)
            nc.vector.tensor_scalar(scale, scale, 1.0 / QMAX, 1e-12, ALU.mult, ALU.max).then_inc(chain, 1)
            dve.wait_ge(chain, 2)
            nc.vector.reciprocal(inv, scale).then_inc(chain, 1)
            dve.wait_ge(chain, 3)


def running_max(nc, dve, new, total, x, s_new, s_total, n):
    dve.wait_ge(s_total.sem, s_total.before(n))
    nc.vector.tensor_reduce(new, x, AX.X, ALU.max, apply_absolute_value=True).then_inc(s_new.sem, 1)
    dve.wait_ge(s_new.sem, s_new.at(n))
    nc.vector.tensor_tensor(total, total, new, ALU.max).then_inc(s_total.sem, 1)


def phase_b(nc, ps, NB, magic, x0_dram, gateT, upT, scale, inv, gate_dram, up_dram, amax_gate, amax_up):
    ctx = ExitStack()
    with ctx:
        def sb(name, shape, dt=F32):
            return ctx.enter_context(nc.sbuf_tensor("b_" + name, shape, dt))

        def sem(name):
            return nc.alloc_semaphore("b_" + name)

        x = sb("x", [128, 2, CT, T])
        xm = sb("xm", [128, 2, CT, T])
        gu = sb("gu", [128, 2, 2, FT, T])
        new = sb("new", [128, 2, 2])
        x_loaded = [sem(f"x_loaded{u}") for u in range(2)]
        gu_stored = [sem(f"gu_stored{u}") for u in range(2)]
        S = signals(ctx, nc, "b", xm=1, xq=1, mm=2 * FT, out=2 * FT, newg=1, maxg=1, newu=1, maxu=1)
        block = ctx.enter_context(nc.Block())

        @block.sync
        def _(sp):
            def load(n, u):
                sp.dma_start(x[:, u], x0_dram[n].rearrange("(c p) t -> p c t", p=128)).then_inc(x_loaded[u], 16)

            def pair(i, more):
                for u in range(2):
                    n = 2 * i + u
                    if more:
                        sp.wait_ge(S["mm"].sem, S["mm"].at(n))
                        load(n + 2, u)
                    for j, dram in enumerate((gate_dram, up_dram)):
                        sp.wait_ge(S["out"].sem, S["out"].at(n, (j + 1) * FT))
                        sp.dma_start(dram[n], gu[:, u, j].rearrange("p f t -> p (f t)")).then_inc(gu_stored[u], 16)

            for u in range(2):
                load(u, u)
            with sp.Fori(0, NB // 2 - 1) as i:
                pair(i, True)
            pair(NB // 2 - 1, False)
            for u in range(2):
                sp.wait_ge(gu_stored[u], 32 * (NB // 2))

        @block.scalar
        def _(act):
            for k in ("xm", "out"):
                S[k].give(act)
            with act.Fori(0, NB // 2) as i:
                for u in range(2):
                    n = 2 * i + u
                    act.wait_ge(x_loaded[u], 16 * i + 16)
                    act.wait_ge(S["xq"].sem, S["xq"].before(n))
                    nc.scalar.activation(xm[:, u], x[:, u], ACT.Identity, scale=inv, bias=magic)\
                        .then_inc(S["xm"].sem, 1)
                for u in range(2):
                    n = 2 * i + u
                    act.wait_ge(gu_stored[u], 32 * i)
                    act.wait_ge(S["maxu"].sem, S["maxu"].before(n))
                    for m in range(2 * FT):
                        act.wait_ge(S["mm"].sem, S["mm"].at(n, m + 1))
                        nc.scalar.copy(gu[:, u, m // FT, m % FT, :], ps[:, 4 * u + m % 4, 0:T])\
                            .then_inc(S["out"].sem, 1)

        @block.vector
        def _(dve):
            for k in ("xq", "newg", "maxg", "newu", "maxu"):
                S[k].give(dve)
            with dve.Fori(0, NB // 2) as i:
                for u in range(2):
                    n = 2 * i + u
                    dve.wait_ge(S["xm"].sem, S["xm"].at(n))
                    dve.wait_ge(S["mm"].sem, S["mm"].before(n))
                    nc.vector.tensor_scalar(x[:, u], xm[:, u], MAGIC, scale, ALU.subtract, ALU.mult)\
                        .then_inc(S["xq"].sem, 1)
                for u in range(2):
                    n = 2 * i + u
                    for j, (k, amax) in enumerate((("g", amax_gate), ("u", amax_up))):
                        dve.wait_ge(S["out"].sem, S["out"].at(n, (j + 1) * FT))
                        running_max(nc, dve, new[:, u, j:j + 1], amax[:, u:u + 1],
                                    gu[:, u, j].rearrange("p f t -> p (f t)"), S["new" + k], S["max" + k], n)

        @block.tensor
        def _(pe):
            S["mm"].give(pe)
            with pe.Fori(0, NB // 2) as i:
                for u in range(2):
                    n = 2 * i + u
                    pe.wait_ge(S["xq"].sem, S["xq"].at(n))
                    for m in range(2 * FT):
                        if m < 4:
                            pe.wait_ge(S["out"].sem, S["out"].before(n))
                        else:
                            pe.wait_ge(S["out"].sem, S["out"].at(n, m - 3))
                        w = (gateT, upT)[m // FT]
                        for k in range(CT):
                            last = nc.tensor.matmul(ps[:, 4 * u + m % 4, 0:T],
                                                    w[:, k, (m % FT) * 128:(m % FT + 1) * 128],
                                                    x[:, u, k, :], start=(k == 0), stop=(k == CT - 1))
                        last.then_inc(S["mm"].sem, 1)


def phase_c(nc, NB, magic, gate_dram, scale, inv, g2_dram, amax_g2):
    ctx = ExitStack()
    N = FT * T
    with ctx:
        def sb(name):
            return ctx.enter_context(nc.sbuf_tensor("c_" + name, [128, 2, N], F32))

        def sem(name):
            return nc.alloc_semaphore("c_" + name)

        g, gm, gq, sg, sm, g2 = (sb(n) for n in ("g", "gm", "gq", "sg", "sm", "g2"))
        new = ctx.enter_context(nc.sbuf_tensor("c_new", [128, 2], F32))
        loaded = [sem(f"loaded{u}") for u in range(2)]
        stored = [sem(f"stored{u}") for u in range(2)]
        S = signals(ctx, nc, "c", gm=1, gq=1, sg=1, sm=1, sr=1, g2=1, new=1, max=1)
        block = ctx.enter_context(nc.Block())

        @block.sync
        def _(sp):
            def load(n, u):
                sp.dma_start(g[:, u], gate_dram[n]).then_inc(loaded[u], 16)

            def pair(i, more):
                for u in range(2):
                    n = 2 * i + u
                    if more:
                        sp.wait_ge(S["gm"].sem, S["gm"].at(n))
                        load(n + 2, u)
                for u in range(2):
                    n = 2 * i + u
                    sp.wait_ge(S["g2"].sem, S["g2"].at(n))
                    sp.dma_start(g2_dram[n], g2[:, u]).then_inc(stored[u], 16)

            for u in range(2):
                load(u, u)
            with sp.Fori(0, NB // 2 - 1) as i:
                pair(i, True)
            pair(NB // 2 - 1, False)
            for u in range(2):
                sp.wait_ge(stored[u], 16 * (NB // 2))

        @block.scalar
        def _(act):
            for k in ("gm", "sg"):
                S[k].give(act)
            with act.Fori(0, NB // 2) as i:
                for u in range(2):
                    n = 2 * i + u
                    act.wait_ge(loaded[u], 16 * i + 16)
                    act.wait_ge(S["gq"].sem, S["gq"].before(n))
                    nc.scalar.activation(gm[:, u], g[:, u], ACT.Identity, scale=inv, bias=magic)\
                        .then_inc(S["gm"].sem, 1)
                for u in range(2):
                    n = 2 * i + u
                    act.wait_ge(S["gq"].sem, S["gq"].at(n))
                    act.wait_ge(S["sm"].sem, S["sm"].before(n))
                    nc.scalar.activation(sg[:, u], gq[:, u], ACT.Sigmoid).then_inc(S["sg"].sem, 1)

        @block.vector
        def _(dve):
            for k in ("gq", "sm", "sr", "g2", "new", "max"):
                S[k].give(dve)
            with dve.Fori(0, NB // 2) as i:
                for u in range(2):
                    n = 2 * i + u
                    dve.wait_ge(S["gm"].sem, S["gm"].at(n))
                    dve.wait_ge(S["g2"].sem, S["g2"].before(n))
                    nc.vector.tensor_scalar(gq[:, u], gm[:, u], MAGIC, scale, ALU.subtract, ALU.mult)\
                        .then_inc(S["gq"].sem, 1)
                for u in range(2):
                    n = 2 * i + u
                    dve.wait_ge(S["sg"].sem, S["sg"].at(n))
                    dve.wait_ge(S["g2"].sem, S["g2"].before(n))
                    nc.vector.tensor_scalar(sm[:, u], sg[:, u], 65536.0, MAGIC, ALU.mult, ALU.add)\
                        .then_inc(S["sm"].sem, 1)
                    dve.wait_ge(S["sm"].sem, S["sm"].at(n))
                    nc.vector.tensor_scalar(sm[:, u], sm[:, u], MAGIC + 65535.0, MAGIC, ALU.min, ALU.subtract)\
                        .then_inc(S["sr"].sem, 1)
                for u in range(2):
                    n = 2 * i + u
                    dve.wait_ge(S["sr"].sem, S["sr"].at(n))
                    dve.wait_ge(stored[u], 16 * i)
                    dve.wait_ge(S["new"].sem, S["new"].before(n))
                    nc.vector.scalar_tensor_tensor(out=g2[:, u], in0=sm[:, u], scalar=1.0 / 65536.0,
                                                   in1=gq[:, u], op0=ALU.mult, op1=ALU.mult)\
                        .then_inc(S["g2"].sem, 1)
                for u in range(2):
                    n = 2 * i + u
                    dve.wait_ge(S["g2"].sem, S["g2"].at(n))
                    running_max(nc, dve, new[:, u:u + 1], amax_g2[:, u:u + 1], g2[:, u], S["new"], S["max"], n)


def phase_d(nc, NB, magic, g2_dram, up_dram, scale_g, inv_g, scale_u, inv_u, o_dram, amax_o):
    ctx = ExitStack()
    N = FT * T
    with ctx:
        def sb(name):
            return ctx.enter_context(nc.sbuf_tensor("d_" + name, [128, 2, N], F32))

        def sem(name):
            return nc.alloc_semaphore("d_" + name)

        src = {k: sb(k) for k in "gu"}
        rounded = {k: sb(k + "m") for k in "gu"}
        quant = {k: sb(k + "q") for k in "gu"}
        o = sb("o")
        new = ctx.enter_context(nc.sbuf_tensor("d_new", [128, 2], F32))
        dram = {"g": g2_dram, "u": up_dram}
        scale, inv = {"g": scale_g, "u": scale_u}, {"g": inv_g, "u": inv_u}
        loaded = {k: [sem(f"loaded_{k}{u}") for u in range(2)] for k in "gu"}
        stored = [sem(f"stored{u}") for u in range(2)]
        S = signals(ctx, nc, "d", gm=1, um=1, gq=1, uq=1, o=1, new=1, max=1)
        block = ctx.enter_context(nc.Block())

        @block.sync
        def _(sp):
            def load(k, n, u):
                sp.dma_start(src[k][:, u], dram[k][n]).then_inc(loaded[k][u], 16)

            def pair(i, more):
                for u in range(2):
                    n = 2 * i + u
                    for k in "gu":
                        if more:
                            sp.wait_ge(S[k + "m"].sem, S[k + "m"].at(n))
                            load(k, n + 2, u)
                for u in range(2):
                    n = 2 * i + u
                    sp.wait_ge(S["o"].sem, S["o"].at(n))
                    sp.dma_start(o_dram[n], o[:, u]).then_inc(stored[u], 16)

            for u in range(2):
                for k in "gu":
                    load(k, u, u)
            with sp.Fori(0, NB // 2 - 1) as i:
                pair(i, True)
            pair(NB // 2 - 1, False)
            for u in range(2):
                sp.wait_ge(stored[u], 16 * (NB // 2))

        @block.scalar
        def _(act):
            for k in ("gm", "um"):
                S[k].give(act)
            with act.Fori(0, NB // 2) as i:
                for u in range(2):
                    n = 2 * i + u
                    for k in "gu":
                        act.wait_ge(loaded[k][u], 16 * i + 16)
                        act.wait_ge(S[k + "q"].sem, S[k + "q"].before(n))
                        nc.scalar.activation(rounded[k][:, u], src[k][:, u], ACT.Identity, scale=inv[k],
                                             bias=magic).then_inc(S[k + "m"].sem, 1)

        @block.vector
        def _(dve):
            for k in ("gq", "uq", "o", "new", "max"):
                S[k].give(dve)
            with dve.Fori(0, NB // 2) as i:
                for u in range(2):
                    n = 2 * i + u
                    for k in "gu":
                        dve.wait_ge(S[k + "m"].sem, S[k + "m"].at(n))
                        dve.wait_ge(S["o"].sem, S["o"].before(n))
                        nc.vector.tensor_scalar(quant[k][:, u], rounded[k][:, u], MAGIC, scale[k],
                                                ALU.subtract, ALU.mult).then_inc(S[k + "q"].sem, 1)
                for u in range(2):
                    n = 2 * i + u
                    dve.wait_ge(S["uq"].sem, S["uq"].at(n))
                    dve.wait_ge(S["gq"].sem, S["gq"].at(n))
                    dve.wait_ge(stored[u], 16 * i)
                    dve.wait_ge(S["new"].sem, S["new"].before(n))
                    nc.vector.tensor_tensor(o[:, u], quant["g"][:, u], quant["u"][:, u], ALU.mult)\
                        .then_inc(S["o"].sem, 1)
                for u in range(2):
                    n = 2 * i + u
                    dve.wait_ge(S["o"].sem, S["o"].at(n))
                    running_max(nc, dve, new[:, u:u + 1], amax_o[:, u:u + 1], o[:, u], S["new"], S["max"], n)


PARTS = 3
Q_PART = (0, 0, 0, 1, 1, 2)
K_PART = (0, 1, 2, 0, 1, 0)
SLOTS = len(Q_PART)
SDPA, HYP, COS = range(3)
KINDS = [SDPA] * 6 + [HYP] * 4 + [COS] * 6
NSCALED = 10
HD1 = HD + 1
VW = 2 * HD


def phase_f1(nc, c, ps, NB, magic, o_dram, h1_dram, downT, scale, inv, wqkv_dram, curv_dram,
             h2_dram, parts_dram, v_dram):
    ctx = ExitStack()
    with ctx:
        def sb(name, shape, dt=F32):
            return ctx.enter_context(nc.sbuf_tensor("f_" + name, shape, dt))

        def sem(name):
            return nc.alloc_semaphore("f_" + name)

        GH = 6
        GROUPS = [(0, 6), (6, 6), (12, 4)]
        wqkv = sb("wqkv", [128, CT, 3 * D])
        icurv = sb("icurv", [R, 4])
        power = sb("power", [R, NT * 2, NSCALED])
        o = sb("o", [128, 2, FT, T])
        om = sb("om", [128, 2, FT, T])
        h = sb("h", [R, 2, NT, D])
        stats = sb("stats", [R, 2, NT, 6])
        mv = sb("mv", [R, 2, NT, 2])
        var_eps = sb("var_eps", [R, 2, NT])
        rstd = sb("rstd", [R, 2, NT])
        xn = sb("xn", [R, 2, NT, D])
        xT = sb("xT", [128, 2, CT, T])
        rc = sb("rc", [R, 2, 2 * H, HD])
        rs = sb("rs", [R, 2, 2 * H, HD])
        qk = sb("qk", [R, 2, NT, 2 * H, HD1])
        sq = sb("sq", [R, 2, 2, NSCALED, HD])
        ss = sb("ss", [R, 2, NT * 2, NSCALED])
        norm = sb("norm", [R, 2, NT * 2, NSCALED])
        parts = sb("parts", [GH * HD1, 2, 6, PARTS, T], BF16)
        rest = sb("rest", [GH * HD1, 2, 2, T])
        vp = sb("vp", [R, 2, NT, H, VW])
        w_loaded = sem("w_loaded")
        powers = sem("powers")
        filled = sem("filled")
        o_loaded = [sem(f"o_loaded{u}") for u in range(2)]
        h_loaded = [sem(f"h_loaded{u}") for u in range(2)]
        h_stored = [sem(f"h_stored{u}") for u in range(2)]
        p_stored = [sem(f"p_stored{u}") for u in range(2)]
        v_stored = [sem(f"v_stored{u}") for u in range(2)]
        S = signals(ctx, nc, "f", om=1, oq=1, y=1, h2=1, bn=NT + 1, mv=1, eps=1, rstd=1, xn=NT, xT=1, xT_out=1,
                    qk=NT, v=2, v_out=2, rc=2 * NT, rot=NT, sq=NT, ss=NT, cap=2, norm=1, tq=2, scaled=NT,
                    turn=6, hi=6, rest=6, mid=6, lo=6)
        banks = [lambda k, u=u: ps[:, 4 * u + k, :] for u in range(2)]
        block = ctx.enter_context(nc.Block())

        @block.sync
        def _(sp):
            def load_o(n, u):
                sp.dma_start(o[:, u].rearrange("p f t -> p (f t)"), o_dram[n]).then_inc(o_loaded[u], 16)

            def load_h(n, u):
                sp.dma_start(h[:, u], h1_dram[n].rearrange("(t p) d -> p t d", p=R)).then_inc(h_loaded[u], 16)

            def pair(i, more):
                for u in range(2):
                    n = 2 * i + u
                    if more:
                        sp.wait_ge(S["y"].sem, S["y"].at(n))
                        load_o(n + 2, u)
                for u in range(2):
                    n = 2 * i + u
                    sp.wait_ge(S["h2"].sem, S["h2"].at(n))
                    sp.dma_start(h2_dram[n].rearrange("(t p) d -> p t d", p=R), h[:, u]).then_inc(h_stored[u], 16)
                for u in range(2):
                    n = 2 * i + u
                    sp.wait_ge(S["v_out"].sem, S["v_out"].at(n))
                    sp.dma_start(v_dram[n], vp[:, u].rearrange("p t h w -> p (t h w)")).then_inc(v_stored[u], 16)
                    if more:
                        sp.wait_ge(S["xn"].sem, S["xn"].at(n))
                        sp.wait_ge(h_stored[u], 16 * i + 16)
                        load_h(n + 2, u)
                for u in range(2):
                    n = 2 * i + u
                    for j in range(6):
                        h0, nh = GROUPS[j % 3]
                        sp.wait_ge(S["lo"].sem, S["lo"].at(n, j + 1))
                        sp.dma_start(parts_dram[n, j // 3, h0 * HD1:(h0 + nh) * HD1].rearrange("r k t -> r (k t)"),
                                     parts[0:nh * HD1, u, j].rearrange("p k t -> p (k t)")).then_inc(p_stored[u], 16)

            sp.dma_start(wqkv[:], wqkv_dram.rearrange("(k p) n -> p k n", p=128)).then_inc(w_loaded, 16)
            sp.dma_start(icurv[:], curv_dram.rearrange("(a h) -> a h", a=1).broadcast_to([R, 4])).then_inc(w_loaded, 16)
            for u in range(2):
                load_o(u, u)
                load_h(u, u)
            with sp.Fori(0, NB // 2 - 1) as i:
                pair(i, True)
            pair(NB // 2 - 1, False)
            for u in range(2):
                sp.wait_ge(h_stored[u], 16 * (NB // 2))
                sp.wait_ge(p_stored[u], 96 * (NB // 2))
                sp.wait_ge(v_stored[u], 16 * (NB // 2))

        @block.gpsimd
        def _(pool):
            for k in ("eps", "rstd", "cap", "norm"):
                S[k].give(pool)
            nc.gpsimd.memset(power[:, :, 0:4], 0.5)
            nc.gpsimd.memset(power[:, :, 4:NSCALED], -0.5).then_inc(powers, 1)
            pool.wait_ge(powers, 1)
            pool.wait_ge(filled, 1)
            with pool.Fori(0, NB // 2) as i:
                for u in range(2):
                    ln_rstd(nc, pool, c, mv[:, u], var_eps[:, u], rstd[:, u],
                            S["mv"], S["eps"], S["rstd"], 2 * i + u)
                for u in range(2):
                    n = 2 * i + u
                    pool.wait_ge(S["ss"].sem, S["ss"].at(n))
                    nc.gpsimd.tensor_tensor(ss[:, u, :, 0:4], ss[:, u, :, 0:4],
                                            icurv[:].unsqueeze(1).to_broadcast([R, NT * 2, 4]), ALU.add)\
                        .then_inc(S["cap"].sem, 1)
                    nc.gpsimd.tensor_scalar(ss[:, u, :, 4:NSCALED], ss[:, u, :, 4:NSCALED], 1e-24, None, ALU.max)\
                        .then_inc(S["cap"].sem, 1)
                    pool.wait_ge(S["cap"].sem, S["cap"].at(n))
                    pool.wait_ge(S["scaled"].sem, S["scaled"].before(n))
                    nc.gpsimd.tensor_tensor(norm[:, u], ss[:, u], power[:], ALU.pow).then_inc(S["norm"].sem, 1)

        @block.scalar
        def _(act):
            for k in ("om", "xT_out", "v_out", "sq", "hi", "mid"):
                S[k].give(act)
            with act.Fori(0, NB // 2) as i:
                for u in range(2):
                    n = 2 * i + u
                    act.wait_ge(o_loaded[u], 16 * i + 16)
                    act.wait_ge(S["oq"].sem, S["oq"].before(n))
                    nc.scalar.activation(om[:, u], o[:, u], ACT.Identity, scale=inv, bias=magic)\
                        .then_inc(S["om"].sem, 1)
                for u in range(2):
                    n = 2 * i + u
                    act.wait_ge(S["xT"].sem, S["xT"].at(n))
                    act.wait_ge(S["v"].sem, S["v"].before(n))
                    nc.scalar.copy(xT[:, u], ps[:, 4 * u + 2:4 * u + 4, 0:T]).then_inc(S["xT_out"].sem, 1)
                for u in range(2):
                    n, B = 2 * i + u, banks[u]
                    act.wait_ge(v_stored[u], 16 * i)
                    act.wait_ge(S["v"].sem, S["v"].at(n, 1))
                    nc.scalar.copy(vp[:, u, 0:2, :, 0:HD], B(3)[0:R, :].rearrange("p (t h w) -> p t h w", t=2, w=HD))\
                        .then_inc(S["v_out"].sem, 1)
                    act.wait_ge(S["v"].sem, S["v"].at(n, 2))
                    nc.scalar.copy(vp[:, u, 2, :, 0:HD], B(0)[0:R, 0:D].rearrange("p (h w) -> p h w", w=HD))\
                        .then_inc(S["v_out"].sem, 1)
                    for t in range(NT):
                        act.wait_ge(S["rot"].sem, S["rot"].at(n, t + 1))
                        if t:
                            act.wait_ge(S["ss"].sem, S["ss"].at(n, t))
                        else:
                            act.wait_ge(S["ss"].sem, S["ss"].before(n))
                        heads = qk[:, u, t].rearrange("p (a h) w -> p a h w", a=2)[:, :, 6:16, 0:HD]
                        nc.scalar.activation(sq[:, u], heads, ACT.Square).then_inc(S["sq"].sem, 1)
                for u in range(2):
                    n, B = 2 * i + u, banks[u]
                    act.wait_ge(p_stored[u], 96 * i)
                    for j in range(6):
                        rows = GROUPS[j % 3][1] * HD1
                        act.wait_ge(S["turn"].sem, S["turn"].at(n, j + 1))
                        nc.scalar.copy(parts[0:rows, u, j, 0, :], B(j % 4)[0:rows, 0:T]).then_inc(S["hi"].sem, 1)
                        act.wait_ge(S["rest"].sem, S["rest"].at(n, j + 1))
                        nc.scalar.copy(parts[0:rows, u, j, 1, :], rest[0:rows, u, j % 2]).then_inc(S["mid"].sem, 1)

        @block.vector
        def _(dve):
            for k in ("oq", "h2", "bn", "mv", "xn", "rc", "rot", "ss", "tq", "scaled", "rest", "lo"):
                S[k].give(dve)
            dve.wait_ge(w_loaded, 32)
            nc.vector.reciprocal(icurv[:], icurv[:]).then_inc(filled, 1)
            nc.vector.tensor_scalar(wqkv[:, :, 0:6 * HD], wqkv[:, :, 0:6 * HD], float(HD) ** -0.5, None, ALU.mult)\
                .then_inc(filled, 1)
            nc.vector.memset(vp[:], 1.0)
            nc.vector.memset(qk[:], 0.0).then_inc(filled, 1)
            dve.wait_ge(filled, 3)
            with dve.Fori(0, NB // 2) as i:
                for u in range(2):
                    n = 2 * i + u
                    dve.wait_ge(S["om"].sem, S["om"].at(n))
                    nc.vector.tensor_scalar(o[:, u], om[:, u], MAGIC, scale, ALU.subtract, ALU.mult)\
                        .then_inc(S["oq"].sem, 1)
                for u in range(2):
                    n, B = 2 * i + u, banks[u]
                    dve.wait_ge(S["y"].sem, S["y"].at(n))
                    dve.wait_ge(h_loaded[u], 16 * i + 16)
                    nc.vector.tensor_tensor(h[:, u, 0:2, :], B(0)[0:R, :].rearrange("p (t d) -> p t d", t=2),
                                            h[:, u, 0:2, :], ALU.add)
                    nc.vector.tensor_tensor(h[:, u, 2, :], B(1)[0:R, 0:D], h[:, u, 2, :], ALU.add)\
                        .then_inc(S["h2"].sem, 1)
                for u in range(2):
                    n = 2 * i + u
                    dve.wait_ge(S["h2"].sem, S["h2"].at(n))
                    ln_stats(nc, dve, h[:, u], stats[:, u], mv[:, u], (S["bn"].sem, S["bn"].at(n)), S["mv"])
                for u in range(2):
                    n = 2 * i + u
                    dve.wait_ge(S["rstd"].sem, S["rstd"].at(n))
                    dve.wait_ge(S["xT"].sem, S["xT"].before(n))
                    ln_apply(nc, xn[:, u], h[:, u], mv[:, u], rstd[:, u], S["xn"])
                for u in range(2):
                    n, B = 2 * i + u, banks[u]
                    dve.wait_ge(S["turn"].sem, S["turn"].before(n))
                    for t in range(NT):
                        x = B(t)[0:R, :].rearrange("p (h w) -> p h w", w=HD)
                        cos = c["cos"][:, t].unsqueeze(1).to_broadcast([R, 2 * H, HD])
                        sin = c["sin"][:, t].unsqueeze(1)
                        half = HD // 2
                        dve.wait_ge(S["qk"].sem, S["qk"].at(n, t + 1))
                        if t:
                            dve.wait_ge(S["rot"].sem, S["rot"].at(n, t))
                        nc.vector.tensor_tensor(rc[:, u], x, cos, ALU.mult)
                        nc.vector.tensor_tensor(rs[:, u, :, 0:half], x[:, :, half:HD],
                                                sin[:, :, 0:half].to_broadcast([R, 2 * H, half]), ALU.mult)\
                            .then_inc(S["rc"].sem, 1)
                        nc.vector.tensor_tensor(rs[:, u, :, half:HD], x[:, :, 0:half],
                                                sin[:, :, half:HD].to_broadcast([R, 2 * H, half]), ALU.mult)\
                            .then_inc(S["rc"].sem, 1)
                        dve.wait_ge(S["rc"].sem, S["rc"].at(n, 2 * t + 2))
                        nc.vector.tensor_tensor(qk[:, u, t, :, 0:HD], rc[:, u], rs[:, u], ALU.add)\
                            .then_inc(S["rot"].sem, 1)
                    for t in range(NT):
                        dve.wait_ge(S["sq"].sem, S["sq"].at(n, t + 1))
                        if t == 0:
                            dve.wait_ge(S["norm"].sem, S["norm"].before(n))
                        nc.vector.reduce_sum(ss[:, u, 2 * t:2 * t + 2, :], sq[:, u], AX.X).then_inc(S["ss"].sem, 1)
                for u in range(2):
                    n = 2 * i + u
                    dve.wait_ge(S["norm"].sem, S["norm"].at(n))
                    split = norm[:, u].rearrange("p (t a) h -> p t a h", a=2)
                    nc.vector.tensor_copy(qk[:, u, :, 6:10, HD], split[:, :, 0, 0:4]).then_inc(S["tq"].sem, 1)
                    nc.vector.tensor_scalar(qk[:, u, :, H + 6:H + 10, HD], split[:, :, 1, 0:4], -1.0, None, ALU.mult)\
                        .then_inc(S["tq"].sem, 1)
                    for t in range(NT):
                        heads = qk[:, u, t].rearrange("p (a h) w -> p a h w", a=2)[:, :, 10:16, 0:HD]
                        nc.vector.tensor_tensor(heads, heads, split[:, t, :, 4:NSCALED].unsqueeze(3)
                                                .to_broadcast([R, 2, 6, HD]), ALU.mult).then_inc(S["scaled"].sem, 1)
                for u in range(2):
                    n, B = 2 * i + u, banks[u]
                    for j in range(6):
                        rows = GROUPS[j % 3][1] * HD1
                        dve.wait_ge(S["hi"].sem, S["hi"].at(n, j + 1))
                        if j >= 2:
                            dve.wait_ge(S["lo"].sem, S["lo"].at(n, j - 1))
                        nc.vector.tensor_tensor(rest[0:rows, u, j % 2], B(j % 4)[0:rows, 0:T],
                                                parts[0:rows, u, j, 0, :], ALU.subtract).then_inc(S["rest"].sem, 1)
                        dve.wait_ge(S["mid"].sem, S["mid"].at(n, j + 1))
                        nc.vector.tensor_tensor(parts[0:rows, u, j, 2, :], rest[0:rows, u, j % 2],
                                                parts[0:rows, u, j, 1, :], ALU.subtract).then_inc(S["lo"].sem, 1)

        @block.tensor
        def _(pe):
            for k in ("y", "xT", "qk", "v", "turn"):
                S[k].give(pe)
            pe.wait_ge(filled, 2)
            with pe.Fori(0, NB // 2) as i:
                for u in range(2):
                    n, B = 2 * i + u, banks[u]
                    pe.wait_ge(S["oq"].sem, S["oq"].at(n))
                    pe.wait_ge(S["lo"].sem, S["lo"].before(n))
                    for t in range(NT):
                        for k in range(FT):
                            last = nc.tensor.matmul(B(t // 2)[0:R, (t % 2) * D:(t % 2 + 1) * D],
                                                    o[:, u, k, t * R:(t + 1) * R], downT[:, k, :],
                                                    start=(k == 0), stop=(k == FT - 1))
                    last.then_inc(S["y"].sem, 1)
                for u in range(2):
                    n, B = 2 * i + u, banks[u]
                    pe.wait_ge(S["xn"].sem, S["xn"].at(n))
                    transpose_tokens(nc, pe, c, xn[:, u], lambda k: B(2 + k)).then_inc(S["xT"].sem, 1)
                for u in range(2):
                    n, B = 2 * i + u, banks[u]
                    pe.wait_ge(S["xT_out"].sem, S["xT_out"].at(n))
                    pe.wait_ge(S["h2"].sem, S["h2"].at(n))
                    for t in range(NT):
                        for k in range(CT):
                            last = nc.tensor.matmul(B(t)[0:R, :], xT[:, u, k, t * R:(t + 1) * R],
                                                    wqkv[:, k, 0:2 * D], start=(k == 0), stop=(k == CT - 1))
                        last.then_inc(S["qk"].sem, 1)
                    for t in range(NT):
                        if t == 2:
                            last.then_inc(S["v"].sem, 1)
                            pe.wait_ge(S["rot"].sem, S["rot"].at(n, 1))
                        for k in range(CT):
                            last = nc.tensor.matmul(B(0 if t == 2 else 3)[0:R, (t % 2) * D:(t % 2 + 1) * D],
                                                    xT[:, u, k, t * R:(t + 1) * R], wqkv[:, k, 2 * D:3 * D],
                                                    start=(k == 0), stop=(k == CT - 1))
                    last.then_inc(S["v"].sem, 1)
                for u in range(2):
                    n, B = 2 * i + u, banks[u]
                    pe.wait_ge(S["v_out"].sem, S["v_out"].at(n))
                    pe.wait_ge(S["tq"].sem, S["tq"].at(n))
                    pe.wait_ge(S["scaled"].sem, S["scaled"].at(n))
                    for j in range(6):
                        h0, nh = GROUPS[j % 3]
                        if j >= 4:
                            pe.wait_ge(S["rest"].sem, S["rest"].at(n, j - 3))
                        x = qk[:, u].rearrange("p t h w -> p t (h w)")
                        first = (H * (j // 3) + h0) * HD1
                        for t in range(NT):
                            last = nc.tensor.transpose(B(j % 4)[0:nh * HD1, t * R:(t + 1) * R],
                                                       x[:, t, first:first + nh * HD1], c["ident"][0:R, 0:R])
                        last.then_inc(S["turn"].sem, 1)


def attention_core(nc, c, ps, NB, name, kinds, causal, hd, parts_dram, v_dram, ctx_dram, curv_dram=None):
    ctx = ExitStack()
    with ctx:
        def sb(n_, shape, dt=F32):
            return ctx.enter_context(nc.sbuf_tensor(f"{name}_{n_}", shape, dt))

        def sem(n_):
            return nc.alloc_semaphore(f"{name}_{n_}")

        rows = SLOTS * hd
        if causal:
            ORDER = [0, 1, 2, 3, 12, 13, 14, 15, 4, 5, 6, 7, 8, 9, 10, 11]
            LOOK, UNITS, SETS = 1, 2, ((0, 1), (2, 3))
            TURN = (4, 5)
            QTILE = {2: (0, 0), 1: (1, 0), 0: (1, 2 * R)}
            KTILE = {0: (0, 0), 1: (1, 0), 2: (1, 2 * R)}
            EVAC = ("act", "dve")
        else:
            ORDER = list(range(H))
            LOOK, UNITS, SETS = 0, 3, ((0, 1, 2),)
            TURN = (3, 4, 5)
            QTILE = {t: (t, 0) for t in range(NT)}
            KTILE = {t: (t, 0) for t in range(NT)}
            EVAC = ("dve", "act", "dve")
        QORDER = sorted(QTILE, key=lambda t: (QTILE[t][0], QTILE[t][1]))
        HYPS = [h for h in ORDER if kinds[h] == HYP]
        NHYP = len(HYPS)
        NORMAL = [j for j, h in enumerate(ORDER) if kinds[h] != HYP]
        MAXED = [j for j, h in enumerate(ORDER) if kinds[h] != COS]
        USES = NHYP + len(NORMAL)
        SLOTN, STEPS = 2 * H, 2 * H + 3 + LOOK
        width = {t: (t + 1) * R if causal else T for t in range(NT)}
        share = {e: [m for m in range(UNITS) if EVAC[m] == e] for e in ("act", "dve")}

        q = sb("q", [rows, 2, H, T], BF16)
        k = sb("k", [rows, 2, H, T], BF16)
        vp = sb("vp", [R, 2, NT, H, VW])
        neg = sb("neg", [R, 4, NT])
        prob = sb("prob", [R, 2, NT, T])
        probT = sb("probT", [R, 8, UNITS, T])
        oT = sb("oT", [128, 2, T])
        rec = sb("rec", [R, 2, NT, 4])
        out = sb("out", [R, 2, NT, H, HD])
        qk_loaded = [sem(f"qk_loaded{u}") for u in range(2)]
        v_loaded = [sem(f"v_loaded{u}") for u in range(2)]
        stored = [sem(f"stored{u}") for u in range(2)]
        sigs = dict(s=USES * UNITS, neg=len(MAXED) * NT, exp=H * NT, turn=H * UNITS,
                    act=H * len(share["act"]), dve=H * len(share["dve"]), pv=4, oT=4, back=4, rec=4, out=4)
        if NHYP:
            negc = sb("negc", [R, 4])
            root_ic = sb("root_ic", [R, 4])
            one = sb("one", [R, 1])
            eps6 = sb("eps6", [R, 1])
            hw = sb("hw", [R, NHYP, 2, T])
            hu = sb("hu", [R, NHYP, 2, T])
            curv_loaded, ready = sem("curv_loaded"), sem("ready")
            sigs |= dict(w=NHYP, wc=NHYP, hu=NHYP, hl=NHYP, root=NHYP, z=NHYP, l1=NHYP, l2=NHYP, score=NHYP,
                         masked=NHYP)
        S = signals(ctx, nc, name, **sigs)
        block = ctx.enter_context(nc.Block())

        def slots(p, back):
            s = p - back
            return (s // H, s % H, ORDER[s % H]) if 0 <= s < SLOTN else None

        def use_of(j):
            return NHYP + NORMAL.index(j)

        def wait_units(eng, n, j):
            for e in ("act", "dve"):
                m = len(share[e])
                if m:
                    eng.wait_ge(S[e].sem, S[e].at(n, (j + 1) * m))

        @block.sync
        def _(sp):
            def load(n, u):
                for x, which, dst in ((0, Q_PART, q), (1, K_PART, k)):
                    rowsd = parts_dram[n, x].rearrange("(h d) k t -> d h k t", d=hd)
                    for s, part in enumerate(which):
                        sp.dma_start(dst[s * hd:(s + 1) * hd, u], rowsd[:, :, part, :]).then_inc(qk_loaded[u], 16)
                sp.dma_start(vp[:, u].rearrange("p t h w -> p (t h w)"), v_dram[n]).then_inc(v_loaded[u], 16)

            def pair(i, more):
                for u in range(2):
                    n = 2 * i + u
                    if more:
                        sp.wait_ge(S["s"].sem, S["s"].at(n))
                        sp.wait_ge(S["pv"].sem, S["pv"].at(n))
                        load(n + 2, u)
                    sp.wait_ge(S["out"].sem, S["out"].at(n))
                    sp.dma_start(ctx_dram[n].rearrange("(t p) d -> p t d", p=R),
                                 out[:, u].rearrange("p t h w -> p t (h w)")).then_inc(stored[u], 16)

            for u in range(2):
                load(u, u)
            with sp.Fori(0, NB // 2 - 1) as i:
                pair(i, True)
            pair(NB // 2 - 1, False)
            for u in range(2):
                sp.wait_ge(stored[u], 16 * (NB // 2))

        if NHYP:
            @block.gpsimd
            def _(pool):
                pool.dma_start(negc[:], curv_dram.rearrange("(a h) -> a h", a=1).broadcast_to([R, 4]))\
                    .then_inc(curv_loaded, 16)
                nc.gpsimd.memset(one[:], 1.0)
                nc.gpsimd.memset(eps6[:], 1e-6).then_inc(ready, 1)
                pool.wait_ge(curv_loaded, 16)
                pool.wait_ge(ready, 1)
                nc.gpsimd.tensor_tensor(root_ic[:], negc[:], c["minus_half"][:, 0:4], ALU.pow).then_inc(ready, 1)
                pool.wait_ge(ready, 2)
                nc.gpsimd.tensor_scalar(negc[:], negc[:], -1.0, None, ALU.mult).then_inc(ready, 1)

        @block.tensor
        def _(pe):
            for x in ("s", "turn", "pv", "back"):
                S[x].give(pe)

            def scores(n, u, h, use):
                banks = SETS[use % len(SETS)]
                for t in QORDER:
                    b, col = QTILE[t]
                    w = width[t]
                    out_ = ps[0:R, banks[b], col:col + w]
                    masked = causal and kinds[h] != HYP
                    if masked:
                        nc.tensor.matmul(ps[0:R, banks[b], col + t * R:col + w], c["identb"][0:R, 0:R],
                                         c["mask_qk"][:], start=True, stop=False, skip_group_check=True)
                    last = nc.tensor.matmul(out_, q[:, u, h, t * R:(t + 1) * R], k[:, u, h, 0:w],
                                            start=not masked, stop=True, skip_group_check=masked)
                    if col + w == T or not causal:
                        last.then_inc(S["s"].sem, 1)

            def body(i):
                for p in range(STEPS):
                    if slot := slots(p, 0):
                        u, j, h = slot
                        n = 2 * i + u
                        if j == 0:
                            pe.wait_ge(qk_loaded[u], 16 * 2 * SLOTS * (i + 1))
                            for a, hh in enumerate(HYPS):
                                if a < 2:
                                    pe.wait_ge(S["exp"].sem, S["exp"].at(n, (NORMAL[a - 2] - H + 1) * NT))
                                else:
                                    pe.wait_ge(S["w"].sem, S["w"].at(n, a - 1))
                                scores(n, u, hh, a)
                        if kinds[h] != HYP:
                            use = use_of(j)
                            before = use - len(SETS)
                            if before < 0:
                                pe.wait_ge(S["exp"].sem, S["exp"].at(n, (j - 1 + 1) * NT))
                            elif before < NHYP:
                                pe.wait_ge(S["w"].sem, S["w"].at(n, before + 1))
                            else:
                                pe.wait_ge(S["exp"].sem, S["exp"].at(n, (NORMAL[before - NHYP] + 1) * NT))
                            scores(n, u, h, use)
                    if slot := slots(p, 1 + LOOK):
                        u, j, h = slot
                        n = 2 * i + u
                        pe.wait_ge(S["exp"].sem, S["exp"].at(n, (j + 1) * NT))
                        wait_units(pe, n, j - 1)
                        for kt in range(NT):
                            b, col = KTILE[kt]
                            q0 = kt if causal else 0
                            for t in range(q0, NT):
                                last = nc.tensor.transpose(
                                    ps[0:R, TURN[b], col + (t - q0) * R:col + (t - q0 + 1) * R],
                                    prob[:, j % 2, t, kt * R:(kt + 1) * R], c["ident"][0:R, 0:R])
                            if not causal or kt != 1:
                                last.then_inc(S["turn"].sem, 1)
                    if (slot := slots(p, 2 + LOOK)) and slot[1] % 4 == 3:
                        u, j, h = slot
                        n, g = 2 * i + u, j // 4
                        if g == 0:
                            pe.wait_ge(v_loaded[u], 16 * (i + 1))
                        wait_units(pe, n, j)
                        pe.wait_ge(S["oT"].sem, S["oT"].at(n, g))
                        for kt in range(NT):
                            b, col = KTILE[kt]
                            q0 = kt * R if causal else 0
                            for a in range(4):
                                last = nc.tensor.matmul(ps[32 * a:32 * a + VW, 6, q0:T],
                                                        vp[:, u, kt, ORDER[4 * g + a], :],
                                                        probT[:, (4 * g + a) % 8, b, col:col + T - q0],
                                                        start=(kt == 0), stop=(kt == NT - 1),
                                                        tile_position=(0, 32 * a))
                        last.then_inc(S["pv"].sem, 1)
                    if (slot := slots(p, 3 + LOOK)) and slot[1] % 4 == 3:
                        u, j, h = slot
                        n, g = 2 * i + u, j // 4
                        pe.wait_ge(S["oT"].sem, S["oT"].at(n, g + 1))
                        pe.wait_ge(S["out"].sem, S["out"].at(n, g))
                        for t in range(NT):
                            last = nc.tensor.transpose(ps[0:R, 7, t * 128:(t + 1) * 128],
                                                       oT[:, g % 2, t * R:(t + 1) * R], c["ident"][:])
                        last.then_inc(S["back"].sem, 1)

            with pe.Fori(0, NB // 2) as i:
                body(i)

        def evacuate(eng, copy, which, n, u, j):
            for x, m in enumerate(share[which]):
                eng.wait_ge(S["turn"].sem, S["turn"].at(n, j * UNITS + m + 1))
                if x == 0:
                    eng.wait_ge(S["pv"].sem, S["pv"].at(n, j // 4 - 1))
                copy(probT[:, j % 8, m, :], ps[0:R, TURN[m], 0:T]).then_inc(S[which].sem, 1)

        @block.scalar
        def _(act):
            for x in ("exp", "act", "oT") + (("hl", "root", "l1", "l2", "score") if NHYP else ()):
                S[x].give(act)
            if NHYP:
                act.wait_ge(ready, 3)

            def body(i):
                for p in range(STEPS):
                    slot = slots(p, 0)
                    if NHYP and slot and slot[1] == 2:
                        n = 2 * i + slot[0]
                        for a in range(NHYP):
                            act.wait_ge(S["hu"].sem, S["hu"].at(n, a + 1))
                            nc.scalar.activation(hu[:, a], hu[:, a], ACT.Ln).then_inc(S["hl"].sem, 1)
                        for a in range(NHYP):
                            act.wait_ge(S["hl"].sem, S["hl"].at(n, a + 1))
                            nc.scalar.activation(hu[:, a], hu[:, a], ACT.Exp, scale=0.5).then_inc(S["root"].sem, 1)
                    if NHYP and slot and slot[1] == 5:
                        n = 2 * i + slot[0]
                        for a in range(NHYP):
                            act.wait_ge(S["z"].sem, S["z"].at(n, a + 1))
                            nc.scalar.activation(hw[:, a], hw[:, a], ACT.Ln, bias=one[:]).then_inc(S["l1"].sem, 1)
                        for a in range(NHYP):
                            act.wait_ge(S["l1"].sem, S["l1"].at(n, a + 1))
                            nc.scalar.activation(hw[:, a], hw[:, a], ACT.Ln, bias=eps6[:],
                                                 scale=root_ic[:, a:a + 1]).then_inc(S["l2"].sem, 1)
                        for a in range(NHYP):
                            act.wait_ge(S["l2"].sem, S["l2"].at(n, a + 1))
                            nc.scalar.activation(hw[:, a], hw[:, a], ACT.Exp, scale=-1.0).then_inc(S["score"].sem, 1)
                    if slot := slots(p, LOOK):
                        u, j, h = slot
                        n = 2 * i + u
                        act.wait_ge(S["turn"].sem, S["turn"].at(n, (j - 1) * UNITS))
                        for x, t in enumerate(QORDER):
                            b, col = QTILE[t]
                            if kinds[h] == HYP:
                                src = hw[:, HYPS.index(h), b, col:col + width[t]]
                            else:
                                src = ps[0:R, SETS[use_of(j) % len(SETS)][b], col:col + width[t]]
                                act.wait_ge(S["s"].sem, S["s"].at(n, use_of(j) * UNITS + b + 1))
                            if kinds[h] == COS:
                                e = nc.scalar.activation(prob[:, j % 2, t, 0:width[t]], src, ACT.Exp,
                                                         scale=float(HD) ** 0.5)
                            else:
                                m = MAXED.index(j) * NT + (NT if causal else x + 1)
                                act.wait_ge(S["neg"].sem, S["neg"].at(n, m))
                                e = nc.scalar.activation(prob[:, j % 2, t, 0:width[t]], src, ACT.Exp,
                                                         bias=neg[:, j % 4, t:t + 1])
                            e.then_inc(S["exp"].sem, 1)
                    if slot := slots(p, 1 + LOOK):
                        u, j, h = slot
                        evacuate(act, nc.scalar.copy, "act", 2 * i + u, u, j)
                    if (slot := slots(p, 2 + LOOK)) and slot[1] % 4 == 3:
                        u, j, h = slot
                        n, g = 2 * i + u, j // 4
                        act.wait_ge(S["pv"].sem, S["pv"].at(n, g + 1))
                        act.wait_ge(S["back"].sem, S["back"].at(n, g - 1))
                        nc.scalar.copy(oT[:, g % 2], ps[:, 6, 0:T]).then_inc(S["oT"].sem, 1)

            with act.Fori(0, NB // 2) as i:
                body(i)

        @block.vector
        def _(dve):
            for x in ("neg", "dve", "rec", "out") + (("w", "wc", "hu", "z", "masked") if NHYP else ()):
                S[x].give(dve)
            if NHYP:
                dve.wait_ge(ready, 3)

            def body(i):
                for p in range(STEPS):
                    slot = slots(p, 0)
                    if NHYP and slot and slot[1] == 0:
                        n = 2 * i + slot[0]
                        dve.wait_ge(S["exp"].sem, S["exp"].at(n, (ORDER.index(HYPS[-1]) - H + 1) * NT))
                        for a, hh in enumerate(HYPS):
                            dve.wait_ge(S["s"].sem, S["s"].at(n, (a + 1) * UNITS))
                            b = SETS[a % 2][0]
                            nc.vector.tensor_scalar(hw[:, a], ps[0:R, b:b + 2, 0:T], negc[:, a:a + 1], -1.0,
                                                    ALU.mult, ALU.add).then_inc(S["w"].sem, 1)
                        for a in range(NHYP):
                            dve.wait_ge(S["w"].sem, S["w"].at(n, a + 1))
                            nc.vector.tensor_scalar(hw[:, a], hw[:, a], 2.0 ** -23, None, ALU.max)\
                                .then_inc(S["wc"].sem, 1)
                        for a in range(NHYP):
                            dve.wait_ge(S["wc"].sem, S["wc"].at(n, a + 1))
                            nc.vector.scalar_tensor_tensor(out=hu[:, a], in0=hw[:, a], scalar=2.0, in1=hw[:, a],
                                                           op0=ALU.add, op1=ALU.mult).then_inc(S["hu"].sem, 1)
                    if NHYP and slot and slot[1] == 4:
                        n = 2 * i + slot[0]
                        for a in range(NHYP):
                            dve.wait_ge(S["root"].sem, S["root"].at(n, a + 1))
                            nc.vector.tensor_tensor(hw[:, a], hw[:, a], hu[:, a], ALU.add).then_inc(S["z"].sem, 1)
                    if NHYP and slot and slot[1] == 7:
                        n = 2 * i + slot[0]
                        for a in range(NHYP):
                            dve.wait_ge(S["score"].sem, S["score"].at(n, a + 1))
                            for t in QORDER:
                                b, col = QTILE[t]
                                d = hw[:, a, b, col + t * R:col + (t + 1) * R]
                                last = nc.vector.tensor_tensor(d, d, c["mask_qk"][:], ALU.add)
                            last.then_inc(S["masked"].sem, 1)
                    if slot and kinds[slot[2]] != COS:
                        u, j, h = slot
                        n = 2 * i + u
                        dve.wait_ge(S["exp"].sem, S["exp"].at(n, (j - 3) * NT))
                        for t in QORDER:
                            b, col = QTILE[t]
                            if kinds[h] == HYP:
                                a = HYPS.index(h)
                                dve.wait_ge(S["masked"].sem, S["masked"].at(n, a + 1))
                                src = hw[:, a, b, col:col + width[t]]
                            else:
                                dve.wait_ge(S["s"].sem, S["s"].at(n, use_of(j) * UNITS + b + 1))
                                src = ps[0:R, SETS[use_of(j) % len(SETS)][b], col:col + width[t]]
                            nc.vector.tensor_reduce(neg[:, j % 4, t:t + 1], src, AX.X, ALU.max, negate=True)\
                                .then_inc(S["neg"].sem, 1)
                    if slot := slots(p, 1 + LOOK):
                        u, j, h = slot
                        evacuate(dve, nc.vector.tensor_copy, "dve", 2 * i + u, u, j)
                    if (slot := slots(p, 3 + LOOK)) and slot[1] % 4 == 3:
                        u, j, h = slot
                        n, g = 2 * i + u, j // 4
                        if g == 0:
                            dve.wait_ge(stored[u], 16 * i)
                        dve.wait_ge(S["back"].sem, S["back"].at(n, g + 1))
                        dve.wait_ge(S["out"].sem, S["out"].at(n, g - 1))
                        x = ps[0:R, 7, 0:NT * 128].rearrange("p (t a w) -> p t a w", t=NT, a=4)
                        nc.vector.reciprocal(rec[:, g % 2], x[:, :, :, HD]).then_inc(S["rec"].sem, 1)
                        dve.wait_ge(S["rec"].sem, S["rec"].at(n, g + 1))
                        h0 = ORDER[4 * g]
                        nc.vector.tensor_tensor(out[:, u, :, h0:h0 + 4, :], x[:, :, :, 0:HD],
                                                rec[:, g % 2].unsqueeze(3).to_broadcast([R, NT, 4, HD]), ALU.mult)\
                            .then_inc(S["out"].sem, 1)

            with dve.Fori(0, NB // 2) as i:
                body(i)


def row(dram):
    return dram.rearrange("(a d) -> a d", a=1)


def phase_g1(nc, c, ps, NB, ctx_dram, h2_dram, proj_dram, projb_dram, wq_dram, wk_dram, wv_dram,
             bq_dram, bk_dram, bv_dram, h3_dram, x3_dram, parts_dram, v_dram):
    ctx = ExitStack()
    with ctx:
        def sb(name, shape, dt=F32):
            return ctx.enter_context(nc.sbuf_tensor("p_" + name, shape, dt))

        def sem(name):
            return nc.alloc_semaphore("p_" + name)

        proj, wv = sb("proj", [128, CT, D]), sb("wv", [128, CT, D])
        wqk = sb("wqk", [128, CT, 2, D])
        bqk = sb("bqk", [128, 2, CT])
        projb, bv = sb("projb", [R, D]), sb("bv", [R, D])
        cx = sb("cx", [R, 2, NT, D])
        cT = sb("cT", [128, 2, CT, T])
        h = sb("h", [R, 2, NT, D])
        stats = sb("stats", [R, 2, NT, 6])
        mv = sb("mv", [R, 2, NT, 2])
        var_eps = sb("var_eps", [R, 2, NT])
        rstd = sb("rstd", [R, 2, NT])
        xn = sb("xn", [R, 2, NT, D])
        xT = sb("xT", [128, 2, CT, T])
        parts = sb("parts", [128, 2, 2 * CT, PARTS, T], BF16)
        rest = sb("rest", [128, 2, 2, T])
        vp = sb("vp", [R, 2, NT, H, VW])
        w_loaded, scaled, filled = sem("w_loaded"), sem("scaled"), sem("filled")
        c_loaded = [sem(f"c_loaded{u}") for u in range(2)]
        h_loaded = [sem(f"h_loaded{u}") for u in range(2)]
        h_stored = [sem(f"h_stored{u}") for u in range(2)]
        x_stored = [sem(f"x_stored{u}") for u in range(2)]
        p_stored = [sem(f"p_stored{u}") for u in range(2)]
        v_stored = [sem(f"v_stored{u}") for u in range(2)]
        S = signals(ctx, nc, "p", cT=1, cT_out=1, y=1, hb=1, h3=1, bn=NT + 1, mv=1, eps=1, rstd=1, xn=NT, xT=1,
                    xT_out=1, v=1, v_out=2, qk=2 * CT, hi=2 * CT, rest=2 * CT, mid=2 * CT, lo=2 * CT)
        banks = [lambda k, u=u: ps[:, 4 * u + k, :] for u in range(2)]
        QK_BANK = (2, 3, 0, 1)
        WEIGHTS = 16 * (4 + 2 * CT + 2)
        block = ctx.enter_context(nc.Block())

        @block.sync
        def _(sp):
            def load_c(n, u):
                sp.dma_start(cx[:, u], ctx_dram[n].rearrange("(t p) d -> p t d", p=R)).then_inc(c_loaded[u], 16)

            def load_h(n, u):
                sp.dma_start(h[:, u], h2_dram[n].rearrange("(t p) d -> p t d", p=R)).then_inc(h_loaded[u], 16)

            def pair(i, more):
                for u in range(2):
                    n = 2 * i + u
                    if more:
                        sp.wait_ge(S["cT"].sem, S["cT"].at(n))
                        load_c(n + 2, u)
                for u in range(2):
                    n = 2 * i + u
                    sp.wait_ge(S["h3"].sem, S["h3"].at(n))
                    sp.dma_start(h3_dram[n].rearrange("(t p) d -> p t d", p=R), h[:, u]).then_inc(h_stored[u], 16)
                for u in range(2):
                    n = 2 * i + u
                    sp.wait_ge(S["xn"].sem, S["xn"].at(n))
                    sp.dma_start(x3_dram[n].rearrange("(t p) d -> p t d", p=R), xn[:, u]).then_inc(x_stored[u], 16)
                    if more:
                        sp.wait_ge(h_stored[u], 16 * i + 16)
                        load_h(n + 2, u)
                for u in range(2):
                    n = 2 * i + u
                    sp.wait_ge(S["v_out"].sem, S["v_out"].at(n))
                    sp.dma_start(v_dram[n], vp[:, u].rearrange("p t h w -> p (t h w)")).then_inc(v_stored[u], 16)
                for u in range(2):
                    n = 2 * i + u
                    for j in range(2 * CT):
                        sp.wait_ge(S["lo"].sem, S["lo"].at(n, j + 1))
                        sp.dma_start(parts_dram[n, j // CT, (j % CT) * 128:(j % CT + 1) * 128]
                                     .rearrange("r k t -> r (k t)"),
                                     parts[:, u, j].rearrange("p k t -> p (k t)")).then_inc(p_stored[u], 16)

            sp.dma_start(wqk[:, :, 0], wq_dram.rearrange("(k p) n -> p k n", p=128)).then_inc(w_loaded, 16)
            sp.dma_start(wqk[:, :, 1], wk_dram.rearrange("(k p) n -> p k n", p=128)).then_inc(w_loaded, 16)
            sp.dma_start(proj[:], proj_dram.rearrange("(k p) n -> p k n", p=128)).then_inc(w_loaded, 16)
            sp.dma_start(wv[:], wv_dram.rearrange("(k p) n -> p k n", p=128)).then_inc(w_loaded, 16)
            for j, dram in enumerate((bq_dram, bk_dram)):
                for k in range(CT):
                    sp.dma_start(bqk[:, j, k:k + 1], dram[k * 128:(k + 1) * 128].rearrange("(p a) -> p a", a=1))\
                        .then_inc(w_loaded, 16)
            sp.dma_start(projb[:], row(projb_dram).broadcast_to([R, D])).then_inc(w_loaded, 16)
            sp.dma_start(bv[:], row(bv_dram).broadcast_to([R, D])).then_inc(w_loaded, 16)
            for u in range(2):
                load_c(u, u)
                load_h(u, u)
            with sp.Fori(0, NB // 2 - 1) as i:
                pair(i, True)
            pair(NB // 2 - 1, False)
            for u in range(2):
                for s, times in ((h_stored, 1), (x_stored, 1), (p_stored, 2 * CT), (v_stored, 1)):
                    sp.wait_ge(s[u], 16 * times * (NB // 2))

        @block.gpsimd
        def _(pool):
            for k in ("hb", "eps", "rstd"):
                S[k].give(pool)
            pool.wait_ge(w_loaded, WEIGHTS)
            with pool.Fori(0, NB // 2) as i:
                for u in range(2):
                    n = 2 * i + u
                    pool.wait_ge(h_loaded[u], 16 * i + 16)
                    nc.gpsimd.tensor_tensor(h[:, u], h[:, u], projb[:].unsqueeze(1).to_broadcast([R, NT, D]), ALU.add)\
                        .then_inc(S["hb"].sem, 1)
                for u in range(2):
                    ln_rstd(nc, pool, c, mv[:, u], var_eps[:, u], rstd[:, u],
                            S["mv"], S["eps"], S["rstd"], 2 * i + u)

        @block.scalar
        def _(act):
            for k in ("cT_out", "xT_out", "hi", "mid"):
                S[k].give(act)
            act.wait_ge(scaled, 2)
            with act.Fori(0, NB // 2) as i:
                for u in range(2):
                    n = 2 * i + u
                    act.wait_ge(S["cT"].sem, S["cT"].at(n))
                    act.wait_ge(S["y"].sem, S["y"].before(n))
                    nc.scalar.copy(cT[:, u], ps[:, 4 * u + 2:4 * u + 4, 0:T]).then_inc(S["cT_out"].sem, 1)
                for u in range(2):
                    n = 2 * i + u
                    act.wait_ge(S["xT"].sem, S["xT"].at(n))
                    act.wait_ge(S["qk"].sem, S["qk"].before(n))
                    nc.scalar.copy(xT[:, u], ps[:, 4 * u + 2:4 * u + 4, 0:T]).then_inc(S["xT_out"].sem, 1)
                for u in range(2):
                    n, B = 2 * i + u, banks[u]
                    act.wait_ge(p_stored[u], 16 * 2 * CT * i)
                    for j in range(2 * CT):
                        act.wait_ge(S["qk"].sem, S["qk"].at(n, j + 1))
                        nc.scalar.activation(parts[:, u, j, 0, :], B(QK_BANK[j])[:, 0:T], ACT.Identity,
                                             bias=bqk[:, j // CT, j % CT:j % CT + 1]).then_inc(S["hi"].sem, 1)
                        act.wait_ge(S["rest"].sem, S["rest"].at(n, j + 1))
                        nc.scalar.copy(parts[:, u, j, 1, :], rest[:, u, j % 2]).then_inc(S["mid"].sem, 1)

        @block.vector
        def _(dve):
            for k in ("h3", "bn", "mv", "xn", "v_out", "rest", "lo"):
                S[k].give(dve)
            dve.wait_ge(w_loaded, WEIGHTS)
            nc.vector.tensor_scalar(wqk[:, :, 0], wqk[:, :, 0], float(HD) ** -0.5, None, ALU.mult).then_inc(scaled, 1)
            nc.vector.tensor_scalar(bqk[:, 0], bqk[:, 0], float(HD) ** -0.5, None, ALU.mult).then_inc(scaled, 1)
            nc.vector.memset(vp[:], 1.0).then_inc(filled, 1)
            dve.wait_ge(filled, 1)
            dve.wait_ge(scaled, 2)
            with dve.Fori(0, NB // 2) as i:
                for u in range(2):
                    n, B = 2 * i + u, banks[u]
                    dve.wait_ge(S["y"].sem, S["y"].at(n))
                    dve.wait_ge(S["hb"].sem, S["hb"].at(n))
                    nc.vector.tensor_tensor(h[:, u, 0:2, :], B(0)[0:R, :].rearrange("p (t d) -> p t d", t=2),
                                            h[:, u, 0:2, :], ALU.add)
                    nc.vector.tensor_tensor(h[:, u, 2, :], B(1)[0:R, 0:D], h[:, u, 2, :], ALU.add)\
                        .then_inc(S["h3"].sem, 1)
                for u in range(2):
                    n = 2 * i + u
                    dve.wait_ge(S["h3"].sem, S["h3"].at(n))
                    ln_stats(nc, dve, h[:, u], stats[:, u], mv[:, u], (S["bn"].sem, S["bn"].at(n)), S["mv"])
                for u in range(2):
                    n = 2 * i + u
                    dve.wait_ge(S["rstd"].sem, S["rstd"].at(n))
                    dve.wait_ge(S["xT"].sem, S["xT"].before(n))
                    dve.wait_ge(x_stored[u], 16 * i)
                    ln_apply(nc, xn[:, u], h[:, u], mv[:, u], rstd[:, u], S["xn"])
                for u in range(2):
                    n, B = 2 * i + u, banks[u]
                    dve.wait_ge(S["v"].sem, S["v"].at(n))
                    dve.wait_ge(v_stored[u], 16 * i)
                    bias = bv[:].rearrange("p (h w) -> p h w", w=HD)
                    for t in range(NT):
                        x = B(t // 2)[0:R, (t % 2) * D:(t % 2 + 1) * D].rearrange("p (h w) -> p h w", w=HD)
                        last = nc.vector.tensor_tensor(vp[:, u, t, :, 0:HD], x, bias, ALU.add)
                        if t > 0:
                            last.then_inc(S["v_out"].sem, 1)
                for u in range(2):
                    n, B = 2 * i + u, banks[u]
                    for j in range(2 * CT):
                        dve.wait_ge(S["hi"].sem, S["hi"].at(n, j + 1))
                        if j >= 2:
                            dve.wait_ge(S["lo"].sem, S["lo"].at(n, j - 1))
                        nc.vector.scalar_tensor_tensor(out=rest[:, u, j % 2], in0=B(QK_BANK[j])[:, 0:T],
                                                       scalar=bqk[:, j // CT, j % CT:j % CT + 1],
                                                       in1=parts[:, u, j, 0, :], op0=ALU.add, op1=ALU.subtract)\
                            .then_inc(S["rest"].sem, 1)
                        dve.wait_ge(S["mid"].sem, S["mid"].at(n, j + 1))
                        nc.vector.tensor_tensor(parts[:, u, j, 2, :], rest[:, u, j % 2], parts[:, u, j, 1, :],
                                                ALU.subtract).then_inc(S["lo"].sem, 1)

        @block.tensor
        def _(pe):
            for k in ("cT", "y", "xT", "v", "qk"):
                S[k].give(pe)
            pe.wait_ge(w_loaded, WEIGHTS)
            pe.wait_ge(scaled, 1)
            with pe.Fori(0, NB // 2) as i:
                for u in range(2):
                    n, B = 2 * i + u, banks[u]
                    pe.wait_ge(c_loaded[u], 16 * i + 16)
                    pe.wait_ge(S["lo"].sem, S["lo"].before(n))
                    transpose_tokens(nc, pe, c, cx[:, u], lambda k: B(2 + k)).then_inc(S["cT"].sem, 1)
                for u in range(2):
                    n, B = 2 * i + u, banks[u]
                    pe.wait_ge(S["cT_out"].sem, S["cT_out"].at(n))
                    for t in range(NT):
                        for k in range(CT):
                            last = nc.tensor.matmul(B(t // 2)[0:R, (t % 2) * D:(t % 2 + 1) * D],
                                                    cT[:, u, k, t * R:(t + 1) * R], proj[:, k, :],
                                                    start=(k == 0), stop=(k == CT - 1))
                    last.then_inc(S["y"].sem, 1)
                for u in range(2):
                    n, B = 2 * i + u, banks[u]
                    pe.wait_ge(S["xn"].sem, S["xn"].at(n))
                    transpose_tokens(nc, pe, c, xn[:, u], lambda k: B(2 + k)).then_inc(S["xT"].sem, 1)
                for u in range(2):
                    n, B = 2 * i + u, banks[u]
                    pe.wait_ge(S["xT_out"].sem, S["xT_out"].at(n))
                    pe.wait_ge(S["h3"].sem, S["h3"].at(n))
                    for t in range(NT):
                        for k in range(CT):
                            last = nc.tensor.matmul(B(t // 2)[0:R, (t % 2) * D:(t % 2 + 1) * D],
                                                    xT[:, u, k, t * R:(t + 1) * R], wv[:, k, :],
                                                    start=(k == 0), stop=(k == CT - 1))
                    last.then_inc(S["v"].sem, 1)
                for u in range(2):
                    n, B = 2 * i + u, banks[u]
                    for j in range(2 * CT):
                        if j >= 2:
                            pe.wait_ge(S["v_out"].sem, S["v_out"].at(n, j - 1))
                        for k in range(CT):
                            last = nc.tensor.matmul(B(QK_BANK[j])[:, 0:T],
                                                    wqk[:, k, j // CT, (j % CT) * 128:(j % CT + 1) * 128],
                                                    xT[:, u, k, :], start=(k == 0), stop=(k == CT - 1))
                        last.then_inc(S["qk"].sem, 1)


def phase_g3(nc, c, ps, NB, ctx_dram, x3_dram, h3_dram, wo_dram, bo_dram, g1_dram, be1_dram, wg_dram, bg_dram,
             we_dram, bexp_dram, g2_dram, be2_dram, out_dram):
    ctx = ExitStack()
    E, PE_ = EXPERTS, EXPERTS // 2
    with ctx:
        def sb(name, shape, dt=F32):
            return ctx.enter_context(nc.sbuf_tensor("m_" + name, shape, dt))

        def sem(name):
            return nc.alloc_semaphore("m_" + name)

        wo, wg = sb("wo", [128, CT, D]), sb("wg", [128, CT, E])
        we = sb("we", [128, CT, E, D])
        bexp = sb("bexp", [E, D])
        rows = {k: sb(k, [R, D]) for k in ("bo", "g1", "be1", "g2", "be2")}
        bg = sb("bg", [R, E])
        lower = sb("lower", [R, E, E])
        cx = sb("cx", [R, 2, NT, D])
        x = sb("x", [R, 2, NT, D])
        h = sb("h", [R, 2, NT, D])
        cT = sb("cT", [128, 2, CT, T])
        xT = sb("xT", [128, 2, CT, T])
        a = sb("a", [R, 2, NT, D])
        ag = sb("ag", [R, 2, NT, D])
        acc = sb("acc", [R, 2, NT, D])
        accg = sb("accg", [R, 2, NT, D])
        stats = sb("stats", [R, 2, NT, 6])
        mv = sb("mv", [R, 2, NT, 2])
        var_eps = sb("var_eps", [R, 2, NT])
        rstd = sb("rstd", [R, 2, NT])
        logit = sb("logit", [R, 2 * NT, E])
        top = sb("top", [R, 2 * NT])
        shifted = sb("shifted", [R, 2 * NT, E])
        expl = sb("expl", [R, 2 * NT, E])
        total = sb("total", [R, 2 * NT])
        greater = sb("greater", [R, 2 * NT, E, E])
        equal = sb("equal", [R, 2 * NT, E, E])
        rank = sb("rank", [R, 2 * NT, E])
        chosen = sb("chosen", [R, 2 * NT, E])
        weight = sb("weight", [R, 2 * NT, E])
        weightT = sb("weightT", [E, 2, T])
        w_loaded, filled = sem("w_loaded"), sem("filled")
        c_loaded = [sem(f"c_loaded{u}") for u in range(2)]
        x_loaded = [sem(f"x_loaded{u}") for u in range(2)]
        h_loaded = [sem(f"h_loaded{u}") for u in range(2)]
        stored = [sem(f"stored{u}") for u in range(2)]
        M = PE_ * NT
        EARLY = 2
        S = signals(ctx, nc, "m", cT=1, cT_out=1, y=1, xb=1, hb=1, a=1, bn=NT + 1, mv=1, eps=1, rstd=1, an=NT, ag=1,
                    x4=1, xT=1, xT_out=1, gl=1, logit=1, wT=1, wT_out=1, bias=1, acc0=1, early=EARLY, me=M - EARLY, acc=2 * M,
                    hx=1, bn2=NT + 1, mv2=1, eps2=1, rstd2=1, accn=NT, accg=1, out=1)
        G = signals(ctx, nc, "mg", top=1, shifted=1, exp=1, greater=1, equal=1, lower=1, above=1, rank=1,
                    total=1, inv=1, chosen=1, weight=1)
        banks = [lambda k, u=u: ps[:, 4 * u + k, :] for u in range(2)]
        block = ctx.enter_context(nc.Block())

        @block.sync
        def _(sp):
            def tokens(dram):
                return dram.rearrange("(t p) d -> p t d", p=R)

            def pair(i, more):
                for u in range(2):
                    n = 2 * i + u
                    if more:
                        sp.wait_ge(S["cT"].sem, S["cT"].at(n))
                        sp.dma_start(cx[:, u], tokens(ctx_dram[n + 2])).then_inc(c_loaded[u], 16)
                for u in range(2):
                    n = 2 * i + u
                    if more:
                        sp.wait_ge(S["xT"].sem, S["xT"].at(n))
                        sp.wait_ge(S["hx"].sem, S["hx"].at(n))
                        sp.dma_start(x[:, u], tokens(x3_dram[n + 2])).then_inc(x_loaded[u], 16)
                for u in range(2):
                    n = 2 * i + u
                    sp.wait_ge(S["out"].sem, S["out"].at(n))
                    sp.dma_start(tokens(out_dram[n]), h[:, u]).then_inc(stored[u], 16)
                for u in range(2):
                    n = 2 * i + u
                    if more:
                        sp.wait_ge(stored[u], 16 * i + 16)
                        sp.dma_start(h[:, u], tokens(h3_dram[n + 2])).then_inc(h_loaded[u], 16)

            sp.dma_start(wo[:], wo_dram.rearrange("(k p) n -> p k n", p=128)).then_inc(w_loaded, 16)
            sp.dma_start(wg[:], wg_dram.rearrange("(k p) n -> p k n", p=128)).then_inc(w_loaded, 16)
            for e in range(E):
                sp.dma_start(we[:, :, e], we_dram[e].rearrange("(k p) n -> p k n", p=128)).then_inc(w_loaded, 16)
            sp.dma_start(bexp[:], bexp_dram).then_inc(w_loaded, 16)
            for k, dram in (("bo", bo_dram), ("g1", g1_dram), ("be1", be1_dram), ("g2", g2_dram), ("be2", be2_dram)):
                sp.dma_start(rows[k][:], row(dram).broadcast_to([R, D])).then_inc(w_loaded, 16)
            sp.dma_start(bg[:], row(bg_dram).broadcast_to([R, E])).then_inc(w_loaded, 16)
            for u in range(2):
                sp.dma_start(cx[:, u], tokens(ctx_dram[u])).then_inc(c_loaded[u], 16)
                sp.dma_start(x[:, u], tokens(x3_dram[u])).then_inc(x_loaded[u], 16)
                sp.dma_start(h[:, u], tokens(h3_dram[u])).then_inc(h_loaded[u], 16)
            with sp.Fori(0, NB // 2 - 1) as i:
                pair(i, True)
            pair(NB // 2 - 1, False)
            for u in range(2):
                sp.wait_ge(stored[u], 16 * (NB // 2))

        WEIGHTS = 16 * (2 + E + 1 + 5 + 1)

        def everywhere(k):
            return rows[k][:].unsqueeze(1).to_broadcast([R, NT, D])

        @block.gpsimd
        def _(pool):
            for k in ("xb", "hb", "eps", "rstd", "hx", "eps2", "rstd2"):
                S[k].give(pool)
            nc.gpsimd.memset(lower[:], 1.0).then_inc(filled, 1)
            pool.wait_ge(filled, 1)
            nc.gpsimd.affine_select(out=lower[:], in_=lower[:], compare_op=ALU.is_gt, fill=0.0, base=0,
                                    pattern=[[1, E], [-1, E]], channel_multiplier=0).then_inc(filled, 1)
            pool.wait_ge(w_loaded, WEIGHTS)
            with pool.Fori(0, NB // 2) as i:
                for u in range(2):
                    n = 2 * i + u
                    pool.wait_ge(x_loaded[u], 16 * i + 16)
                    nc.gpsimd.tensor_tensor(x[:, u], x[:, u], everywhere("be1"), ALU.add).then_inc(S["xb"].sem, 1)
                for u in range(2):
                    ln_rstd(nc, pool, c, mv[:, u], var_eps[:, u], rstd[:, u],
                            S["mv"], S["eps"], S["rstd"], 2 * i + u)
                for u in range(2):
                    n = 2 * i + u
                    pool.wait_ge(h_loaded[u], 16 * i + 16)
                    nc.gpsimd.tensor_tensor(h[:, u], h[:, u], everywhere("be2"), ALU.add).then_inc(S["hb"].sem, 1)
                    pool.wait_ge(S["hb"].sem, S["hb"].at(n))
                    pool.wait_ge(S["x4"].sem, S["x4"].at(n))
                    nc.gpsimd.tensor_tensor(h[:, u], h[:, u], x[:, u], ALU.add).then_inc(S["hx"].sem, 1)
                for u in range(2):
                    ln_rstd(nc, pool, c, mv[:, u], var_eps[:, u], rstd[:, u],
                            S["mv2"], S["eps2"], S["rstd2"], 2 * i + u)

        @block.scalar
        def _(act):
            for k in ("cT_out", "xT_out", "wT_out", "acc0"):
                S[k].give(act)
            G["exp"].give(act)
            with act.Fori(0, NB // 2) as i:
                for u in range(2):
                    n = 2 * i + u
                    act.wait_ge(S["cT"].sem, S["cT"].at(n))
                    act.wait_ge(S["y"].sem, S["y"].before(n))
                    nc.scalar.copy(cT[:, u], ps[:, 4 * u + 2:4 * u + 4, 0:T]).then_inc(S["cT_out"].sem, 1)
                for u in range(2):
                    n = 2 * i + u
                    act.wait_ge(S["xT"].sem, S["xT"].at(n))
                    act.wait_ge(S["me"].sem, S["me"].before(n))
                    nc.scalar.copy(xT[:, u], ps[:, 4 * u + 2:4 * u + 4, 0:T]).then_inc(S["xT_out"].sem, 1)
                act.wait_ge(G["shifted"].sem, G["shifted"].at(i))
                act.wait_ge(G["chosen"].sem, G["chosen"].at(i - 1))
                nc.scalar.activation(expl[:], shifted[:], ACT.Exp).then_inc(G["exp"].sem, 1)
                for u in range(2):
                    n = 2 * i + u
                    act.wait_ge(S["wT"].sem, S["wT"].at(n))
                    act.wait_ge(S["bias"].sem, S["bias"].before(n))
                    nc.scalar.copy(weightT[:, u], banks[u](1)[0:E, 0:T]).then_inc(S["wT_out"].sem, 1)
                for u in range(2):
                    n, B = 2 * i + u, banks[u]
                    act.wait_ge(S["bias"].sem, S["bias"].at(n))
                    act.wait_ge(S["accg"].sem, S["accg"].before(n))
                    nc.scalar.copy(acc[:, u, 0:2], B(0)[0:R, :].rearrange("p (t d) -> p t d", t=2))
                    nc.scalar.copy(acc[:, u, 2], B(1)[0:R, 0:D]).then_inc(S["acc0"].sem, 1)

        @block.vector
        def _(dve):
            for k in ("a", "bn", "mv", "an", "ag", "x4", "logit", "acc", "bn2", "mv2", "accn", "accg", "out"):
                S[k].give(dve)
            for k in G:
                if k != "exp":
                    G[k].give(dve)
            dve.wait_ge(w_loaded, WEIGHTS)
            dve.wait_ge(filled, 2)
            with dve.Fori(0, NB // 2) as i:
                for u in range(2):
                    n, B = 2 * i + u, banks[u]
                    dve.wait_ge(S["y"].sem, S["y"].at(n))
                    dve.wait_ge(S["ag"].sem, S["ag"].before(n))
                    for t in range(NT):
                        last = nc.vector.tensor_tensor(a[:, u, t], B(t // 2)[0:R, (t % 2) * D:(t % 2 + 1) * D],
                                                       rows["bo"][:], ALU.add)
                    last.then_inc(S["a"].sem, 1)
                for u in range(2):
                    n = 2 * i + u
                    dve.wait_ge(S["a"].sem, S["a"].at(n))
                    ln_stats(nc, dve, a[:, u], stats[:, u], mv[:, u], (S["bn"].sem, S["bn"].at(n)), S["mv"])
                for u in range(2):
                    n = 2 * i + u
                    dve.wait_ge(S["rstd"].sem, S["rstd"].at(n))
                    ln_apply(nc, a[:, u], a[:, u], mv[:, u], rstd[:, u], S["an"])
                for u in range(2):
                    n = 2 * i + u
                    dve.wait_ge(S["an"].sem, S["an"].at(n))
                    dve.wait_ge(S["x4"].sem, S["x4"].before(n))
                    nc.vector.tensor_tensor(ag[:, u], a[:, u], everywhere("g1"), ALU.mult).then_inc(S["ag"].sem, 1)
                for u in range(2):
                    n = 2 * i + u
                    dve.wait_ge(S["ag"].sem, S["ag"].at(n))
                    dve.wait_ge(S["xb"].sem, S["xb"].at(n))
                    nc.vector.tensor_tensor(x[:, u], x[:, u], ag[:, u], ALU.add).then_inc(S["x4"].sem, 1)
                for u in range(2):
                    n = 2 * i + u
                    dve.wait_ge(S["gl"].sem, S["gl"].at(n))
                    nc.vector.tensor_tensor(logit[:, u * NT:(u + 1) * NT],
                                            banks[u](1)[0:R, D:D + NT * E].rearrange("p (t e) -> p t e", e=E),
                                            bg[:].unsqueeze(1).to_broadcast([R, NT, E]), ALU.add)\
                        .then_inc(S["logit"].sem, 1)
                dve.wait_ge(S["logit"].sem, S["logit"].at(2 * i + 1))
                nc.vector.reduce_max(top[:], logit[:], AX.X).then_inc(G["top"].sem, 1)
                dve.wait_ge(G["top"].sem, G["top"].at(i))
                nc.vector.tensor_tensor(shifted[:], logit[:], top[:].unsqueeze(2).to_broadcast([R, 2 * NT, E]),
                                        ALU.subtract).then_inc(G["shifted"].sem, 1)
                every = [R, 2 * NT, E, E]
                other, own = logit[:].unsqueeze(2).to_broadcast(every), logit[:].unsqueeze(3).to_broadcast(every)
                nc.vector.tensor_tensor(equal[:], other, own, ALU.is_equal).then_inc(G["equal"].sem, 1)
                nc.vector.tensor_tensor(greater[:], other, own, ALU.is_gt).then_inc(G["greater"].sem, 1)
                dve.wait_ge(G["equal"].sem, G["equal"].at(i))
                nc.vector.tensor_tensor(equal[:], equal[:], lower[:].unsqueeze(1).to_broadcast(every), ALU.mult)\
                    .then_inc(G["lower"].sem, 1)
                dve.wait_ge(G["greater"].sem, G["greater"].at(i))
                dve.wait_ge(G["lower"].sem, G["lower"].at(i))
                nc.vector.tensor_tensor(equal[:], equal[:], greater[:], ALU.add).then_inc(G["above"].sem, 1)
                dve.wait_ge(G["above"].sem, G["above"].at(i))
                nc.vector.reduce_sum(rank[:], equal[:], AX.X).then_inc(G["rank"].sem, 1)
                dve.wait_ge(G["exp"].sem, G["exp"].at(i))
                nc.vector.reduce_sum(total[:], expl[:], AX.X).then_inc(G["total"].sem, 1)
                dve.wait_ge(G["rank"].sem, G["rank"].at(i))
                nc.vector.scalar_tensor_tensor(out=chosen[:], in0=rank[:], scalar=2.0, in1=expl[:],
                                               op0=ALU.is_lt, op1=ALU.mult).then_inc(G["chosen"].sem, 1)
                dve.wait_ge(G["total"].sem, G["total"].at(i))
                nc.vector.reciprocal(total[:], total[:]).then_inc(G["inv"].sem, 1)
                dve.wait_ge(G["inv"].sem, G["inv"].at(i))
                dve.wait_ge(G["chosen"].sem, G["chosen"].at(i))
                nc.vector.tensor_tensor(weight[:], chosen[:], total[:].unsqueeze(2).to_broadcast([R, 2 * NT, E]),
                                        ALU.mult).then_inc(G["weight"].sem, 1)
                dve.wait_ge(G["weight"].sem, G["weight"].at(i))
                for u in range(2):
                    n, B = 2 * i + u, banks[u]
                    dve.wait_ge(S["acc0"].sem, S["acc0"].at(n))
                    for m in range(M):
                        p, t = divmod(m, NT)
                        if m < EARLY:
                            dve.wait_ge(S["early"].sem, S["early"].at(n, m + 1))
                        else:
                            dve.wait_ge(S["me"].sem, S["me"].at(n, m + 1 - EARLY))
                        for j in range(2):
                            if m >= NT or j:
                                dve.wait_ge(S["acc"].sem, S["acc"].at(n, 2 * m + 1 if j else 2 * (m - NT) + 2))
                            nc.vector.scalar_tensor_tensor(out=acc[:, u, t], in0=B(2 + m % 2)[0:R, j * D:(j + 1) * D],
                                                           scalar=weight[:, u * NT + t, 2 * p + j:2 * p + j + 1],
                                                           in1=acc[:, u, t], op0=ALU.mult, op1=ALU.add)\
                                .then_inc(S["acc"].sem, 1)
                for u in range(2):
                    n = 2 * i + u
                    dve.wait_ge(S["acc"].sem, S["acc"].at(n))
                    ln_stats(nc, dve, acc[:, u], stats[:, u], mv[:, u], (S["bn2"].sem, S["bn2"].at(n)), S["mv2"])
                for u in range(2):
                    n = 2 * i + u
                    dve.wait_ge(S["rstd2"].sem, S["rstd2"].at(n))
                    ln_apply(nc, acc[:, u], acc[:, u], mv[:, u], rstd[:, u], S["accn"])
                for u in range(2):
                    n = 2 * i + u
                    dve.wait_ge(S["accn"].sem, S["accn"].at(n))
                    dve.wait_ge(S["out"].sem, S["out"].before(n))
                    nc.vector.tensor_tensor(accg[:, u], acc[:, u], everywhere("g2"), ALU.mult)\
                        .then_inc(S["accg"].sem, 1)
                for u in range(2):
                    n = 2 * i + u
                    dve.wait_ge(S["accg"].sem, S["accg"].at(n))
                    dve.wait_ge(S["hx"].sem, S["hx"].at(n))
                    nc.vector.tensor_tensor(h[:, u], h[:, u], accg[:, u], ALU.add).then_inc(S["out"].sem, 1)

        @block.tensor
        def _(pe):
            for k in ("cT", "y", "xT", "gl", "early", "me", "wT", "bias"):
                S[k].give(pe)
            pe.wait_ge(w_loaded, WEIGHTS)

            def experts(n, u, ms):
                B = banks[u]
                for m in ms:
                    p, t = divmod(m, NT)
                    if m >= 2:
                        pe.wait_ge(S["acc"].sem, S["acc"].at(n, 2 * (m - 2) + 2))
                    for k in range(CT):
                        last = nc.tensor.matmul(B(2 + m % 2)[0:R, :], xT[:, u, k, t * R:(t + 1) * R],
                                                we[:, k, 2 * p:2 * p + 2, :].rearrange("p e d -> p (e d)"),
                                                start=(k == 0), stop=(k == CT - 1))
                    last.then_inc(S["early" if m < EARLY else "me"].sem, 1)

            with pe.Fori(0, NB // 2) as i:
                for u in range(2):
                    n, B = 2 * i + u, banks[u]
                    pe.wait_ge(c_loaded[u], 16 * i + 16)
                    pe.wait_ge(S["acc"].sem, S["acc"].before(n))
                    transpose_tokens(nc, pe, c, cx[:, u], lambda k: B(2 + k)).then_inc(S["cT"].sem, 1)
                for u in range(2):
                    n, B = 2 * i + u, banks[u]
                    pe.wait_ge(S["cT_out"].sem, S["cT_out"].at(n))
                    pe.wait_ge(S["acc0"].sem, S["acc0"].before(n))
                    for t in range(NT):
                        for k in range(CT):
                            last = nc.tensor.matmul(B(t // 2)[0:R, (t % 2) * D:(t % 2 + 1) * D],
                                                    cT[:, u, k, t * R:(t + 1) * R], wo[:, k, :],
                                                    start=(k == 0), stop=(k == CT - 1))
                    last.then_inc(S["y"].sem, 1)
                for u in range(2):
                    n, B = 2 * i + u, banks[u]
                    pe.wait_ge(S["x4"].sem, S["x4"].at(n))
                    transpose_tokens(nc, pe, c, x[:, u], lambda k: B(2 + k)).then_inc(S["xT"].sem, 1)
                for u in range(2):
                    n, B = 2 * i + u, banks[u]
                    pe.wait_ge(S["xT_out"].sem, S["xT_out"].at(n))
                    for t in range(NT):
                        for k in range(CT):
                            last = nc.tensor.matmul(B(1)[0:R, D + t * E:D + (t + 1) * E],
                                                    xT[:, u, k, t * R:(t + 1) * R], wg[:, k, :],
                                                    start=(k == 0), stop=(k == CT - 1))
                    last.then_inc(S["gl"].sem, 1)
                for u in range(2):
                    experts(2 * i + u, u, range(EARLY))
                for u in range(2):
                    n, B = 2 * i + u, banks[u]
                    pe.wait_ge(G["weight"].sem, G["weight"].at(i))
                    for t in range(NT):
                        last = nc.tensor.transpose(B(1)[0:E, t * R:(t + 1) * R], weight[:, u * NT + t, :],
                                                   c["ident"][0:R, 0:R])
                    last.then_inc(S["wT"].sem, 1)
                for u in range(2):
                    n, B = 2 * i + u, banks[u]
                    pe.wait_ge(S["wT_out"].sem, S["wT_out"].at(n))
                    for t in range(NT):
                        last = nc.tensor.matmul(B(t // 2)[0:R, (t % 2) * D:(t % 2 + 1) * D],
                                                weightT[:, u, t * R:(t + 1) * R], bexp[:], start=True, stop=True)
                    last.then_inc(S["bias"].sem, 1)
                for u in range(2):
                    experts(2 * i + u, u, range(EARLY, M))


def program(nc, NB, patches, txt, rot, wtok, a_wq, a_wk, a_wv, a_wo, gate_w, up_w, down_w,
            wqkv, curv, proj, projb, f_wq, f_bq, f_wk, f_bk, f_wv, f_bv, f_wo, f_bo, g1, be1, g2, be2,
            wg, bg, we, bexp, out):
    def scratch(name, shape, dt=F32):
        return nc.dram_tensor("s_" + name, shape, dt, kind="Internal").ap()

    tokens = [NB, T, D]
    h1, h2, h3, x3, ctx1, ctx2 = (scratch(n, tokens) for n in ("h1", "h2", "h3", "x3", "ctx1", "ctx2"))
    x0 = scratch("x0", [NB, D, T])
    gate, up, gated, o = (scratch(n, [NB, 128, FT * T]) for n in ("gate", "up", "gated", "o"))
    parts1 = scratch("parts1", [NB, 2, H * HD1, PARTS, T], BF16)
    parts2 = scratch("parts2", [NB, 2, H * HD, PARTS, T], BF16)
    v1, v2 = (scratch(n, [NB, R, NT * H * VW]) for n in ("v1", "v2"))
    ctx = ExitStack()
    with ctx:
        ps = ctx.enter_context(nc.psum_tensor("ps", [128, 8, 512], F32))

        def run(stage, *args):
            with nc.cleanup_on_exit():
                stage(nc, *args)

        c = setup_constants(nc, ctx, rot)
        with ExitStack() as ffn:
            def sb(name, shape):
                return ffn.enter_context(nc.sbuf_tensor("k_" + name, shape, F32))

            gateT, upT, downT = sb("gateT", [128, CT, FF]), sb("upT", [128, CT, FF]), sb("downT", [128, FT, D])
            quantised = ("x", "gate", "up", "gated", "o")
            amax = {k: sb("amax_" + k, [128, 2]) for k in quantised}
            scale = {k: sb("scale_" + k, [128, 1]) for k in quantised}
            inv = {k: sb("inv_" + k, [128, 1]) for k in quantised}
            magic = sb("magic", [128, 1])
            with nc.Block() as block:
                @block.vector
                def _(dve):
                    nc.vector.memset(magic[:], MAGIC)
                    for k in quantised:
                        nc.vector.memset(amax[k][:], 0.0)

            def fix_scale(k):
                run(set_scale, "z_" + k, amax[k][:], scale[k][:], inv[k][:])

            run(quantise_weights, c, ps, gate_w, up_w, down_w, gateT, upT, downT)
            run(phase_a, c, ps, NB, patches, txt, wtok, a_wq, a_wk, a_wv, a_wo, h1, x0, amax["x"][0:R])
            fix_scale("x")
            run(phase_b, ps, NB, magic[:], x0, gateT, upT, scale["x"][:], inv["x"][:], gate, up,
                    amax["gate"], amax["up"])
            fix_scale("gate")
            fix_scale("up")
            run(phase_c, NB, magic[:], gate, scale["gate"][:], inv["gate"][:], gated, amax["gated"])
            fix_scale("gated")
            run(phase_d, NB, magic[:], gated, up, scale["gated"][:], inv["gated"][:], scale["up"][:], inv["up"][:],
                    o, amax["o"])
            fix_scale("o")
            run(phase_f1, c, ps, NB, magic[:], o, h1, downT, scale["o"][:], inv["o"][:], wqkv, curv, h2, parts1, v1)
        run(attention_core, c, ps, NB, "g", KINDS, True, HD1, parts1, v1, ctx1, curv)
        run(phase_g1, c, ps, NB, ctx1, h2, proj, projb, f_wq, f_wk, f_wv, f_bq, f_bk, f_bv, h3, x3, parts2, v2)
        run(attention_core, c, ps, NB, "e", [SDPA] * H, False, HD, parts2, v2, ctx2)
        run(phase_g3, c, ps, NB, ctx2, x3, h3, f_wo, f_bo, g1, be1, wg, bg, we, bexp, g2, be2, out)


def kernel(**inputs):
    import concourse.bacc as bacc
    from concourse.bass_utils import run_bass_kernel_spmd

    a = {k: np.asarray(v) for k, v in inputs.items()}
    NB = a["x"].shape[0]
    P = 16
    side = a["x"].shape[-1] // P
    patches = a["x"].reshape(NB, 3, side, P, side, P).transpose(0, 1, 3, 5, 2, 4).reshape(NB, 3 * P * P, side * side)
    frequencies = 1.0 / 10000.0 ** (np.arange(0, HD, 2, dtype=np.float32) / HD)
    angles = np.outer(np.arange(T, dtype=np.float32), frequencies).astype(np.float32)
    cos, sin = np.cos(angles), np.sin(angles)
    rot = np.stack([np.concatenate([cos, cos], 1), np.concatenate([sin, -sin], 1)]).astype(np.float32)

    def ffn(*names):
        return [a["L1_ffn_" + k] for k in names]

    arrays = [patches, a["txt"], rot, a["L0_tok_W"].T] + [a["L0_attn_W" + k] for k in "qkvo"]
    arrays += [a["L0_ffn_w_" + k] for k in ("gate", "up", "down")]
    arrays += [a["L1_attn_qkv_w"].T, a["L1_attn_curvature"].reshape(4), a["L1_attn_proj_w"].T, a["L1_attn_proj_b"]]
    arrays += ffn("Wq", "bq", "Wk", "bk", "Wv", "bv", "Wo", "bo", "g1", "be1", "g2", "be2", "Wg", "bg", "We", "bexp")
    nc = bacc.Bacc("TRN2", target_bir_lowering=False, num_devices=1)
    named, args = {}, []
    for i, x in enumerate(arrays):
        x = np.ascontiguousarray(x)
        named[f"in_{i}"] = x
        args.append(nc.dram_tensor(f"in_{i}", x.shape, mybir.dt.from_np(x.dtype), kind="ExternalInput").ap())
    args.append(nc.dram_tensor("out_0", [NB, T, D], F32, kind="ExternalOutput").ap())
    program(nc, NB, *args)
    return run_bass_kernel_spmd(nc, [named], core_ids=[0]).results[0]["out_0"]
```

```python
import numpy as np
import concourse.bass as bass
from concourse import mybir
from contextlib import ExitStack

F32 = mybir.dt.float32
BF16 = mybir.dt.bfloat16
ALU = mybir.AluOpType
ACT = mybir.ActivationFunctionType
AX = mybir.AxisListType

D = 256
CT = D // 128
PATCHES, TEXT = 196, 77
T = PATCHES + TEXT
R = 91
NT = T // R
P_LAST = PATCHES - (NT - 1) * R
KP = 768 // 128
FF = 768
FT = FF // 128
QBLOCK = 32
H, HD = 16, 16
EXPERTS = 8
EPS = 1e-5
NEG = -1e30
MAGIC = 12582912.0
QMAX = 32767.0


class Signal:

    def __init__(self, nc, name, per, skew):
        self.sem, self.per, self.start = nc.alloc_semaphore(name), per, 2 * per + skew

    def give(self, engine):
        engine.sem_inc(self.sem, self.start)

    def at(self, n, count=None):
        done = self.start + (self.per if count is None else count)
        if isinstance(n, tuple):
            return n[0] * (2 * self.per) + (n[1] * self.per + done)
        return n * self.per + done

    def before(self, n):
        return self.at(n, -self.per)


def signals(ctx, nc, prefix, **pers):
    return {k: Signal(nc, f"{prefix}_{k}", per, skew) for skew, (k, per) in enumerate(pers.items())}


def setup_constants(nc, ctx, rot_dram):
    c = {}
    for name, shape, dt in (("ident", [128, 128], F32), ("identb", [128, 128], BF16),
                            ("mask_qk", [R, R], BF16), ("mask_kq", [R, R], BF16),
                            ("minus_half", [R, 64], F32), ("eps", [R, NT], F32),
                            ("cos", [R, NT, HD], F32), ("sin", [R, NT, HD], F32)):
        c[name] = ctx.enter_context(nc.sbuf_tensor("c_" + name, shape, dt))
    filled = nc.alloc_semaphore("const_filled")
    loaded = nc.alloc_semaphore("const_loaded")
    with nc.Block() as block:
        @block.gpsimd
        def _(pool):
            fills = (("ident", 0.0), ("identb", 0.0), ("mask_qk", 0.0), ("mask_kq", 0.0),
                     ("minus_half", -0.5), ("eps", EPS))
            for name, value in fills:
                nc.gpsimd.memset(c[name][:], value).then_inc(filled, 1)
            pool.wait_ge(filled, len(fills))
            for name in ("ident", "identb"):
                nc.gpsimd.affine_select(out=c[name][:], in_=c[name][:], compare_op=ALU.not_equal,
                                        fill=1.0, base=0, pattern=[[-1, 128]], channel_multiplier=1)
            nc.gpsimd.affine_select(out=c["mask_qk"][:], in_=c["mask_qk"][:], compare_op=ALU.is_ge,
                                    fill=NEG, base=0, pattern=[[-1, R]], channel_multiplier=1)
            nc.gpsimd.affine_select(out=c["mask_kq"][:], in_=c["mask_kq"][:], compare_op=ALU.is_ge,
                                    fill=NEG, base=0, pattern=[[1, R]], channel_multiplier=-1)

        @block.sync
        def _(sp):
            for k, name in enumerate(("cos", "sin")):
                sp.dma_start(c[name][:], rot_dram[k].rearrange("(t p) d -> p t d", p=R)).then_inc(loaded, 16)
            sp.wait_ge(loaded, 32)
    return c


def ln_stats(nc, dve, x, stats, mv, bn, s_mv):
    for t in range(NT):
        nc.vector.bn_stats(stats[:, t, :], x[:, t, :]).then_inc(bn[0], 1)
    dve.wait_ge(bn[0], bn[1] - 1)
    dve.sem_inc(bn[0], 1)
    for t in range(NT):
        last = nc.vector.bn_aggr(mv[:, t, :], stats[:, t, :])
    last.then_inc(s_mv.sem, 1)


def ln_apply(nc, out, x, mv, rstd, done):
    for t in range(NT):
        nc.vector.tensor_scalar(out[:, t, :], x[:, t, :], mv[:, t, 0:1], rstd[:, t:t + 1],
                                ALU.subtract, ALU.mult).then_inc(done.sem, 1)


def ln_rstd(nc, pool, c, mv, var_eps, rstd, s_mv, s_eps, s_rstd, n):
    pool.wait_ge(s_mv.sem, s_mv.at(n))
    pool.wait_ge(s_rstd.sem, s_rstd.before(n))
    nc.gpsimd.tensor_tensor(var_eps[:], mv[:, :, 1], c["eps"][:, 0:NT], ALU.add).then_inc(s_eps.sem, 1)
    pool.wait_ge(s_eps.sem, s_eps.at(n))
    nc.gpsimd.tensor_tensor(rstd[:], var_eps[:], c["minus_half"][:, 0:NT], ALU.pow).then_inc(s_rstd.sem, 1)


def transpose_tokens(nc, pe, c, x, banks):
    for ct in range(CT):
        for t in range(NT):
            last = nc.tensor.transpose(banks(ct)[:, t * R:(t + 1) * R],
                                       x[:, t, ct * 128:(ct + 1) * 128], c["ident"][0:R, 0:R])
    return last


def phase_a(nc, c, ps, NB, patches_dram, txt_dram, wtok_dram, wq_dram, wk_dram, wv_dram, wo_dram,
            h1_dram, x0_dram, amax_x):
    ctx = ExitStack()
    with ctx:
        def sb(name, shape, dt=F32):
            return ctx.enter_context(nc.sbuf_tensor("a_" + name, shape, dt))

        def sem(name):
            return nc.alloc_semaphore("a_" + name)

        wtok = sb("wtok", [128, KP, D])
        wq, wk, wv, wo = (sb(n, [128, CT, D]) for n in ("wq", "wk", "wv", "wo"))
        patches = sb("patches", [128, 2, KP, PATCHES])
        h = sb("h", [R, 2, NT, D])
        stats = sb("stats", [R, 2, NT, 6])
        mv = sb("mv", [R, 2, NT, 2])
        var_eps = sb("var_eps", [R, 2, NT])
        rstd = sb("rstd", [R, 2, NT])
        xn = sb("xn", [R, 2, NT, D])
        xT = sb("xT", [128, 2, CT, T])
        qT = sb("qT", [128, 2, CT, T])
        kT = sb("kT", [128, 2, CT, T])
        v = sb("v", [R, 2, NT, D])
        mx = sb("mx", [R, 2, NT])
        nb = sb("nb", [R, 2, NT])
        prob = sb("prob", [R, 2, NT, T])
        den = sb("den", [R, 2, NT])
        rden = sb("rden", [R, 2, NT])
        probT = sb("probT", [R, 2, 2, T])
        aT = sb("aT", [128, 2, CT, T])
        x0T = sb("x0T", [128, 2, CT, T])
        amax_new = sb("amax_new", [R, 2, 1])

        w_loaded = sem("w_loaded")
        patches_loaded = [sem(f"patches_loaded{u}") for u in range(2)]
        txt_loaded = [sem(f"txt_loaded{u}") for u in range(2)]
        h1_stored = [sem(f"h1_stored{u}") for u in range(2)]
        x0_stored = [sem(f"x0_stored{u}") for u in range(2)]
        amax_step = sem("amax_step")
        S = signals(ctx, nc, "a", tok=1, tok_out=2, bn=NT + 1, mv=1, eps=1, rstd=1, xn=NT, xT=1, xT_out=1,
                    qk=1, qk_out=2, v=1, v_out=1, s=NT, mx=NT, nb=1, p=NT, pT=1, pT_out=1, a=1,
                    a_out=1, rden=1, y=1, h1=1, bn2=NT + 1, mv2=1, eps2=1, rstd2=1, x0=NT, x0T=1, x0T_out=1,
                    amr=1, amax=1)
        banks = [lambda k, u=u: ps[:, 4 * u + k, :] for u in range(2)]
        causal = {0: (1, 182), 1: (1, 0), 2: (0, 0)}
        scale = float(D) ** -0.5

        block = ctx.enter_context(nc.Block())

        @block.sync
        def _(sp):
            def load_patches(n, u):
                sp.dma_start(patches[:, u], patches_dram[n].rearrange("(k p) n -> p k n", p=128))\
                    .then_inc(patches_loaded[u], 16)

            def load_text(n, u):
                sp.dma_start(h[P_LAST:R, u, NT - 1, :], txt_dram[n]).then_inc(txt_loaded[u], 16)

            def pair(i, more):
                for u in range(2):
                    n = 2 * i + u
                    if more:
                        sp.wait_ge(S["tok"].sem, S["tok"].at(n))
                        load_patches(n + 2, u)
                for u in range(2):
                    n = 2 * i + u
                    sp.wait_ge(S["h1"].sem, S["h1"].at(n))
                    sp.dma_start(h1_dram[n].rearrange("(t p) d -> p t d", p=R), h[:, u])\
                        .then_inc(h1_stored[u], 16)
                for u in range(2):
                    n = 2 * i + u
                    if more:
                        sp.wait_ge(S["x0"].sem, S["x0"].at(n))
                        sp.wait_ge(h1_stored[u], 16 * i + 16)
                        load_text(n + 2, u)
                    sp.wait_ge(S["x0T_out"].sem, S["x0T_out"].at(n))
                    sp.dma_start(x0_dram[n].rearrange("(c p) t -> p c t", p=128), x0T[:, u])\
                        .then_inc(x0_stored[u], 16)

            sp.dma_start(wtok[:], wtok_dram.rearrange("(k p) n -> p k n", p=128)).then_inc(w_loaded, 16)
            for w, dram in ((wq, wq_dram), (wk, wk_dram), (wv, wv_dram), (wo, wo_dram)):
                sp.dma_start(w[:], dram.rearrange("(k p) n -> p k n", p=128)).then_inc(w_loaded, 16)
            for u in range(2):
                load_patches(u, u)
                load_text(u, u)
            with sp.Fori(0, NB // 2 - 1) as i:
                pair(i, True)
            pair(NB // 2 - 1, False)
            for u in range(2):
                sp.wait_ge(h1_stored[u], 16 * (NB // 2))
                sp.wait_ge(x0_stored[u], 16 * (NB // 2))

        @block.gpsimd
        def _(pool):
            for k in ("eps", "rstd", "eps2", "rstd2"):
                S[k].give(pool)
            with pool.Fori(0, NB // 2) as i:
                for u in range(2):
                    ln_rstd(nc, pool, c, mv[:, u], var_eps[:, u], rstd[:, u],
                            S["mv"], S["eps"], S["rstd"], 2 * i + u)
                for u in range(2):
                    ln_rstd(nc, pool, c, mv[:, u], var_eps[:, u], rstd[:, u],
                            S["mv2"], S["eps2"], S["rstd2"], 2 * i + u)

        @block.scalar
        def _(act):
            for k in ("tok_out", "xT_out", "v_out", "p", "a_out", "x0T_out"):
                S[k].give(act)
            with act.Fori(0, NB // 2) as i:
                for u in range(2):
                    n, B = 2 * i + u, banks[u]
                    act.wait_ge(S["tok"].sem, S["tok"].at(n))
                    act.wait_ge(S["x0"].sem, S["x0"].before(n))
                    act.wait_ge(h1_stored[u], 16 * i)
                    nc.scalar.copy(h[:, u, 0:2, :], B(0)[0:R, :].rearrange("p (t d) -> p t d", t=2))\
                        .then_inc(S["tok_out"].sem, 1)
                    nc.scalar.copy(h[0:P_LAST, u, 2, :], B(1)[0:P_LAST, 0:D]).then_inc(S["tok_out"].sem, 1)
                for u in range(2):
                    n, B = 2 * i + u, banks[u]
                    act.wait_ge(S["xT"].sem, S["xT"].at(n))
                    act.wait_ge(S["v"].sem, S["v"].before(n))
                    nc.scalar.copy(xT[:, u], ps[:, 4 * u + 2:4 * u + 4, 0:T]).then_inc(S["xT_out"].sem, 1)
                for u in range(2):
                    n, B = 2 * i + u, banks[u]
                    act.wait_ge(S["v"].sem, S["v"].at(n))
                    act.wait_ge(S["a"].sem, S["a"].before(n))
                    nc.scalar.copy(v[:, u, 0:2, :], B(0)[0:R, :].rearrange("p (t d) -> p t d", t=2))
                    nc.scalar.copy(v[:, u, 2, :], B(1)[0:R, 0:D]).then_inc(S["v_out"].sem, 1)
                for u in range(2):
                    n = 2 * i + u
                    act.wait_ge(S["nb"].sem, S["nb"].at(n))
                    act.wait_ge(S["pT"].sem, S["pT"].before(n))
                    act.wait_ge(S["rden"].sem, S["rden"].before(n))
                    for t in range(NT):
                        bank, col = causal[t]
                        w = (t + 1) * R
                        nc.scalar.activation(prob[:, u, t, 0:w], banks[u](bank + 2)[0:R, col:col + w], ACT.Exp,
                                             bias=nb[:, u, t:t + 1], scale=scale,
                                             accum_out=den[:, u, t:t + 1]).then_inc(S["p"].sem, 1)
                for u in range(2):
                    n = 2 * i + u
                    act.wait_ge(S["a"].sem, S["a"].at(n))
                    act.wait_ge(S["y"].sem, S["y"].before(n))
                    nc.scalar.copy(aT[:, u], ps[:, 4 * u + 2:4 * u + 4, 0:T]).then_inc(S["a_out"].sem, 1)
                for u in range(2):
                    n = 2 * i + u
                    act.wait_ge(S["x0T"].sem, S["x0T"].at(n))
                    act.wait_ge(x0_stored[u], 16 * i)
                    nc.scalar.copy(x0T[:, u], ps[:, 4 * u + 2:4 * u + 4, 0:T]).then_inc(S["x0T_out"].sem, 1)

        @block.vector
        def _(dve):
            for k in ("bn", "mv", "xn", "qk_out", "mx", "nb", "pT_out", "rden", "h1", "bn2", "mv2", "x0",
                      "amr", "amax"):
                S[k].give(dve)
            nc.vector.memset(amax_x[:], 0.0).then_inc(amax_step, 1)
            dve.wait_ge(amax_step, 1)
            with dve.Fori(0, NB // 2) as i:
                for u in range(2):
                    n = 2 * i + u
                    dve.wait_ge(S["tok_out"].sem, S["tok_out"].at(n))
                    dve.wait_ge(txt_loaded[u], 16 * i + 16)
                    dve.wait_ge(S["x0"].sem, S["x0"].before(n))
                    dve.wait_ge(S["rstd2"].sem, S["rstd2"].before(n))
                    ln_stats(nc, dve, h[:, u], stats[:, u], mv[:, u], (S["bn"].sem, S["bn"].at(n)), S["mv"])
                for u in range(2):
                    n = 2 * i + u
                    dve.wait_ge(S["rstd"].sem, S["rstd"].at(n))
                    dve.wait_ge(S["x0T"].sem, S["x0T"].before(n))
                    dve.wait_ge(S["amr"].sem, S["amr"].before(n))
                    ln_apply(nc, xn[:, u], h[:, u], mv[:, u], rstd[:, u], S["xn"])
                for u in range(2):
                    n = 2 * i + u
                    dve.wait_ge(S["qk"].sem, S["qk"].at(n))
                    dve.wait_ge(S["s"].sem, S["s"].before(n))
                    nc.vector.tensor_copy(qT[:, u], ps[:, 4 * u:4 * u + 2, 0:T]).then_inc(S["qk_out"].sem, 1)
                    nc.vector.tensor_copy(kT[:, u], ps[:, 4 * u + 2:4 * u + 4, 0:T]).then_inc(S["qk_out"].sem, 1)
                for u in range(2):
                    n = 2 * i + u
                    dve.wait_ge(S["s"].sem, S["s"].at(n))
                    dve.wait_ge(S["nb"].sem, S["nb"].before(n))
                    for t in range(NT):
                        bank, col = causal[t]
                        nc.vector.reduce_max(mx[:, u, t:t + 1], banks[u](bank + 2)[0:R, col:col + (t + 1) * R], AX.X)\
                            .then_inc(S["mx"].sem, 1)
                    dve.wait_ge(S["mx"].sem, S["mx"].at(n))
                    dve.wait_ge(S["p"].sem, S["p"].before(n))
                    nc.vector.tensor_scalar(nb[:, u], mx[:, u], -scale, None, ALU.mult).then_inc(S["nb"].sem, 1)
                for u in range(2):
                    n = 2 * i + u
                    dve.wait_ge(S["pT"].sem, S["pT"].at(n))
                    dve.wait_ge(S["a"].sem, S["a"].before(n))
                    nc.vector.tensor_copy(probT[:, u], ps[0:R, 4 * u:4 * u + 2, 0:T]).then_inc(S["pT_out"].sem, 1)
                    dve.wait_ge(S["p"].sem, S["p"].at(n))
                    nc.vector.reciprocal(rden[:, u], den[:, u]).then_inc(S["rden"].sem, 1)
                for u in range(2):
                    n, B = 2 * i + u, banks[u]
                    dve.wait_ge(S["y"].sem, S["y"].at(n))
                    dve.wait_ge(S["rden"].sem, S["rden"].at(n))
                    dve.wait_ge(S["xn"].sem, S["xn"].at(n))
                    for t in range(NT):
                        y = B(t // 2)[0:R, (t % 2) * D:(t % 2 + 1) * D]
                        last = nc.vector.scalar_tensor_tensor(out=h[:, u, t, :], in0=y, scalar=rden[:, u, t:t + 1],
                                                              in1=h[:, u, t, :], op0=ALU.mult, op1=ALU.add)
                    last.then_inc(S["h1"].sem, 1)
                for u in range(2):
                    n = 2 * i + u
                    dve.wait_ge(S["h1"].sem, S["h1"].at(n))
                    ln_stats(nc, dve, h[:, u], stats[:, u], mv[:, u], (S["bn2"].sem, S["bn2"].at(n)), S["mv2"])
                for u in range(2):
                    n = 2 * i + u
                    dve.wait_ge(S["rstd2"].sem, S["rstd2"].at(n))
                    dve.wait_ge(S["xT"].sem, S["xT"].at(n))
                    ln_apply(nc, xn[:, u], h[:, u], mv[:, u], rstd[:, u], S["x0"])
                for u in range(2):
                    n = 2 * i + u
                    dve.wait_ge(S["x0"].sem, S["x0"].at(n))
                    dve.wait_ge(S["amax"].sem, S["amax"].before(n))
                    nc.vector.tensor_reduce(amax_new[:, u], xn[:, u].rearrange("p t d -> p (t d)"), AX.X, ALU.max,
                                            apply_absolute_value=True).then_inc(S["amr"].sem, 1)
                    dve.wait_ge(S["amr"].sem, S["amr"].at(n))
                    nc.vector.tensor_tensor(amax_x[:, u:u + 1], amax_x[:, u:u + 1], amax_new[:, u], ALU.max)\
                        .then_inc(S["amax"].sem, 1)

        @block.tensor
        def _(pe):
            for k in ("tok", "xT", "qk", "v", "s", "pT", "a", "y", "x0T"):
                S[k].give(pe)
            pe.wait_ge(w_loaded, 16 * 5)
            with pe.Fori(0, NB // 2) as i:
                for u in range(2):
                    n, B = 2 * i + u, banks[u]
                    pe.wait_ge(patches_loaded[u], 16 * i + 16)
                    pe.wait_ge(S["h1"].sem, S["h1"].before(n))
                    for t in range(NT):
                        m = R if t < NT - 1 else P_LAST
                        for k in range(KP):
                            last = nc.tensor.matmul(B(t // 2)[0:m, (t % 2) * D:(t % 2 + 1) * D],
                                                    patches[:, u, k, t * R:t * R + m], wtok[:, k, :],
                                                    start=(k == 0), stop=(k == KP - 1))
                    last.then_inc(S["tok"].sem, 1)
                for u in range(2):
                    n, B = 2 * i + u, banks[u]
                    pe.wait_ge(S["xn"].sem, S["xn"].at(n))
                    pe.wait_ge(S["x0T_out"].sem, S["x0T_out"].before(n))
                    transpose_tokens(nc, pe, c, xn[:, u], lambda k: B(2 + k)).then_inc(S["xT"].sem, 1)
                for u in range(2):
                    n, B = 2 * i + u, banks[u]
                    pe.wait_ge(S["xT_out"].sem, S["xT_out"].at(n))
                    pe.wait_ge(S["tok_out"].sem, S["tok_out"].at(n))
                    for m in range(2 * CT):
                        w = (wq, wk)[m // CT]
                        for k in range(CT):
                            last = nc.tensor.matmul(B(m)[:, 0:T], w[:, k, (m % CT) * 128:(m % CT + 1) * 128],
                                                    xT[:, u, k, :], start=(k == 0), stop=(k == CT - 1))
                    last.then_inc(S["qk"].sem, 1)
                for u in range(2):
                    n, B = 2 * i + u, banks[u]
                    pe.wait_ge(S["qk_out"].sem, S["qk_out"].at(n, 1))
                    for t in range(NT):
                        for k in range(CT):
                            last = nc.tensor.matmul(B(t // 2)[0:R, (t % 2) * D:(t % 2 + 1) * D],
                                                    xT[:, u, k, t * R:(t + 1) * R], wv[:, k, :],
                                                    start=(k == 0), stop=(k == CT - 1))
                    last.then_inc(S["v"].sem, 1)
                for u in range(2):
                    n, B = 2 * i + u, banks[u]
                    pe.wait_ge(S["qk_out"].sem, S["qk_out"].at(n))
                    for t in range(NT):
                        bank, col = causal[t]
                        w = (t + 1) * R
                        for k in range(CT):
                            last = nc.tensor.matmul(B(bank + 2)[0:R, col:col + w], qT[:, u, k, t * R:(t + 1) * R],
                                                    kT[:, u, k, 0:w], start=(k == 0), stop=(k == CT - 1))
                            if k == 0:
                                nc.tensor.matmul(B(bank + 2)[0:R, col + t * R:col + w], c["identb"][0:R, 0:R],
                                                 c["mask_qk"][:], start=False, stop=False, skip_group_check=True)
                        last.then_inc(S["s"].sem, 1)
                for u in range(2):
                    n, B = 2 * i + u, banks[u]
                    pe.wait_ge(S["p"].sem, S["p"].at(n))
                    pe.wait_ge(S["v_out"].sem, S["v_out"].at(n))
                    for k in range(NT):
                        for t in range(k, NT):
                            out = B(0)[0:R, t * R:(t + 1) * R] if k == 0 else \
                                B(1)[0:R, ((k - 1) * 2 + t - k) * R:((k - 1) * 2 + t - k + 1) * R]
                            last = nc.tensor.transpose(out, prob[:, u, t, k * R:(k + 1) * R], c["ident"][0:R, 0:R])
                    last.then_inc(S["pT"].sem, 1)
                for u in range(2):
                    n, B = 2 * i + u, banks[u]
                    pe.wait_ge(S["pT_out"].sem, S["pT_out"].at(n))
                    for m in range(CT):
                        for k in range(NT):
                            moving = probT[:, u, 0, :] if k == 0 else \
                                probT[:, u, 1, (k - 1) * 2 * R:(k - 1) * 2 * R + (NT - k) * R]
                            last = nc.tensor.matmul(B(2 + m)[:, k * R:T], v[:, u, k, m * 128:(m + 1) * 128],
                                                    moving, start=(k == 0), stop=(k == NT - 1))
                    last.then_inc(S["a"].sem, 1)
                for u in range(2):
                    n, B = 2 * i + u, banks[u]
                    pe.wait_ge(S["a_out"].sem, S["a_out"].at(n))
                    for t in range(NT):
                        for k in range(CT):
                            last = nc.tensor.matmul(B(t // 2)[0:R, (t % 2) * D:(t % 2 + 1) * D],
                                                    aT[:, u, k, t * R:(t + 1) * R], wo[:, k, :],
                                                    start=(k == 0), stop=(k == CT - 1))
                    last.then_inc(S["y"].sem, 1)
                for u in range(2):
                    n, B = 2 * i + u, banks[u]
                    pe.wait_ge(S["x0"].sem, S["x0"].at(n))
                    transpose_tokens(nc, pe, c, xn[:, u], lambda k: B(2 + k)).then_inc(S["x0T"].sem, 1)


def quantise_weights(nc, c, ps, gate_dram, up_dram, down_dram, gateT, upT, downT):
    ctx = ExitStack()
    NBLK = FT * D // QBLOCK
    srcs = ((gate_dram, gateT, FT, CT), (up_dram, upT, FT, CT), (down_dram, downT, CT, FT))
    with ctx:
        w = ctx.enter_context(nc.sbuf_tensor("q_w", [128, 3, NBLK, QBLOCK], F32))
        step = ctx.enter_context(nc.sbuf_tensor("q_step", [128, 3, NBLK], F32))
        inv = ctx.enter_context(nc.sbuf_tensor("q_inv", [128, 3, NBLK], F32))
        loaded = [nc.alloc_semaphore(f"q_loaded{k}") for k in range(3)]
        chain = nc.alloc_semaphore("q_chain")
        done = nc.alloc_semaphore("q_done")
        turned = nc.alloc_semaphore("q_turned")
        out = nc.alloc_semaphore("q_out")
        block = ctx.enter_context(nc.Block())

        @block.sync
        def _(sp):
            for k, (dram, _, ot, _) in enumerate(srcs):
                sp.dma_start(w[:, k].rearrange("p b q -> p (b q)").rearrange("p (o i) -> p o i", o=ot),
                             dram.rearrange("(o p) i -> p o i", p=128)).then_inc(loaded[k], 16)

        @block.vector
        def _(dve):
            for k in range(3):
                def wide(a):
                    return a[:, k, :].unsqueeze(2).to_broadcast([128, NBLK, QBLOCK])

                dve.wait_ge(loaded[k], 16)
                nc.vector.tensor_reduce(step[:, k], w[:, k], AX.X, ALU.max, apply_absolute_value=True)\
                    .then_inc(chain, 1)
                dve.wait_ge(chain, 6 * k + 1)
                nc.vector.tensor_scalar(step[:, k], step[:, k], 1.0 / 7.0, 1e-12, ALU.mult, ALU.max)\
                    .then_inc(chain, 1)
                dve.wait_ge(chain, 6 * k + 2)
                nc.vector.reciprocal(inv[:, k], step[:, k]).then_inc(chain, 1)
                dve.wait_ge(chain, 6 * k + 3)
                nc.vector.tensor_tensor(w[:, k], w[:, k], wide(inv), ALU.mult).then_inc(chain, 1)
                dve.wait_ge(chain, 6 * k + 4)
                nc.vector.tensor_scalar(w[:, k], w[:, k], MAGIC, MAGIC, ALU.add, ALU.subtract).then_inc(chain, 1)
                dve.wait_ge(chain, 6 * k + 5)
                nc.vector.tensor_tensor(w[:, k], w[:, k], wide(step), ALU.mult).then_inc(chain, 1)
                dve.wait_ge(chain, 6 * k + 6)
                dve.sem_inc(done, 1)

        @block.tensor
        def _(pe):
            turn = 0
            for k, (_, dst, ot, it) in enumerate(srcs):
                pe.wait_ge(done, k + 1)
                src = w[:, k].rearrange("p b q -> p (b q)")
                for i in range(it):
                    for o0 in range(0, ot, 2):
                        if turn >= 8:
                            pe.wait_ge(out, turn - 7)
                        for o in (o0, o0 + 1):
                            last = nc.tensor.transpose(ps[:, turn % 8, (o - o0) * 128:(o - o0 + 1) * 128],
                                                       src[:, (o * it + i) * 128:(o * it + i + 1) * 128],
                                                       c["ident"][:])
                        last.then_inc(turned, 1)
                        turn += 1

        @block.scalar
        def _(act):
            turn = 0
            for k, (_, dst, ot, it) in enumerate(srcs):
                for i in range(it):
                    for o0 in range(0, ot, 2):
                        act.wait_ge(turned, turn + 1)
                        nc.scalar.copy(dst[:, i, o0 * 128:(o0 + 2) * 128], ps[:, turn % 8, 0:256])\
                            .then_inc(out, 1)
                        turn += 1


def set_scale(nc, name, amax, scale, inv):
    ctx = ExitStack()
    with ctx:
        k = amax.shape[1]
        every = ctx.enter_context(nc.sbuf_tensor(name + "_every", [128, k], F32))
        reduced = nc.alloc_semaphore(name + "_reduced")
        chain = nc.alloc_semaphore(name + "_chain")
        block = ctx.enter_context(nc.Block())

        @block.gpsimd
        def _(pool):
            nc.gpsimd.partition_all_reduce(every[:], amax, 128, bass.bass_isa.ReduceOp.max).then_inc(reduced, 1)

        @block.vector
        def _(dve):
            dve.wait_ge(reduced, 1)
            nc.vector.reduce_max(scale, every[:], AX.X).then_inc(chain, 1)
            dve.wait_ge(chain, 1)
            nc.vector.tensor_scalar(scale, scale, 1.0 / QMAX, 1e-12, ALU.mult, ALU.max).then_inc(chain, 1)
            dve.wait_ge(chain, 2)
            nc.vector.reciprocal(inv, scale).then_inc(chain, 1)
            dve.wait_ge(chain, 3)


def running_max(nc, dve, new, total, x, s_new, s_total, n):
    dve.wait_ge(s_total.sem, s_total.before(n))
    nc.vector.tensor_reduce(new, x, AX.X, ALU.max, apply_absolute_value=True).then_inc(s_new.sem, 1)
    dve.wait_ge(s_new.sem, s_new.at(n))
    nc.vector.tensor_tensor(total, total, new, ALU.max).then_inc(s_total.sem, 1)


def phase_b(nc, ps, NB, magic, x0_dram, gateT, upT, scale, inv, gate_dram, up_dram, amax_gate, amax_up):
    ctx = ExitStack()
    with ctx:
        def sb(name, shape, dt=F32):
            return ctx.enter_context(nc.sbuf_tensor("b_" + name, shape, dt))

        def sem(name):
            return nc.alloc_semaphore("b_" + name)

        x = sb("x", [128, 2, CT, T])
        xm = sb("xm", [128, 2, CT, T])
        gu = sb("gu", [128, 2, 2, FT, T])
        new = sb("new", [128, 2, 2])
        x_loaded = [sem(f"x_loaded{u}") for u in range(2)]
        gu_stored = [sem(f"gu_stored{u}") for u in range(2)]
        S = signals(ctx, nc, "b", xm=1, xq=1, mm=2 * FT, out=2 * FT, newg=1, maxg=1, newu=1, maxu=1)
        block = ctx.enter_context(nc.Block())

        @block.sync
        def _(sp):
            def load(n, u):
                sp.dma_start(x[:, u], x0_dram[n].rearrange("(c p) t -> p c t", p=128)).then_inc(x_loaded[u], 16)

            def pair(i, more):
                for u in range(2):
                    n = 2 * i + u
                    if more:
                        sp.wait_ge(S["mm"].sem, S["mm"].at(n))
                        load(n + 2, u)
                    for j, dram in enumerate((gate_dram, up_dram)):
                        sp.wait_ge(S["out"].sem, S["out"].at(n, (j + 1) * FT))
                        sp.dma_start(dram[n], gu[:, u, j].rearrange("p f t -> p (f t)")).then_inc(gu_stored[u], 16)

            for u in range(2):
                load(u, u)
            with sp.Fori(0, NB // 2 - 1) as i:
                pair(i, True)
            pair(NB // 2 - 1, False)
            for u in range(2):
                sp.wait_ge(gu_stored[u], 32 * (NB // 2))

        @block.scalar
        def _(act):
            for k in ("xm", "out"):
                S[k].give(act)
            with act.Fori(0, NB // 2) as i:
                for u in range(2):
                    n = 2 * i + u
                    act.wait_ge(x_loaded[u], 16 * i + 16)
                    act.wait_ge(S["xq"].sem, S["xq"].before(n))
                    nc.scalar.activation(xm[:, u], x[:, u], ACT.Identity, scale=inv, bias=magic)\
                        .then_inc(S["xm"].sem, 1)
                for u in range(2):
                    n = 2 * i + u
                    act.wait_ge(gu_stored[u], 32 * i)
                    act.wait_ge(S["maxu"].sem, S["maxu"].before(n))
                    for m in range(2 * FT):
                        act.wait_ge(S["mm"].sem, S["mm"].at(n, m + 1))
                        nc.scalar.copy(gu[:, u, m // FT, m % FT, :], ps[:, 4 * u + m % 4, 0:T])\
                            .then_inc(S["out"].sem, 1)

        @block.vector
        def _(dve):
            for k in ("xq", "newg", "maxg", "newu", "maxu"):
                S[k].give(dve)
            with dve.Fori(0, NB // 2) as i:
                for u in range(2):
                    n = 2 * i + u
                    dve.wait_ge(S["xm"].sem, S["xm"].at(n))
                    dve.wait_ge(S["mm"].sem, S["mm"].before(n))
                    nc.vector.tensor_scalar(x[:, u], xm[:, u], MAGIC, scale, ALU.subtract, ALU.mult)\
                        .then_inc(S["xq"].sem, 1)
                for u in range(2):
                    n = 2 * i + u
                    for j, (k, amax) in enumerate((("g", amax_gate), ("u", amax_up))):
                        dve.wait_ge(S["out"].sem, S["out"].at(n, (j + 1) * FT))
                        running_max(nc, dve, new[:, u, j:j + 1], amax[:, u:u + 1],
                                    gu[:, u, j].rearrange("p f t -> p (f t)"), S["new" + k], S["max" + k], n)

        @block.tensor
        def _(pe):
            S["mm"].give(pe)
            with pe.Fori(0, NB // 2) as i:
                for u in range(2):
                    n = 2 * i + u
                    pe.wait_ge(S["xq"].sem, S["xq"].at(n))
                    for m in range(2 * FT):
                        if m < 4:
                            pe.wait_ge(S["out"].sem, S["out"].before(n))
                        else:
                            pe.wait_ge(S["out"].sem, S["out"].at(n, m - 3))
                        w = (gateT, upT)[m // FT]
                        for k in range(CT):
                            last = nc.tensor.matmul(ps[:, 4 * u + m % 4, 0:T],
                                                    w[:, k, (m % FT) * 128:(m % FT + 1) * 128],
                                                    x[:, u, k, :], start=(k == 0), stop=(k == CT - 1))
                        last.then_inc(S["mm"].sem, 1)


def phase_c(nc, NB, magic, gate_dram, scale, inv, g2_dram, amax_g2):
    ctx = ExitStack()
    N = FT * T
    with ctx:
        def sb(name):
            return ctx.enter_context(nc.sbuf_tensor("c_" + name, [128, 2, N], F32))

        def sem(name):
            return nc.alloc_semaphore("c_" + name)

        g, gm, gq, sg, sm, g2 = (sb(n) for n in ("g", "gm", "gq", "sg", "sm", "g2"))
        new = ctx.enter_context(nc.sbuf_tensor("c_new", [128, 2], F32))
        loaded = [sem(f"loaded{u}") for u in range(2)]
        stored = [sem(f"stored{u}") for u in range(2)]
        S = signals(ctx, nc, "c", gm=1, gq=1, sg=1, sm=1, sr=1, g2=1, new=1, max=1)
        block = ctx.enter_context(nc.Block())

        @block.sync
        def _(sp):
            def load(n, u):
                sp.dma_start(g[:, u], gate_dram[n]).then_inc(loaded[u], 16)

            def pair(i, more):
                for u in range(2):
                    n = 2 * i + u
                    if more:
                        sp.wait_ge(S["gm"].sem, S["gm"].at(n))
                        load(n + 2, u)
                for u in range(2):
                    n = 2 * i + u
                    sp.wait_ge(S["g2"].sem, S["g2"].at(n))
                    sp.dma_start(g2_dram[n], g2[:, u]).then_inc(stored[u], 16)

            for u in range(2):
                load(u, u)
            with sp.Fori(0, NB // 2 - 1) as i:
                pair(i, True)
            pair(NB // 2 - 1, False)
            for u in range(2):
                sp.wait_ge(stored[u], 16 * (NB // 2))

        @block.scalar
        def _(act):
            for k in ("gm", "sg"):
                S[k].give(act)
            with act.Fori(0, NB // 2) as i:
                for u in range(2):
                    n = 2 * i + u
                    act.wait_ge(loaded[u], 16 * i + 16)
                    act.wait_ge(S["gq"].sem, S["gq"].before(n))
                    nc.scalar.activation(gm[:, u], g[:, u], ACT.Identity, scale=inv, bias=magic)\
                        .then_inc(S["gm"].sem, 1)
                for u in range(2):
                    n = 2 * i + u
                    act.wait_ge(S["gq"].sem, S["gq"].at(n))
                    act.wait_ge(S["sm"].sem, S["sm"].before(n))
                    nc.scalar.activation(sg[:, u], gq[:, u], ACT.Sigmoid).then_inc(S["sg"].sem, 1)

        @block.vector
        def _(dve):
            for k in ("gq", "sm", "sr", "g2", "new", "max"):
                S[k].give(dve)
            with dve.Fori(0, NB // 2) as i:
                for u in range(2):
                    n = 2 * i + u
                    dve.wait_ge(S["gm"].sem, S["gm"].at(n))
                    dve.wait_ge(S["g2"].sem, S["g2"].before(n))
                    nc.vector.tensor_scalar(gq[:, u], gm[:, u], MAGIC, scale, ALU.subtract, ALU.mult)\
                        .then_inc(S["gq"].sem, 1)
                for u in range(2):
                    n = 2 * i + u
                    dve.wait_ge(S["sg"].sem, S["sg"].at(n))
                    dve.wait_ge(S["g2"].sem, S["g2"].before(n))
                    nc.vector.tensor_scalar(sm[:, u], sg[:, u], 65536.0, MAGIC, ALU.mult, ALU.add)\
                        .then_inc(S["sm"].sem, 1)
                    dve.wait_ge(S["sm"].sem, S["sm"].at(n))
                    nc.vector.tensor_scalar(sm[:, u], sm[:, u], MAGIC + 65535.0, MAGIC, ALU.min, ALU.subtract)\
                        .then_inc(S["sr"].sem, 1)
                for u in range(2):
                    n = 2 * i + u
                    dve.wait_ge(S["sr"].sem, S["sr"].at(n))
                    dve.wait_ge(stored[u], 16 * i)
                    dve.wait_ge(S["new"].sem, S["new"].before(n))
                    nc.vector.scalar_tensor_tensor(out=g2[:, u], in0=sm[:, u], scalar=1.0 / 65536.0,
                                                   in1=gq[:, u], op0=ALU.mult, op1=ALU.mult)\
                        .then_inc(S["g2"].sem, 1)
                for u in range(2):
                    n = 2 * i + u
                    dve.wait_ge(S["g2"].sem, S["g2"].at(n))
                    running_max(nc, dve, new[:, u:u + 1], amax_g2[:, u:u + 1], g2[:, u], S["new"], S["max"], n)


def phase_d(nc, NB, magic, g2_dram, up_dram, scale_g, inv_g, scale_u, inv_u, o_dram, amax_o):
    ctx = ExitStack()
    N = FT * T
    with ctx:
        def sb(name):
            return ctx.enter_context(nc.sbuf_tensor("d_" + name, [128, 2, N], F32))

        def sem(name):
            return nc.alloc_semaphore("d_" + name)

        src = {k: sb(k) for k in "gu"}
        rounded = {k: sb(k + "m") for k in "gu"}
        quant = {k: sb(k + "q") for k in "gu"}
        o = sb("o")
        new = ctx.enter_context(nc.sbuf_tensor("d_new", [128, 2], F32))
        dram = {"g": g2_dram, "u": up_dram}
        scale, inv = {"g": scale_g, "u": scale_u}, {"g": inv_g, "u": inv_u}
        loaded = {k: [sem(f"loaded_{k}{u}") for u in range(2)] for k in "gu"}
        stored = [sem(f"stored{u}") for u in range(2)]
        S = signals(ctx, nc, "d", gm=1, um=1, gq=1, uq=1, o=1, new=1, max=1)
        block = ctx.enter_context(nc.Block())

        @block.sync
        def _(sp):
            def load(k, n, u):
                sp.dma_start(src[k][:, u], dram[k][n]).then_inc(loaded[k][u], 16)

            def pair(i, more):
                for u in range(2):
                    n = 2 * i + u
                    for k in "gu":
                        if more:
                            sp.wait_ge(S[k + "m"].sem, S[k + "m"].at(n))
                            load(k, n + 2, u)
                for u in range(2):
                    n = 2 * i + u
                    sp.wait_ge(S["o"].sem, S["o"].at(n))
                    sp.dma_start(o_dram[n], o[:, u]).then_inc(stored[u], 16)

            for u in range(2):
                for k in "gu":
                    load(k, u, u)
            with sp.Fori(0, NB // 2 - 1) as i:
                pair(i, True)
            pair(NB // 2 - 1, False)
            for u in range(2):
                sp.wait_ge(stored[u], 16 * (NB // 2))

        @block.scalar
        def _(act):
            for k in ("gm", "um"):
                S[k].give(act)
            with act.Fori(0, NB // 2) as i:
                for u in range(2):
                    n = 2 * i + u
                    for k in "gu":
                        act.wait_ge(loaded[k][u], 16 * i + 16)
                        act.wait_ge(S[k + "q"].sem, S[k + "q"].before(n))
                        nc.scalar.activation(rounded[k][:, u], src[k][:, u], ACT.Identity, scale=inv[k],
                                             bias=magic).then_inc(S[k + "m"].sem, 1)

        @block.vector
        def _(dve):
            for k in ("gq", "uq", "o", "new", "max"):
                S[k].give(dve)
            with dve.Fori(0, NB // 2) as i:
                for u in range(2):
                    n = 2 * i + u
                    for k in "gu":
                        dve.wait_ge(S[k + "m"].sem, S[k + "m"].at(n))
                        dve.wait_ge(S["o"].sem, S["o"].before(n))
                        nc.vector.tensor_scalar(quant[k][:, u], rounded[k][:, u], MAGIC, scale[k],
                                                ALU.subtract, ALU.mult).then_inc(S[k + "q"].sem, 1)
                for u in range(2):
                    n = 2 * i + u
                    dve.wait_ge(S["uq"].sem, S["uq"].at(n))
                    dve.wait_ge(S["gq"].sem, S["gq"].at(n))
                    dve.wait_ge(stored[u], 16 * i)
                    dve.wait_ge(S["new"].sem, S["new"].before(n))
                    nc.vector.tensor_tensor(o[:, u], quant["g"][:, u], quant["u"][:, u], ALU.mult)\
                        .then_inc(S["o"].sem, 1)
                for u in range(2):
                    n = 2 * i + u
                    dve.wait_ge(S["o"].sem, S["o"].at(n))
                    running_max(nc, dve, new[:, u:u + 1], amax_o[:, u:u + 1], o[:, u], S["new"], S["max"], n)


PARTS = 3
Q_PART = (0, 0, 0, 1, 1, 2)
K_PART = (0, 1, 2, 0, 1, 0)
SLOTS = len(Q_PART)
SDPA, HYP, COS = range(3)
KINDS = [SDPA] * 6 + [HYP] * 4 + [COS] * 6
NSCALED = 10
HD1 = HD + 1
VW = 2 * HD
RP = 128


def phase_f1(nc, c, ps, NB, magic, o_dram, h1_dram, downT, scale, inv, wqkv_dram, curv_dram,
             h2_dram, parts_dram, v_dram):
    ctx = ExitStack()
    with ctx:
        def sb(name, shape, dt=F32):
            return ctx.enter_context(nc.sbuf_tensor("f_" + name, shape, dt))

        def sem(name):
            return nc.alloc_semaphore("f_" + name)

        GH = 6
        GROUPS = [(0, 6), (6, 6), (12, 4)]
        wqkv = sb("wqkv", [128, CT, 3 * D])
        icurv = sb("icurv", [R, 4])
        power = sb("power", [R, NT * 2, NSCALED])
        o = sb("o", [128, 2, FT, T])
        om = sb("om", [128, 2, FT, T])
        h = sb("h", [R, 2, NT, D])
        stats = sb("stats", [R, 2, NT, 6])
        mv = sb("mv", [R, 2, NT, 2])
        var_eps = sb("var_eps", [R, 2, NT])
        rstd = sb("rstd", [R, 2, NT])
        xn = sb("xn", [R, 2, NT, D])
        xT = sb("xT", [128, 2, CT, T])
        rc = sb("rc", [R, 2, 2 * H, HD])
        rs = sb("rs", [R, 2, 2 * H, HD])
        qk = sb("qk", [R, 2, NT, 2 * H, HD1])
        sq = sb("sq", [R, 2, 2, NSCALED, HD])
        ss = sb("ss", [R, 2, NT * 2, NSCALED])
        norm = sb("norm", [R, 2, NT * 2, NSCALED])
        parts = sb("parts", [GH * HD1, 2, 6, PARTS, T], BF16)
        rest = sb("rest", [GH * HD1, 2, 2, T])
        vp = sb("vp", [R, 2, NT, H, VW])
        w_loaded = sem("w_loaded")
        powers = sem("powers")
        filled = sem("filled")
        o_loaded = [sem(f"o_loaded{u}") for u in range(2)]
        h_loaded = [sem(f"h_loaded{u}") for u in range(2)]
        h_stored = [sem(f"h_stored{u}") for u in range(2)]
        p_stored = [sem(f"p_stored{u}") for u in range(2)]
        v_stored = [sem(f"v_stored{u}") for u in range(2)]
        S = signals(ctx, nc, "f", om=1, oq=1, y=1, h2=1, bn=NT + 1, mv=1, eps=1, rstd=1, xn=NT, xT=1, xT_out=1,
                    qk=NT, v=2, v_out=2, rc=2 * NT, rot=NT, sq=NT, ss=NT, cap=2, norm=1, tq=2, scaled=NT,
                    turn=6, hi=6, rest=6, mid=6, lo=6)
        banks = [lambda k, u=u: ps[:, 4 * u + k, :] for u in range(2)]
        block = ctx.enter_context(nc.Block())

        @block.sync
        def _(sp):
            def load_o(n, u):
                sp.dma_start(o[:, u].rearrange("p f t -> p (f t)"), o_dram[n]).then_inc(o_loaded[u], 16)

            def load_h(n, u):
                sp.dma_start(h[:, u], h1_dram[n].rearrange("(t p) d -> p t d", p=R)).then_inc(h_loaded[u], 16)

            def pair(i, more):
                for u in range(2):
                    n = 2 * i + u
                    if more:
                        sp.wait_ge(S["y"].sem, S["y"].at(n))
                        load_o(n + 2, u)
                for u in range(2):
                    n = 2 * i + u
                    sp.wait_ge(S["h2"].sem, S["h2"].at(n))
                    sp.dma_start(h2_dram[n].rearrange("(t p) d -> p t d", p=R), h[:, u]).then_inc(h_stored[u], 16)
                for u in range(2):
                    n = 2 * i + u
                    sp.wait_ge(S["v_out"].sem, S["v_out"].at(n))
                    sp.dma_start(v_dram[n], vp[:, u].rearrange("p t h w -> p (t h w)")).then_inc(v_stored[u], 16)
                    if more:
                        sp.wait_ge(S["xn"].sem, S["xn"].at(n))
                        sp.wait_ge(h_stored[u], 16 * i + 16)
                        load_h(n + 2, u)
                for u in range(2):
                    n = 2 * i + u
                    for j in range(6):
                        h0, nh = GROUPS[j % 3]
                        sp.wait_ge(S["lo"].sem, S["lo"].at(n, j + 1))
                        sp.dma_start(parts_dram[n, j // 3, h0 * HD1:(h0 + nh) * HD1].rearrange("r k t -> r (k t)"),
                                     parts[0:nh * HD1, u, j].rearrange("p k t -> p (k t)")).then_inc(p_stored[u], 16)

            sp.dma_start(wqkv[:], wqkv_dram.rearrange("(k p) n -> p k n", p=128)).then_inc(w_loaded, 16)
            sp.dma_start(icurv[:], curv_dram.rearrange("(a h) -> a h", a=1).broadcast_to([R, 4])).then_inc(w_loaded, 16)
            for u in range(2):
                load_o(u, u)
                load_h(u, u)
            with sp.Fori(0, NB // 2 - 1) as i:
                pair(i, True)
            pair(NB // 2 - 1, False)
            for u in range(2):
                sp.wait_ge(h_stored[u], 16 * (NB // 2))
                sp.wait_ge(p_stored[u], 96 * (NB // 2))
                sp.wait_ge(v_stored[u], 16 * (NB // 2))

        @block.gpsimd
        def _(pool):
            for k in ("eps", "rstd", "cap", "norm"):
                S[k].give(pool)
            nc.gpsimd.memset(power[:, :, 0:4], 0.5)
            nc.gpsimd.memset(power[:, :, 4:NSCALED], -0.5).then_inc(powers, 1)
            pool.wait_ge(powers, 1)
            pool.wait_ge(filled, 1)
            with pool.Fori(0, NB // 2) as i:
                for u in range(2):
                    ln_rstd(nc, pool, c, mv[:, u], var_eps[:, u], rstd[:, u],
                            S["mv"], S["eps"], S["rstd"], 2 * i + u)
                for u in range(2):
                    n = 2 * i + u
                    pool.wait_ge(S["ss"].sem, S["ss"].at(n))
                    nc.gpsimd.tensor_tensor(ss[:, u, :, 0:4], ss[:, u, :, 0:4],
                                            icurv[:].unsqueeze(1).to_broadcast([R, NT * 2, 4]), ALU.add)\
                        .then_inc(S["cap"].sem, 1)
                    nc.gpsimd.tensor_scalar(ss[:, u, :, 4:NSCALED], ss[:, u, :, 4:NSCALED], 1e-24, None, ALU.max)\
                        .then_inc(S["cap"].sem, 1)
                    pool.wait_ge(S["cap"].sem, S["cap"].at(n))
                    pool.wait_ge(S["scaled"].sem, S["scaled"].before(n))
                    nc.gpsimd.tensor_tensor(norm[:, u], ss[:, u], power[:], ALU.pow).then_inc(S["norm"].sem, 1)

        @block.scalar
        def _(act):
            for k in ("om", "xT_out", "v_out", "sq", "hi", "mid"):
                S[k].give(act)
            with act.Fori(0, NB // 2) as i:
                for u in range(2):
                    n = 2 * i + u
                    act.wait_ge(o_loaded[u], 16 * i + 16)
                    act.wait_ge(S["oq"].sem, S["oq"].before(n))
                    nc.scalar.activation(om[:, u], o[:, u], ACT.Identity, scale=inv, bias=magic)\
                        .then_inc(S["om"].sem, 1)
                for u in range(2):
                    n = 2 * i + u
                    act.wait_ge(S["xT"].sem, S["xT"].at(n))
                    act.wait_ge(S["v"].sem, S["v"].before(n))
                    nc.scalar.copy(xT[:, u], ps[:, 4 * u + 2:4 * u + 4, 0:T]).then_inc(S["xT_out"].sem, 1)
                for u in range(2):
                    n, B = 2 * i + u, banks[u]
                    act.wait_ge(v_stored[u], 16 * i)
                    act.wait_ge(S["v"].sem, S["v"].at(n, 1))
                    nc.scalar.copy(vp[:, u, 0:2, :, 0:HD], B(3)[0:R, :].rearrange("p (t h w) -> p t h w", t=2, w=HD))\
                        .then_inc(S["v_out"].sem, 1)
                    act.wait_ge(S["v"].sem, S["v"].at(n, 2))
                    nc.scalar.copy(vp[:, u, 2, :, 0:HD], B(0)[0:R, 0:D].rearrange("p (h w) -> p h w", w=HD))\
                        .then_inc(S["v_out"].sem, 1)
                    for t in range(NT):
                        act.wait_ge(S["rot"].sem, S["rot"].at(n, t + 1))
                        if t:
                            act.wait_ge(S["ss"].sem, S["ss"].at(n, t))
                        else:
                            act.wait_ge(S["ss"].sem, S["ss"].before(n))
                        heads = qk[:, u, t].rearrange("p (a h) w -> p a h w", a=2)[:, :, 6:16, 0:HD]
                        nc.scalar.activation(sq[:, u], heads, ACT.Square).then_inc(S["sq"].sem, 1)
                for u in range(2):
                    n, B = 2 * i + u, banks[u]
                    act.wait_ge(p_stored[u], 96 * i)
                    for j in range(6):
                        rows = GROUPS[j % 3][1] * HD1
                        act.wait_ge(S["turn"].sem, S["turn"].at(n, j + 1))
                        nc.scalar.copy(parts[0:rows, u, j, 0, :], B(j % 4)[0:rows, 0:T]).then_inc(S["hi"].sem, 1)
                        act.wait_ge(S["rest"].sem, S["rest"].at(n, j + 1))
                        nc.scalar.copy(parts[0:rows, u, j, 1, :], rest[0:rows, u, j % 2]).then_inc(S["mid"].sem, 1)

        @block.vector
        def _(dve):
            for k in ("oq", "h2", "bn", "mv", "xn", "rc", "rot", "ss", "tq", "scaled", "rest", "lo"):
                S[k].give(dve)
            dve.wait_ge(w_loaded, 32)
            nc.vector.reciprocal(icurv[:], icurv[:]).then_inc(filled, 1)
            nc.vector.tensor_scalar(wqkv[:, :, 0:6 * HD], wqkv[:, :, 0:6 * HD], float(HD) ** -0.5, None, ALU.mult)\
                .then_inc(filled, 1)
            nc.vector.memset(vp[:], 1.0)
            nc.vector.memset(qk[:], 0.0).then_inc(filled, 1)
            dve.wait_ge(filled, 3)
            with dve.Fori(0, NB // 2) as i:
                for u in range(2):
                    n = 2 * i + u
                    dve.wait_ge(S["om"].sem, S["om"].at(n))
                    nc.vector.tensor_scalar(o[:, u], om[:, u], MAGIC, scale, ALU.subtract, ALU.mult)\
                        .then_inc(S["oq"].sem, 1)
                for u in range(2):
                    n, B = 2 * i + u, banks[u]
                    dve.wait_ge(S["y"].sem, S["y"].at(n))
                    dve.wait_ge(h_loaded[u], 16 * i + 16)
                    nc.vector.tensor_tensor(h[:, u, 0:2, :], B(0)[0:R, :].rearrange("p (t d) -> p t d", t=2),
                                            h[:, u, 0:2, :], ALU.add)
                    nc.vector.tensor_tensor(h[:, u, 2, :], B(1)[0:R, 0:D], h[:, u, 2, :], ALU.add)\
                        .then_inc(S["h2"].sem, 1)
                for u in range(2):
                    n = 2 * i + u
                    dve.wait_ge(S["h2"].sem, S["h2"].at(n))
                    ln_stats(nc, dve, h[:, u], stats[:, u], mv[:, u], (S["bn"].sem, S["bn"].at(n)), S["mv"])
                for u in range(2):
                    n = 2 * i + u
                    dve.wait_ge(S["rstd"].sem, S["rstd"].at(n))
                    dve.wait_ge(S["xT"].sem, S["xT"].before(n))
                    ln_apply(nc, xn[:, u], h[:, u], mv[:, u], rstd[:, u], S["xn"])
                for u in range(2):
                    n, B = 2 * i + u, banks[u]
                    dve.wait_ge(S["turn"].sem, S["turn"].before(n))
                    for t in range(NT):
                        x = B(t)[0:R, :].rearrange("p (h w) -> p h w", w=HD)
                        cos = c["cos"][:, t].unsqueeze(1).to_broadcast([R, 2 * H, HD])
                        sin = c["sin"][:, t].unsqueeze(1)
                        half = HD // 2
                        dve.wait_ge(S["qk"].sem, S["qk"].at(n, t + 1))
                        if t:
                            dve.wait_ge(S["rot"].sem, S["rot"].at(n, t))
                        nc.vector.tensor_tensor(rc[:, u], x, cos, ALU.mult)
                        nc.vector.tensor_tensor(rs[:, u, :, 0:half], x[:, :, half:HD],
                                                sin[:, :, 0:half].to_broadcast([R, 2 * H, half]), ALU.mult)\
                            .then_inc(S["rc"].sem, 1)
                        nc.vector.tensor_tensor(rs[:, u, :, half:HD], x[:, :, 0:half],
                                                sin[:, :, half:HD].to_broadcast([R, 2 * H, half]), ALU.mult)\
                            .then_inc(S["rc"].sem, 1)
                        dve.wait_ge(S["rc"].sem, S["rc"].at(n, 2 * t + 2))
                        nc.vector.tensor_tensor(qk[:, u, t, :, 0:HD], rc[:, u], rs[:, u], ALU.add)\
                            .then_inc(S["rot"].sem, 1)
                    for t in range(NT):
                        dve.wait_ge(S["sq"].sem, S["sq"].at(n, t + 1))
                        if t == 0:
                            dve.wait_ge(S["norm"].sem, S["norm"].before(n))
                        nc.vector.reduce_sum(ss[:, u, 2 * t:2 * t + 2, :], sq[:, u], AX.X).then_inc(S["ss"].sem, 1)
                for u in range(2):
                    n = 2 * i + u
                    dve.wait_ge(S["norm"].sem, S["norm"].at(n))
                    split = norm[:, u].rearrange("p (t a) h -> p t a h", a=2)
                    nc.vector.tensor_copy(qk[:, u, :, 6:10, HD], split[:, :, 0, 0:4]).then_inc(S["tq"].sem, 1)
                    nc.vector.tensor_scalar(qk[:, u, :, H + 6:H + 10, HD], split[:, :, 1, 0:4], -1.0, None, ALU.mult)\
                        .then_inc(S["tq"].sem, 1)
                    for t in range(NT):
                        heads = qk[:, u, t].rearrange("p (a h) w -> p a h w", a=2)[:, :, 10:16, 0:HD]
                        nc.vector.tensor_tensor(heads, heads, split[:, t, :, 4:NSCALED].unsqueeze(3)
                                                .to_broadcast([R, 2, 6, HD]), ALU.mult).then_inc(S["scaled"].sem, 1)
                for u in range(2):
                    n, B = 2 * i + u, banks[u]
                    for j in range(6):
                        rows = GROUPS[j % 3][1] * HD1
                        dve.wait_ge(S["hi"].sem, S["hi"].at(n, j + 1))
                        if j >= 2:
                            dve.wait_ge(S["lo"].sem, S["lo"].at(n, j - 1))
                        nc.vector.tensor_tensor(rest[0:rows, u, j % 2], B(j % 4)[0:rows, 0:T],
                                                parts[0:rows, u, j, 0, :], ALU.subtract).then_inc(S["rest"].sem, 1)
                        dve.wait_ge(S["mid"].sem, S["mid"].at(n, j + 1))
                        nc.vector.tensor_tensor(parts[0:rows, u, j, 2, :], rest[0:rows, u, j % 2],
                                                parts[0:rows, u, j, 1, :], ALU.subtract).then_inc(S["lo"].sem, 1)

        @block.tensor
        def _(pe):
            for k in ("y", "xT", "qk", "v", "turn"):
                S[k].give(pe)
            pe.wait_ge(filled, 2)
            with pe.Fori(0, NB // 2) as i:
                for u in range(2):
                    n, B = 2 * i + u, banks[u]
                    pe.wait_ge(S["oq"].sem, S["oq"].at(n))
                    pe.wait_ge(S["lo"].sem, S["lo"].before(n))
                    for t in range(NT):
                        for k in range(FT):
                            last = nc.tensor.matmul(B(t // 2)[0:R, (t % 2) * D:(t % 2 + 1) * D],
                                                    o[:, u, k, t * R:(t + 1) * R], downT[:, k, :],
                                                    start=(k == 0), stop=(k == FT - 1))
                    last.then_inc(S["y"].sem, 1)
                for u in range(2):
                    n, B = 2 * i + u, banks[u]
                    pe.wait_ge(S["xn"].sem, S["xn"].at(n))
                    transpose_tokens(nc, pe, c, xn[:, u], lambda k: B(2 + k)).then_inc(S["xT"].sem, 1)
                for u in range(2):
                    n, B = 2 * i + u, banks[u]
                    pe.wait_ge(S["xT_out"].sem, S["xT_out"].at(n))
                    pe.wait_ge(S["h2"].sem, S["h2"].at(n))
                    for t in range(NT):
                        for k in range(CT):
                            last = nc.tensor.matmul(B(t)[0:R, :], xT[:, u, k, t * R:(t + 1) * R],
                                                    wqkv[:, k, 0:2 * D], start=(k == 0), stop=(k == CT - 1))
                        last.then_inc(S["qk"].sem, 1)
                    for t in range(NT):
                        if t == 2:
                            last.then_inc(S["v"].sem, 1)
                            pe.wait_ge(S["rot"].sem, S["rot"].at(n, 1))
                        for k in range(CT):
                            last = nc.tensor.matmul(B(0 if t == 2 else 3)[0:R, (t % 2) * D:(t % 2 + 1) * D],
                                                    xT[:, u, k, t * R:(t + 1) * R], wqkv[:, k, 2 * D:3 * D],
                                                    start=(k == 0), stop=(k == CT - 1))
                    last.then_inc(S["v"].sem, 1)
                for u in range(2):
                    n, B = 2 * i + u, banks[u]
                    pe.wait_ge(S["v_out"].sem, S["v_out"].at(n))
                    pe.wait_ge(S["tq"].sem, S["tq"].at(n))
                    pe.wait_ge(S["scaled"].sem, S["scaled"].at(n))
                    for j in range(6):
                        h0, nh = GROUPS[j % 3]
                        if j >= 4:
                            pe.wait_ge(S["rest"].sem, S["rest"].at(n, j - 3))
                        x = qk[:, u].rearrange("p t h w -> p t (h w)")
                        first = (H * (j // 3) + h0) * HD1
                        for t in range(NT):
                            last = nc.tensor.transpose(B(j % 4)[0:nh * HD1, t * R:(t + 1) * R],
                                                       x[:, t, first:first + nh * HD1], c["ident"][0:R, 0:R])
                        last.then_inc(S["turn"].sem, 1)


def attention_core(nc, c, ps, NB, name, kinds, causal, hd, parts_dram, v_dram, ctx_dram, curv_dram=None):
    ctx = ExitStack()
    with ctx:
        def sb(n_, shape, dt=F32):
            return ctx.enter_context(nc.sbuf_tensor(f"{name}_{n_}", shape, dt))

        def sem(n_):
            return nc.alloc_semaphore(f"{name}_{n_}")

        rows, SHIFT = SLOTS * hd, PARTS
        full = 128
        if causal:
            UNITS = 2
            QTILE = {2: (0, 0), 1: (1, 0), 0: (1, 2 * R)}
            KTILE = {0: (0, 0), 1: (1, 0), 2: (1, 2 * R)}
            ORDER = [12, 13, 14, 15, 10, 11, 8, 9, 4, 5, 6, 7, 0, 1, 2, 3]
        else:
            UNITS = 3
            QTILE = {t: (t, 0) for t in range(NT)}
            KTILE = QTILE
            ORDER = list(range(H))
        HYPS = [h for h in range(H) if kinds[h] == HYP]
        hyp_slot = [[h for h in ORDER if h in HYPS].index(h) for h in HYPS]
        SDPAS = [h for h in range(H) if kinds[h] == SDPA]
        NHYP = len(HYPS)
        MAXED = NHYP + len(SDPAS)

        def place(step):
            return (("pre", step + H) if step < 0 else ("main", step) if step < H else ("post", step - H))

        first = -11 if NHYP else -13
        look_order = [h for pair in zip(HYPS, SDPAS) for h in pair] + SDPAS[NHYP:]
        look_step = {h: first + x for x, h in enumerate(look_order)}
        look = {place(step): h for h, step in look_step.items()}
        if NHYP:
            ROOT, SUM, SCORE = 1, 2, 4
            NEGATE = place(look_step[HYPS[-1]] + SCORE + 1)
            shifts = [(look_step[HYPS[-1]] + SCORE + 2, 0, MAXED)]
        else:
            shifts = [(-7, 0, 6), (-3, 6, 10), (5, 10, H)]
        NSH = len(shifts)
        product = {place(4 * g + 4 + kt): (g, kt) for g in range(4) for kt in range(NT)}
        back_step = {g: 4 * g + 8 for g in range(4)}
        back = {place(step): g for g, step in back_step.items()}
        uses = {}
        for h in look_order:
            for which in (("max", "raw") if kinds[h] == HYP else ("max",)):
                for b in range(UNITS):
                    uses[(h, which, b)] = len(uses)
        RING1, RING2 = (0, 1, 2), (3, 4, 5)

        def shifts_at(when, p, later=0):
            return [(x, lo, hi) for x, (step, lo, hi) in enumerate(shifts) if place(step + later) == (when, p)]

        q = sb("q", [full, 2, H, T], BF16)
        k = sb("k", [full, 2, H, T], BF16)
        vp = sb("vp", [RP, 2, NT, H, VW])
        neg = sb("neg", [R, 2, NT, MAXED])
        shift = sb("shift", [H, 2, PARTS, T], BF16)
        rest = sb("rest", [H, 2, T])
        probT = sb("probT", [RP, 8, UNITS, T])
        oT = sb("oT", [128, 2, T])
        rec = sb("rec", [R, 2, NT, 4])
        out = sb("out", [R, 2, NT, H, HD])
        ones_set, zeros_set = sem("ones_set"), sem("zeros_set")
        qk_loaded = [sem(f"qk_loaded{u}") for u in range(2)]
        v_loaded = [sem(f"v_loaded{u}") for u in range(2)]
        stored = [sem(f"stored{u}") for u in range(2)]
        laid = [sem(f"laid{u}") for u in range(2)]
        passed, sp_passed = sem("passed"), sem("sp_passed")
        sigs = dict(look=len(uses), looked=len(uses), turn=NSH, hi=NSH, rest=NSH, mid=NSH, lo=NSH,
                    s=H * UNITS, exp=H * UNITS, pv=4, oT=4, back=4, rec=4, out=4)
        if NHYP:
            W = 2 * T + NT
            negc = sb("negc", [R, 4])
            root_ic = sb("root_ic", [R, 4])
            one = sb("one", [R, 1])
            eps6 = sb("eps6", [R, 1])
            only_shift = sb("only_shift", [full, R], BF16)
            top = sb("top", [R, 2, NHYP, NT])
            hw = sb("hw", [R, 2, NHYP, W])
            hu = sb("hu", [R, NHYP, W])
            curv_loaded, ready = sem("curv_loaded"), sem("ready")
            sigs |= dict(top=NHYP * NT, w=NHYP, wc=NHYP, hu=NHYP, hl=NHYP, root=NHYP, z=NHYP, l1=NHYP, l2=NHYP,
                         score=NHYP, hneg=1, shifted=NHYP * UNITS)
        S = signals(ctx, nc, name, **sigs)
        block = ctx.enter_context(nc.Block())

        def is_last(u, i):
            return isinstance(i, int) and i == NB // 2 - 1 and u == 1

        def program(eng, step):
            def body(i, b, posts=True, mains=True, pres=True):
                for p in range(H):
                    for when, k, there in (("post", b - 1, posts), ("main", b, mains), ("pre", b + 1, pres)):
                        if there:
                            step(when, p, (i, k), k % 2, i + k // 2)

            body(0, -1, posts=False, mains=False)
            body(0, 0, posts=False)
            body(0, 1)
            with eng.Fori(1, NB // 2 - 1) as i:
                body(i, 0)
                body(i, 1)
            body(NB // 2 - 1, 0)
            body(NB // 2 - 1, 1, pres=False)
            body(NB // 2 - 1, 2, mains=False, pres=False)

        @block.sync
        def _(sp):
            def load_qk(n, u):
                for x, which, dst in ((0, Q_PART, q), (1, K_PART, k)):
                    rowsd = parts_dram[n, x].rearrange("(h d) k t -> d h k t", d=hd)
                    for s, part in enumerate(which):
                        sp.dma_start(dst[s * hd:(s + 1) * hd, u], rowsd[:, :, part, :]).then_inc(qk_loaded[u], 16)

            def load_v(n, u):
                sp.dma_start(vp[0:R, u].rearrange("p t h w -> p (t h w)"), v_dram[n]).then_inc(v_loaded[u], 16)

            def batch(i, u, more):
                n = 2 * i + u
                if more:
                    sp.wait_ge(S["s"].sem, S["s"].at(n))
                    sp.sem_inc(sp_passed, 1)
                    load_qk(n + 2, u)
                    sp.wait_ge(S["pv"].sem, S["pv"].at(n))
                    sp.sem_inc(sp_passed, 1)
                    load_v(n + 2, u)
                sp.wait_ge(S["out"].sem, S["out"].at(n))
                sp.dma_start(ctx_dram[n].rearrange("(t p) d -> p t d", p=R),
                             out[:, u].rearrange("p t h w -> p t (h w)")).then_inc(stored[u], 16)

            sp.wait_ge(ones_set, 1)
            sp.wait_ge(zeros_set, 2)
            for u in range(2):
                load_qk(u, u)
                load_v(u, u)
            with sp.Fori(0, NB // 2 - 1) as i:
                for u in range(2):
                    batch(i, u, True)
            for u in range(2):
                batch(NB // 2 - 1, u, False)
            for u in range(2):
                sp.wait_ge(stored[u], 16 * (NB // 2))

        @block.gpsimd
        def _(pool):
            nc.gpsimd.memset(k[96:full], 1.0).then_inc(ones_set, 1)
            pool.wait_ge(ones_set, 1)
            if NHYP:
                pool.dma_start(negc[:], curv_dram.rearrange("(a h) -> a h", a=1).broadcast_to([R, 4]))\
                    .then_inc(curv_loaded, 16)
                nc.gpsimd.memset(one[:], 1.0).then_inc(ready, 1)
                nc.gpsimd.memset(eps6[:], 1e-6).then_inc(ready, 1)
                nc.gpsimd.memset(only_shift[0:96], 0.0).then_inc(ready, 1)
                nc.gpsimd.memset(only_shift[96:full], 1.0).then_inc(ready, 1)
                pool.wait_ge(curv_loaded, 16)
                pool.wait_ge(ready, 4)
                nc.gpsimd.affine_select(out=only_shift[96:full], in_=only_shift[96:full], compare_op=ALU.is_ge,
                                        fill=0.0, base=96 - rows, pattern=[[0, R]], channel_multiplier=1)\
                    .then_inc(ready, 1)
                nc.gpsimd.tensor_tensor(root_ic[:], negc[:], c["minus_half"][:, 0:4], ALU.pow).then_inc(ready, 1)
                pool.wait_ge(ready, 6)
                nc.gpsimd.tensor_scalar(negc[:], negc[:], -1.0, None, ALU.mult).then_inc(ready, 1)

            def step(when, p, n, u, i):
                for x, lo, hi in shifts_at(when, p, 2):
                    pool.wait_ge(S["lo"].sem, S["lo"].at(n, x + 1))
                    pool.sem_inc(passed, 1)
                    for part in range(PARTS):
                        pool.dma_start(q[rows + part:rows + part + 1, u, lo:hi, :],
                                       shift[0:hi - lo, u, part, :]).then_inc(laid[u], 16)

            program(pool, step)

        @block.tensor
        def _(pe):
            for x in ("look", "s", "turn", "pv", "back"):
                S[x].give(pe)
            if NHYP:
                pe.wait_ge(ready, 7)

            def tile(bank, col, w, mask, stationary, moving, col_of_mask):
                out_ = ps[0:R, bank, col:col + w]
                if mask is not None:
                    nc.tensor.matmul(ps[0:R, bank, col + col_of_mask:col + col_of_mask + R], c["identb"][0:R, 0:R],
                                     c[mask][:], start=True, stop=False, skip_group_check=True)
                return nc.tensor.matmul(out_, stationary, moving, start=mask is None, stop=True,
                                        skip_group_check=mask is not None)

            def by_query(u, h, b, bank):
                for t, (unit, col) in sorted(QTILE.items(), key=lambda x: x[1]):
                    if unit == b:
                        w = (t + 1) * R if causal else T
                        last = tile(bank, col, w, "mask_qk" if causal else None,
                                    q[0:rows, u, h, t * R:(t + 1) * R], k[0:rows, u, h, 0:w], t * R)
                return last

            def by_key(u, h, b, bank, kind):
                for t, (unit, col) in sorted(KTILE.items(), key=lambda x: x[1]):
                    if unit == b:
                        q0 = t * R if causal else 0
                        size = full if kind in ("shifted", "shift only") else rows
                        stationary = only_shift[:] if kind == "shift only" else k[0:size, u, h, t * R:(t + 1) * R]
                        masked = causal and kind != "raw"
                        last = tile(bank, col, T - q0, "mask_kq" if masked else None,
                                    stationary, q[0:size, u, h, q0:T], 0)
                return last

            def step(when, p, n, u, i):
                if when == "main":
                    h = ORDER[p]
                    if kinds[h] != COS:
                        x = [lo <= h < hi for _, lo, hi in shifts].index(True)
                        pe.wait_ge(laid[u], 16 * PARTS * (NSH * i + x + 1))
                    for b in range(UNITS):
                        y = p * UNITS + b
                        pe.wait_ge(S["exp"].sem, S["exp"].at(n, y - 2))
                        by_key(u, h, b, RING2[y % 3], {SDPA: "shifted", HYP: "shift only", COS: "plain"}[kinds[h]])\
                            .then_inc(S["s"].sem, 1)
                if (when, p) in look:
                    h = look[when, p]
                    if h == look_order[0]:
                        pe.wait_ge(qk_loaded[u], 16 * 2 * SLOTS * (i + 1))
                    for which in (("max", "raw") if kinds[h] == HYP else ("max",)):
                        for b in range(UNITS):
                            y = uses[(h, which, b)]
                            pe.wait_ge(S["looked"].sem, S["looked"].at(n, y - 2))
                            bank = RING1[y % 3]
                            last = by_query(u, h, b, bank) if which == "max" else by_key(u, h, b, bank, "raw")
                            last.then_inc(S["look"].sem, 1)
                for x, lo, hi in shifts_at(when, p):
                    done = [y for (h, _, _), y in uses.items() if lo <= h < hi]
                    pe.wait_ge(S["looked"].sem, S["looked"].at(n, max(done) + 1))
                    if NHYP:
                        pe.wait_ge(S["hneg"].sem, S["hneg"].at(n))
                    ways = 4 + max([g for g in back_step if back_step[g] - H < shifts[x][0]], default=-1)
                    pe.wait_ge(S["out"].sem, S["out"].at((n[0], n[1] - 1), ways - 3))
                    pe.wait_ge(S["rest"].sem, S["rest"].at(n, x))
                    for t in range(NT):
                        last = nc.tensor.transpose(ps[0:hi - lo, 7, t * R:(t + 1) * R], neg[:, u, t, lo:hi],
                                                   c["ident"][0:R, 0:R])
                    last.then_inc(S["turn"].sem, 1)
                if (when, p) in product:
                    g, kt = product[when, p]
                    if g == 0 and kt == 0:
                        pe.wait_ge(v_loaded[u], 16 * (i + 1))
                    if kt == 0:
                        pe.wait_ge(S["exp"].sem, S["exp"].at(n, (4 * g + 4) * UNITS))
                        pe.wait_ge(S["oT"].sem, S["oT"].at(n, g))
                    b, col = KTILE[kt]
                    q0 = kt * R if causal else 0
                    for j in range(4 * g, 4 * g + 4):
                        a = ORDER[j] % 4
                        last = nc.tensor.matmul(ps[32 * a:32 * a + VW, 6, q0:T], vp[:, u, kt, ORDER[j], :],
                                                probT[:, j % 8, b, col:col + T - q0],
                                                start=(kt == 0), stop=(kt == NT - 1), tile_position=(0, 32 * a))
                    if kt == NT - 1:
                        last.then_inc(S["pv"].sem, 1)
                if (when, p) in back:
                    g = back[when, p]
                    pe.wait_ge(S["oT"].sem, S["oT"].at(n, g + 1))
                    pe.wait_ge(S["out"].sem, S["out"].at(n, g))
                    for x, (at, _, _) in enumerate(shifts):
                        for b in (-1, 0) if is_last(u, i) else (-1, 0, 1):
                            if back_step[g] - 4 <= at + b * H < back_step[g]:
                                pe.wait_ge(S["rest"].sem, S["rest"].at((n[0], n[1] + b), x + 1))
                    for t in range(NT):
                        last = nc.tensor.transpose(ps[0:R, 7, t * 128:(t + 1) * 128],
                                                   oT[:, g % 2, t * R:(t + 1) * R], c["ident"][:])
                    last.then_inc(S["back"].sem, 1)

            program(pe, step)

        @block.scalar
        def _(act):
            for x in ("exp", "oT", "hi", "mid") + (("hl", "root", "l1", "l2", "score") if NHYP else ()):
                S[x].give(act)
            act.wait_ge(zeros_set, 3)
            if NHYP:
                nc.scalar.preload_act_table_set("natural_log_exp_and_others")
                act.wait_ge(ready, 7)

            def step(when, p, n, u, i):
                if when == "main":
                    h = ORDER[p]
                    act.wait_ge(S["pv"].sem, S["pv"].at(n, p // 4 - 1))
                    for b in range(UNITS):
                        y = p * UNITS + b
                        if kinds[h] == HYP:
                            a = HYPS.index(h)
                            act.wait_ge(S["shifted"].sem, S["shifted"].at(n, hyp_slot[a] * UNITS + b + 1))
                            src = hw[:, u, a, b * T:(b + 1) * T]
                        else:
                            act.wait_ge(S["s"].sem, S["s"].at(n, y + 1))
                            src = ps[0:R, RING2[y % 3], 0:T]
                        nc.scalar.activation(probT[0:R, p % 8, b, :], src, ACT.Exp,
                                             scale=float(HD) ** 0.5 if kinds[h] == COS else 1.0)\
                            .then_inc(S["exp"].sem, 1)
                if product.get((when, p), (0, 0))[1] == NT - 1:
                    g = product[when, p][0]
                    act.wait_ge(S["pv"].sem, S["pv"].at(n, g + 1))
                    act.wait_ge(S["back"].sem, S["back"].at(n, g - 1))
                    nc.scalar.copy(oT[:, g % 2], ps[:, 6, 0:T]).then_inc(S["oT"].sem, 1)
                for a, h in enumerate(HYPS):
                    if (when, p) == place(look_step[h] + ROOT):
                        act.wait_ge(S["hu"].sem, S["hu"].at(n, a + 1))
                        nc.scalar.activation(hu[:, a], hu[:, a], ACT.Ln).then_inc(S["hl"].sem, 1)
                        act.wait_ge(S["hl"].sem, S["hl"].at(n, a + 1))
                        nc.scalar.activation(hu[:, a], hu[:, a], ACT.Exp, scale=0.5).then_inc(S["root"].sem, 1)
                    if (when, p) == place(look_step[h] + SCORE):
                        act.wait_ge(S["z"].sem, S["z"].at(n, a + 1))
                        nc.scalar.activation(hw[:, u, a], hw[:, u, a], ACT.Ln, bias=one[:]).then_inc(S["l1"].sem, 1)
                        act.wait_ge(S["l1"].sem, S["l1"].at(n, a + 1))
                        nc.scalar.activation(hw[:, u, a], hw[:, u, a], ACT.Ln, bias=eps6[:],
                                             scale=root_ic[:, a:a + 1]).then_inc(S["l2"].sem, 1)
                        act.wait_ge(S["l2"].sem, S["l2"].at(n, a + 1))
                        nc.scalar.activation(hw[:, u, a], hw[:, u, a], ACT.Exp, scale=-1.0)\
                            .then_inc(S["score"].sem, 1)
                for x, lo, hi in shifts_at(when, p, 1):
                    act.wait_ge(S["turn"].sem, S["turn"].at(n, x + 1))
                    act.wait_ge(laid[u], 16 * PARTS * (NSH * i + x))
                    nc.scalar.copy(shift[0:hi - lo, u, 0], ps[0:hi - lo, 7, 0:T]).then_inc(S["hi"].sem, 1)
                for x, lo, hi in shifts_at(when, p, 2):
                    act.wait_ge(S["rest"].sem, S["rest"].at(n, x + 1))
                    nc.scalar.copy(shift[0:hi - lo, u, 1], rest[0:hi - lo, u]).then_inc(S["mid"].sem, 1)

            program(act, step)

        @block.vector
        def _(dve):
            for x in ("looked", "rest", "lo", "rec", "out") + (("top", "w", "wc", "hu", "z", "hneg", "shifted") if NHYP else ()):
                S[x].give(dve)
            nc.vector.memset(q[96:full], 0.0).then_inc(zeros_set, 1)
            nc.vector.memset(vp[64:RP], 0.0).then_inc(zeros_set, 1)
            nc.vector.memset(probT[64:RP], 0.0).then_inc(zeros_set, 1)
            if NHYP:
                dve.wait_ge(ready, 7)

            def step(when, p, n, u, i):
                if when == "main" and kinds[ORDER[p]] == HYP:
                    a = HYPS.index(ORDER[p])
                    for b in range(UNITS):
                        y = p * UNITS + b
                        dve.wait_ge(S["s"].sem, S["s"].at(n, y + 1))
                        dve.wait_ge(S["score"].sem, S["score"].at(n, a + 1))
                        d = hw[:, u, a, b * T:(b + 1) * T]
                        nc.vector.tensor_tensor(d, d, ps[0:R, RING2[y % 3], 0:T], ALU.add)\
                            .then_inc(S["shifted"].sem, 1)
                if (when, p) in look:
                    h = look[when, p]
                    a = HYPS.index(h) if kinds[h] == HYP else None
                    if a is not None:
                        dve.wait_ge(S["exp"].sem, S["exp"].at((n[0], n[1] - 1), 0))
                    for b in range(UNITS):
                        y = uses[(h, "max", b)]
                        dve.wait_ge(S["look"].sem, S["look"].at(n, y + 1))
                        for t, (unit, col) in sorted(QTILE.items(), key=lambda x: x[1]):
                            if unit == b:
                                src = ps[0:R, RING1[y % 3], col:col + ((t + 1) * R if causal else T)]
                                if a is not None:
                                    nc.vector.reduce_max(top[:, u, a, t:t + 1], src, AX.X).then_inc(S["top"].sem, 1)
                                else:
                                    last = nc.vector.tensor_reduce(neg[:, u, t, h:h + 1], src, AX.X, ALU.max,
                                                                   negate=True)
                        if a is None:
                            last.then_inc(S["looked"].sem, 1)
                        else:
                            dve.wait_ge(S["top"].sem, S["top"].at(n, a * NT + (1 if b == 0 else NT)))
                            dve.sem_inc(S["looked"].sem, 1)
                    if a is not None:
                        nc.vector.tensor_scalar(hw[:, u, a, 2 * T:W], top[:, u, a], negc[:, a:a + 1], -1.0,
                                                ALU.mult, ALU.add).then_inc(S["w"].sem, 1)
                        for b in range(UNITS):
                            y = uses[(h, "raw", b)]
                            dve.wait_ge(S["look"].sem, S["look"].at(n, y + 1))
                            nc.vector.tensor_scalar(hw[:, u, a, b * T:(b + 1) * T], ps[0:R, RING1[y % 3], 0:T],
                                                    negc[:, a:a + 1], -1.0, ALU.mult, ALU.add)\
                                .then_inc(S["looked"].sem, 1)
                        dve.wait_ge(S["w"].sem, S["w"].at(n, a + 1))
                        dve.wait_ge(S["looked"].sem, S["looked"].at(n, y + 1))
                        nc.vector.tensor_scalar(hw[:, u, a], hw[:, u, a], 2.0 ** -23, None, ALU.max)\
                            .then_inc(S["wc"].sem, 1)
                        dve.wait_ge(S["z"].sem, S["z"].at(n, a + 1 - NHYP))
                        dve.wait_ge(S["wc"].sem, S["wc"].at(n, a + 1))
                        nc.vector.scalar_tensor_tensor(out=hu[:, a], in0=hw[:, u, a], scalar=2.0,
                                                       in1=hw[:, u, a], op0=ALU.add, op1=ALU.mult)\
                            .then_inc(S["hu"].sem, 1)
                for a, h in enumerate(HYPS):
                    if (when, p) == place(look_step[h] + SUM):
                        dve.wait_ge(S["root"].sem, S["root"].at(n, a + 1))
                        nc.vector.tensor_tensor(hw[:, u, a], hw[:, u, a], hu[:, a], ALU.add).then_inc(S["z"].sem, 1)
                if NHYP and (when, p) == NEGATE:
                    dve.wait_ge(S["score"].sem, S["score"].at(n))
                    nc.vector.tensor_scalar(neg[:, u, :, HYPS[0]:HYPS[0] + NHYP].rearrange("p t a -> p a t"),
                                            hw[:, u, :, 2 * T:W], -1.0, None, ALU.mult).then_inc(S["hneg"].sem, 1)
                for x, lo, hi in shifts_at(when, p, 1):
                    dve.wait_ge(S["hi"].sem, S["hi"].at(n, x + 1))
                    dve.wait_ge(S["lo"].sem, S["lo"].at(n, x))
                    nc.vector.tensor_tensor(rest[0:hi - lo, u], ps[0:hi - lo, 7, 0:T], shift[0:hi - lo, u, 0],
                                            ALU.subtract).then_inc(S["rest"].sem, 1)
                for x, lo, hi in shifts_at(when, p, 2):
                    dve.wait_ge(S["mid"].sem, S["mid"].at(n, x + 1))
                    nc.vector.tensor_tensor(shift[0:hi - lo, u, 2], rest[0:hi - lo, u], shift[0:hi - lo, u, 1],
                                            ALU.subtract).then_inc(S["lo"].sem, 1)
                if (when, p) in back:
                    g = back[when, p]
                    if g == 0:
                        dve.wait_ge(stored[u], 16 * i)
                    dve.wait_ge(S["back"].sem, S["back"].at(n, g + 1))
                    dve.wait_ge(S["out"].sem, S["out"].at(n, g - 1))
                    x = ps[0:R, 7, 0:NT * 128].rearrange("p (t a w) -> p t a w", t=NT, a=4)
                    nc.vector.reciprocal(rec[:, g % 2], x[:, :, :, HD]).then_inc(S["rec"].sem, 1)
                    dve.wait_ge(S["rec"].sem, S["rec"].at(n, g + 1))
                    h0 = min(ORDER[4 * g:4 * g + 4])
                    nc.vector.tensor_tensor(out[:, u, :, h0:h0 + 4, :], x[:, :, :, 0:HD],
                                            rec[:, g % 2].unsqueeze(3).to_broadcast([R, NT, 4, HD]), ALU.mult)\
                        .then_inc(S["out"].sem, 1)

            program(dve, step)


def row(dram):
    return dram.rearrange("(a d) -> a d", a=1)


def phase_g1(nc, c, ps, NB, ctx_dram, h2_dram, proj_dram, projb_dram, wq_dram, wk_dram, wv_dram,
             bq_dram, bk_dram, bv_dram, h3_dram, x3_dram, parts_dram, v_dram):
    ctx = ExitStack()
    with ctx:
        def sb(name, shape, dt=F32):
            return ctx.enter_context(nc.sbuf_tensor("p_" + name, shape, dt))

        def sem(name):
            return nc.alloc_semaphore("p_" + name)

        proj, wv = sb("proj", [128, CT, D]), sb("wv", [128, CT, D])
        wqk = sb("wqk", [128, CT, 2, D])
        bqk = sb("bqk", [128, 2, CT])
        projb, bv = sb("projb", [R, D]), sb("bv", [R, D])
        cx = sb("cx", [R, 2, NT, D])
        cT = sb("cT", [128, 2, CT, T])
        h = sb("h", [R, 2, NT, D])
        stats = sb("stats", [R, 2, NT, 6])
        mv = sb("mv", [R, 2, NT, 2])
        var_eps = sb("var_eps", [R, 2, NT])
        rstd = sb("rstd", [R, 2, NT])
        xn = sb("xn", [R, 2, NT, D])
        xT = sb("xT", [128, 2, CT, T])
        parts = sb("parts", [128, 2, 2 * CT, PARTS, T], BF16)
        rest = sb("rest", [128, 2, 2, T])
        vp = sb("vp", [R, 2, NT, H, VW])
        w_loaded, scaled, filled = sem("w_loaded"), sem("scaled"), sem("filled")
        c_loaded = [sem(f"c_loaded{u}") for u in range(2)]
        h_loaded = [sem(f"h_loaded{u}") for u in range(2)]
        h_stored = [sem(f"h_stored{u}") for u in range(2)]
        x_stored = [sem(f"x_stored{u}") for u in range(2)]
        p_stored = [sem(f"p_stored{u}") for u in range(2)]
        v_stored = [sem(f"v_stored{u}") for u in range(2)]
        S = signals(ctx, nc, "p", cT=1, cT_out=1, y=1, hb=1, h3=1, bn=NT + 1, mv=1, eps=1, rstd=1, xn=NT, xT=1,
                    xT_out=1, v=1, v_out=2, qk=2 * CT, hi=2 * CT, rest=2 * CT, mid=2 * CT, lo=2 * CT)
        banks = [lambda k, u=u: ps[:, 4 * u + k, :] for u in range(2)]
        QK_BANK = (2, 3, 0, 1)
        WEIGHTS = 16 * (4 + 2 * CT + 2)
        block = ctx.enter_context(nc.Block())

        @block.sync
        def _(sp):
            def load_c(n, u):
                sp.dma_start(cx[:, u], ctx_dram[n].rearrange("(t p) d -> p t d", p=R)).then_inc(c_loaded[u], 16)

            def load_h(n, u):
                sp.dma_start(h[:, u], h2_dram[n].rearrange("(t p) d -> p t d", p=R)).then_inc(h_loaded[u], 16)

            def pair(i, more):
                for u in range(2):
                    n = 2 * i + u
                    if more:
                        sp.wait_ge(S["cT"].sem, S["cT"].at(n))
                        load_c(n + 2, u)
                for u in range(2):
                    n = 2 * i + u
                    sp.wait_ge(S["h3"].sem, S["h3"].at(n))
                    sp.dma_start(h3_dram[n].rearrange("(t p) d -> p t d", p=R), h[:, u]).then_inc(h_stored[u], 16)
                for u in range(2):
                    n = 2 * i + u
                    sp.wait_ge(S["xn"].sem, S["xn"].at(n))
                    sp.dma_start(x3_dram[n].rearrange("(t p) d -> p t d", p=R), xn[:, u]).then_inc(x_stored[u], 16)
                    if more:
                        sp.wait_ge(h_stored[u], 16 * i + 16)
                        load_h(n + 2, u)
                for u in range(2):
                    n = 2 * i + u
                    sp.wait_ge(S["v_out"].sem, S["v_out"].at(n))
                    sp.dma_start(v_dram[n], vp[:, u].rearrange("p t h w -> p (t h w)")).then_inc(v_stored[u], 16)
                for u in range(2):
                    n = 2 * i + u
                    for j in range(2 * CT):
                        sp.wait_ge(S["lo"].sem, S["lo"].at(n, j + 1))
                        sp.dma_start(parts_dram[n, j // CT, (j % CT) * 128:(j % CT + 1) * 128]
                                     .rearrange("r k t -> r (k t)"),
                                     parts[:, u, j].rearrange("p k t -> p (k t)")).then_inc(p_stored[u], 16)

            sp.dma_start(wqk[:, :, 0], wq_dram.rearrange("(k p) n -> p k n", p=128)).then_inc(w_loaded, 16)
            sp.dma_start(wqk[:, :, 1], wk_dram.rearrange("(k p) n -> p k n", p=128)).then_inc(w_loaded, 16)
            sp.dma_start(proj[:], proj_dram.rearrange("(k p) n -> p k n", p=128)).then_inc(w_loaded, 16)
            sp.dma_start(wv[:], wv_dram.rearrange("(k p) n -> p k n", p=128)).then_inc(w_loaded, 16)
            for j, dram in enumerate((bq_dram, bk_dram)):
                for k in range(CT):
                    sp.dma_start(bqk[:, j, k:k + 1], dram[k * 128:(k + 1) * 128].rearrange("(p a) -> p a", a=1))\
                        .then_inc(w_loaded, 16)
            sp.dma_start(projb[:], row(projb_dram).broadcast_to([R, D])).then_inc(w_loaded, 16)
            sp.dma_start(bv[:], row(bv_dram).broadcast_to([R, D])).then_inc(w_loaded, 16)
            for u in range(2):
                load_c(u, u)
                load_h(u, u)
            with sp.Fori(0, NB // 2 - 1) as i:
                pair(i, True)
            pair(NB // 2 - 1, False)
            for u in range(2):
                for s, times in ((h_stored, 1), (x_stored, 1), (p_stored, 2 * CT), (v_stored, 1)):
                    sp.wait_ge(s[u], 16 * times * (NB // 2))

        @block.gpsimd
        def _(pool):
            for k in ("hb", "eps", "rstd"):
                S[k].give(pool)
            pool.wait_ge(w_loaded, WEIGHTS)
            with pool.Fori(0, NB // 2) as i:
                for u in range(2):
                    n = 2 * i + u
                    pool.wait_ge(h_loaded[u], 16 * i + 16)
                    nc.gpsimd.tensor_tensor(h[:, u], h[:, u], projb[:].unsqueeze(1).to_broadcast([R, NT, D]), ALU.add)\
                        .then_inc(S["hb"].sem, 1)
                for u in range(2):
                    ln_rstd(nc, pool, c, mv[:, u], var_eps[:, u], rstd[:, u],
                            S["mv"], S["eps"], S["rstd"], 2 * i + u)

        @block.scalar
        def _(act):
            for k in ("cT_out", "xT_out", "hi", "mid"):
                S[k].give(act)
            act.wait_ge(scaled, 2)
            with act.Fori(0, NB // 2) as i:
                for u in range(2):
                    n = 2 * i + u
                    act.wait_ge(S["cT"].sem, S["cT"].at(n))
                    act.wait_ge(S["y"].sem, S["y"].before(n))
                    nc.scalar.copy(cT[:, u], ps[:, 4 * u + 2:4 * u + 4, 0:T]).then_inc(S["cT_out"].sem, 1)
                for u in range(2):
                    n = 2 * i + u
                    act.wait_ge(S["xT"].sem, S["xT"].at(n))
                    act.wait_ge(S["qk"].sem, S["qk"].before(n))
                    nc.scalar.copy(xT[:, u], ps[:, 4 * u + 2:4 * u + 4, 0:T]).then_inc(S["xT_out"].sem, 1)
                for u in range(2):
                    n, B = 2 * i + u, banks[u]
                    act.wait_ge(p_stored[u], 16 * 2 * CT * i)
                    for j in range(2 * CT):
                        act.wait_ge(S["qk"].sem, S["qk"].at(n, j + 1))
                        nc.scalar.activation(parts[:, u, j, 0, :], B(QK_BANK[j])[:, 0:T], ACT.Identity,
                                             bias=bqk[:, j // CT, j % CT:j % CT + 1]).then_inc(S["hi"].sem, 1)
                        act.wait_ge(S["rest"].sem, S["rest"].at(n, j + 1))
                        nc.scalar.copy(parts[:, u, j, 1, :], rest[:, u, j % 2]).then_inc(S["mid"].sem, 1)

        @block.vector
        def _(dve):
            for k in ("h3", "bn", "mv", "xn", "v_out", "rest", "lo"):
                S[k].give(dve)
            dve.wait_ge(w_loaded, WEIGHTS)
            nc.vector.tensor_scalar(wqk[:, :, 0], wqk[:, :, 0], float(HD) ** -0.5, None, ALU.mult).then_inc(scaled, 1)
            nc.vector.tensor_scalar(bqk[:, 0], bqk[:, 0], float(HD) ** -0.5, None, ALU.mult).then_inc(scaled, 1)
            nc.vector.memset(vp[:], 1.0).then_inc(filled, 1)
            dve.wait_ge(filled, 1)
            dve.wait_ge(scaled, 2)
            with dve.Fori(0, NB // 2) as i:
                for u in range(2):
                    n, B = 2 * i + u, banks[u]
                    dve.wait_ge(S["y"].sem, S["y"].at(n))
                    dve.wait_ge(S["hb"].sem, S["hb"].at(n))
                    nc.vector.tensor_tensor(h[:, u, 0:2, :], B(0)[0:R, :].rearrange("p (t d) -> p t d", t=2),
                                            h[:, u, 0:2, :], ALU.add)
                    nc.vector.tensor_tensor(h[:, u, 2, :], B(1)[0:R, 0:D], h[:, u, 2, :], ALU.add)\
                        .then_inc(S["h3"].sem, 1)
                for u in range(2):
                    n = 2 * i + u
                    dve.wait_ge(S["h3"].sem, S["h3"].at(n))
                    ln_stats(nc, dve, h[:, u], stats[:, u], mv[:, u], (S["bn"].sem, S["bn"].at(n)), S["mv"])
                for u in range(2):
                    n = 2 * i + u
                    dve.wait_ge(S["rstd"].sem, S["rstd"].at(n))
                    dve.wait_ge(S["xT"].sem, S["xT"].before(n))
                    dve.wait_ge(x_stored[u], 16 * i)
                    ln_apply(nc, xn[:, u], h[:, u], mv[:, u], rstd[:, u], S["xn"])
                for u in range(2):
                    n, B = 2 * i + u, banks[u]
                    dve.wait_ge(S["v"].sem, S["v"].at(n))
                    dve.wait_ge(v_stored[u], 16 * i)
                    bias = bv[:].rearrange("p (h w) -> p h w", w=HD)
                    for t in range(NT):
                        x = B(t // 2)[0:R, (t % 2) * D:(t % 2 + 1) * D].rearrange("p (h w) -> p h w", w=HD)
                        last = nc.vector.tensor_tensor(vp[:, u, t, :, 0:HD], x, bias, ALU.add)
                        if t > 0:
                            last.then_inc(S["v_out"].sem, 1)
                for u in range(2):
                    n, B = 2 * i + u, banks[u]
                    for j in range(2 * CT):
                        dve.wait_ge(S["hi"].sem, S["hi"].at(n, j + 1))
                        if j >= 2:
                            dve.wait_ge(S["lo"].sem, S["lo"].at(n, j - 1))
                        nc.vector.scalar_tensor_tensor(out=rest[:, u, j % 2], in0=B(QK_BANK[j])[:, 0:T],
                                                       scalar=bqk[:, j // CT, j % CT:j % CT + 1],
                                                       in1=parts[:, u, j, 0, :], op0=ALU.add, op1=ALU.subtract)\
                            .then_inc(S["rest"].sem, 1)
                        dve.wait_ge(S["mid"].sem, S["mid"].at(n, j + 1))
                        nc.vector.tensor_tensor(parts[:, u, j, 2, :], rest[:, u, j % 2], parts[:, u, j, 1, :],
                                                ALU.subtract).then_inc(S["lo"].sem, 1)

        @block.tensor
        def _(pe):
            for k in ("cT", "y", "xT", "v", "qk"):
                S[k].give(pe)
            pe.wait_ge(w_loaded, WEIGHTS)
            pe.wait_ge(scaled, 1)
            with pe.Fori(0, NB // 2) as i:
                for u in range(2):
                    n, B = 2 * i + u, banks[u]
                    pe.wait_ge(c_loaded[u], 16 * i + 16)
                    pe.wait_ge(S["lo"].sem, S["lo"].before(n))
                    transpose_tokens(nc, pe, c, cx[:, u], lambda k: B(2 + k)).then_inc(S["cT"].sem, 1)
                for u in range(2):
                    n, B = 2 * i + u, banks[u]
                    pe.wait_ge(S["cT_out"].sem, S["cT_out"].at(n))
                    for t in range(NT):
                        for k in range(CT):
                            last = nc.tensor.matmul(B(t // 2)[0:R, (t % 2) * D:(t % 2 + 1) * D],
                                                    cT[:, u, k, t * R:(t + 1) * R], proj[:, k, :],
                                                    start=(k == 0), stop=(k == CT - 1))
                    last.then_inc(S["y"].sem, 1)
                for u in range(2):
                    n, B = 2 * i + u, banks[u]
                    pe.wait_ge(S["xn"].sem, S["xn"].at(n))
                    transpose_tokens(nc, pe, c, xn[:, u], lambda k: B(2 + k)).then_inc(S["xT"].sem, 1)
                for u in range(2):
                    n, B = 2 * i + u, banks[u]
                    pe.wait_ge(S["xT_out"].sem, S["xT_out"].at(n))
                    pe.wait_ge(S["h3"].sem, S["h3"].at(n))
                    for t in range(NT):
                        for k in range(CT):
                            last = nc.tensor.matmul(B(t // 2)[0:R, (t % 2) * D:(t % 2 + 1) * D],
                                                    xT[:, u, k, t * R:(t + 1) * R], wv[:, k, :],
                                                    start=(k == 0), stop=(k == CT - 1))
                    last.then_inc(S["v"].sem, 1)
                for u in range(2):
                    n, B = 2 * i + u, banks[u]
                    for j in range(2 * CT):
                        if j >= 2:
                            pe.wait_ge(S["v_out"].sem, S["v_out"].at(n, j - 1))
                        for k in range(CT):
                            last = nc.tensor.matmul(B(QK_BANK[j])[:, 0:T],
                                                    wqk[:, k, j // CT, (j % CT) * 128:(j % CT + 1) * 128],
                                                    xT[:, u, k, :], start=(k == 0), stop=(k == CT - 1))
                        last.then_inc(S["qk"].sem, 1)


def phase_g3(nc, c, ps, NB, ctx_dram, x3_dram, h3_dram, wo_dram, bo_dram, g1_dram, be1_dram, wg_dram, bg_dram,
             we_dram, bexp_dram, g2_dram, be2_dram, out_dram):
    ctx = ExitStack()
    E, PE_ = EXPERTS, EXPERTS // 2
    with ctx:
        def sb(name, shape, dt=F32):
            return ctx.enter_context(nc.sbuf_tensor("m_" + name, shape, dt))

        def sem(name):
            return nc.alloc_semaphore("m_" + name)

        wo, wg = sb("wo", [128, CT, D]), sb("wg", [128, CT, E])
        we = sb("we", [128, CT, E, D])
        bexp = sb("bexp", [E, D])
        rows = {k: sb(k, [R, D]) for k in ("bo", "g1", "be1", "g2", "be2")}
        bg = sb("bg", [R, E])
        lower = sb("lower", [R, E, E])
        cx = sb("cx", [R, 2, NT, D])
        x = sb("x", [R, 2, NT, D])
        h = sb("h", [R, 2, NT, D])
        cT = sb("cT", [128, 2, CT, T])
        xT = sb("xT", [128, 2, CT, T])
        a = sb("a", [R, 2, NT, D])
        ag = sb("ag", [R, 2, NT, D])
        acc = sb("acc", [R, 2, NT, D])
        accg = sb("accg", [R, 2, NT, D])
        stats = sb("stats", [R, 2, NT, 6])
        mv = sb("mv", [R, 2, NT, 2])
        var_eps = sb("var_eps", [R, 2, NT])
        rstd = sb("rstd", [R, 2, NT])
        logit = sb("logit", [R, 2 * NT, E])
        top = sb("top", [R, 2 * NT])
        shifted = sb("shifted", [R, 2 * NT, E])
        expl = sb("expl", [R, 2 * NT, E])
        total = sb("total", [R, 2 * NT])
        greater = sb("greater", [R, 2 * NT, E, E])
        equal = sb("equal", [R, 2 * NT, E, E])
        rank = sb("rank", [R, 2 * NT, E])
        chosen = sb("chosen", [R, 2 * NT, E])
        weight = sb("weight", [R, 2 * NT, E])
        weightT = sb("weightT", [E, 2, T])
        w_loaded, filled, passed = sem("w_loaded"), sem("filled"), sem("passed")
        c_loaded = [sem(f"c_loaded{u}") for u in range(2)]
        x_loaded = [sem(f"x_loaded{u}") for u in range(2)]
        h_loaded = [sem(f"h_loaded{u}") for u in range(2)]
        stored = [sem(f"stored{u}") for u in range(2)]
        M = PE_ * NT
        EARLY = 2
        S = signals(ctx, nc, "m", cT=1, cT_out=1, y=1, xb=1, hb=1, a=1, bn=NT + 1, mv=1, eps=1, rstd=1, an=NT, ag=1,
                    x4=1, xT=1, xT_out=1, gl=1, logit=1, wT=1, wT_out=1, bias=1, acc0=1, early=EARLY, me=M - EARLY, acc=2 * M,
                    hx=1, bn2=NT + 1, mv2=1, eps2=1, rstd2=1, accn=NT, accg=1, out=1)
        G = signals(ctx, nc, "mg", top=1, shifted=1, exp=1, greater=1, equal=1, lower=1, above=1, rank=1,
                    total=1, inv=1, chosen=1, weight=1)
        banks = [lambda k, u=u: ps[:, 4 * u + k, :] for u in range(2)]
        block = ctx.enter_context(nc.Block())

        @block.sync
        def _(sp):
            def tokens(dram):
                return dram.rearrange("(t p) d -> p t d", p=R)

            def pair(i, more):
                for u in range(2):
                    n = 2 * i + u
                    if more:
                        sp.wait_ge(S["cT"].sem, S["cT"].at(n))
                        sp.dma_start(cx[:, u], tokens(ctx_dram[n + 2])).then_inc(c_loaded[u], 16)
                for u in range(2):
                    n = 2 * i + u
                    if more:
                        sp.wait_ge(S["xT"].sem, S["xT"].at(n))
                        sp.sem_inc(passed, 1)
                        sp.wait_ge(S["hx"].sem, S["hx"].at(n))
                        sp.dma_start(x[:, u], tokens(x3_dram[n + 2])).then_inc(x_loaded[u], 16)
                for u in range(2):
                    n = 2 * i + u
                    sp.wait_ge(S["out"].sem, S["out"].at(n))
                    sp.dma_start(tokens(out_dram[n]), h[:, u]).then_inc(stored[u], 16)
                for u in range(2):
                    n = 2 * i + u
                    if more:
                        sp.wait_ge(stored[u], 16 * i + 16)
                        sp.dma_start(h[:, u], tokens(h3_dram[n + 2])).then_inc(h_loaded[u], 16)

            sp.dma_start(wo[:], wo_dram.rearrange("(k p) n -> p k n", p=128)).then_inc(w_loaded, 16)
            sp.dma_start(wg[:], wg_dram.rearrange("(k p) n -> p k n", p=128)).then_inc(w_loaded, 16)
            for e in range(E):
                sp.dma_start(we[:, :, e], we_dram[e].rearrange("(k p) n -> p k n", p=128)).then_inc(w_loaded, 16)
            sp.dma_start(bexp[:], bexp_dram).then_inc(w_loaded, 16)
            for k, dram in (("bo", bo_dram), ("g1", g1_dram), ("be1", be1_dram), ("g2", g2_dram), ("be2", be2_dram)):
                sp.dma_start(rows[k][:], row(dram).broadcast_to([R, D])).then_inc(w_loaded, 16)
            sp.dma_start(bg[:], row(bg_dram).broadcast_to([R, E])).then_inc(w_loaded, 16)
            for u in range(2):
                sp.dma_start(cx[:, u], tokens(ctx_dram[u])).then_inc(c_loaded[u], 16)
                sp.dma_start(x[:, u], tokens(x3_dram[u])).then_inc(x_loaded[u], 16)
                sp.dma_start(h[:, u], tokens(h3_dram[u])).then_inc(h_loaded[u], 16)
            with sp.Fori(0, NB // 2 - 1) as i:
                pair(i, True)
            pair(NB // 2 - 1, False)
            for u in range(2):
                sp.wait_ge(stored[u], 16 * (NB // 2))

        WEIGHTS = 16 * (2 + E + 1 + 5 + 1)

        def everywhere(k):
            return rows[k][:].unsqueeze(1).to_broadcast([R, NT, D])

        @block.gpsimd
        def _(pool):
            for k in ("xb", "hb", "eps", "rstd", "hx", "eps2", "rstd2"):
                S[k].give(pool)
            nc.gpsimd.memset(lower[:], 1.0).then_inc(filled, 1)
            pool.wait_ge(filled, 1)
            nc.gpsimd.affine_select(out=lower[:], in_=lower[:], compare_op=ALU.is_gt, fill=0.0, base=0,
                                    pattern=[[1, E], [-1, E]], channel_multiplier=0).then_inc(filled, 1)
            pool.wait_ge(w_loaded, WEIGHTS)
            with pool.Fori(0, NB // 2) as i:
                for u in range(2):
                    n = 2 * i + u
                    pool.wait_ge(x_loaded[u], 16 * i + 16)
                    nc.gpsimd.tensor_tensor(x[:, u], x[:, u], everywhere("be1"), ALU.add).then_inc(S["xb"].sem, 1)
                for u in range(2):
                    ln_rstd(nc, pool, c, mv[:, u], var_eps[:, u], rstd[:, u],
                            S["mv"], S["eps"], S["rstd"], 2 * i + u)
                for u in range(2):
                    n = 2 * i + u
                    pool.wait_ge(h_loaded[u], 16 * i + 16)
                    nc.gpsimd.tensor_tensor(h[:, u], h[:, u], everywhere("be2"), ALU.add).then_inc(S["hb"].sem, 1)
                    pool.wait_ge(S["hb"].sem, S["hb"].at(n))
                    pool.wait_ge(S["x4"].sem, S["x4"].at(n))
                    nc.gpsimd.tensor_tensor(h[:, u], h[:, u], x[:, u], ALU.add).then_inc(S["hx"].sem, 1)
                for u in range(2):
                    ln_rstd(nc, pool, c, mv[:, u], var_eps[:, u], rstd[:, u],
                            S["mv2"], S["eps2"], S["rstd2"], 2 * i + u)

        @block.scalar
        def _(act):
            for k in ("cT_out", "xT_out", "wT_out", "acc0"):
                S[k].give(act)
            G["exp"].give(act)
            with act.Fori(0, NB // 2) as i:
                for u in range(2):
                    n = 2 * i + u
                    act.wait_ge(S["cT"].sem, S["cT"].at(n))
                    act.wait_ge(S["y"].sem, S["y"].before(n))
                    nc.scalar.copy(cT[:, u], ps[:, 4 * u + 2:4 * u + 4, 0:T]).then_inc(S["cT_out"].sem, 1)
                for u in range(2):
                    n = 2 * i + u
                    act.wait_ge(S["xT"].sem, S["xT"].at(n))
                    act.wait_ge(S["me"].sem, S["me"].before(n))
                    nc.scalar.copy(xT[:, u], ps[:, 4 * u + 2:4 * u + 4, 0:T]).then_inc(S["xT_out"].sem, 1)
                act.wait_ge(G["shifted"].sem, G["shifted"].at(i))
                act.wait_ge(G["chosen"].sem, G["chosen"].at(i - 1))
                nc.scalar.activation(expl[:], shifted[:], ACT.Exp).then_inc(G["exp"].sem, 1)
                for u in range(2):
                    n = 2 * i + u
                    act.wait_ge(S["wT"].sem, S["wT"].at(n))
                    act.wait_ge(S["bias"].sem, S["bias"].before(n))
                    nc.scalar.copy(weightT[:, u], banks[u](1)[0:E, 0:T]).then_inc(S["wT_out"].sem, 1)
                for u in range(2):
                    n, B = 2 * i + u, banks[u]
                    act.wait_ge(S["bias"].sem, S["bias"].at(n))
                    act.wait_ge(S["accg"].sem, S["accg"].before(n))
                    nc.scalar.copy(acc[:, u, 0:2], B(0)[0:R, :].rearrange("p (t d) -> p t d", t=2))
                    nc.scalar.copy(acc[:, u, 2], B(1)[0:R, 0:D]).then_inc(S["acc0"].sem, 1)

        @block.vector
        def _(dve):
            for k in ("a", "bn", "mv", "an", "ag", "x4", "logit", "acc", "bn2", "mv2", "accn", "accg", "out"):
                S[k].give(dve)
            for k in G:
                if k != "exp":
                    G[k].give(dve)
            dve.wait_ge(w_loaded, WEIGHTS)
            dve.wait_ge(filled, 2)
            with dve.Fori(0, NB // 2) as i:
                for u in range(2):
                    n, B = 2 * i + u, banks[u]
                    dve.wait_ge(S["y"].sem, S["y"].at(n))
                    dve.wait_ge(S["ag"].sem, S["ag"].before(n))
                    for t in range(NT):
                        last = nc.vector.tensor_tensor(a[:, u, t], B(t // 2)[0:R, (t % 2) * D:(t % 2 + 1) * D],
                                                       rows["bo"][:], ALU.add)
                    last.then_inc(S["a"].sem, 1)
                for u in range(2):
                    n = 2 * i + u
                    dve.wait_ge(S["a"].sem, S["a"].at(n))
                    ln_stats(nc, dve, a[:, u], stats[:, u], mv[:, u], (S["bn"].sem, S["bn"].at(n)), S["mv"])
                for u in range(2):
                    n = 2 * i + u
                    dve.wait_ge(S["rstd"].sem, S["rstd"].at(n))
                    ln_apply(nc, a[:, u], a[:, u], mv[:, u], rstd[:, u], S["an"])
                for u in range(2):
                    n = 2 * i + u
                    dve.wait_ge(S["an"].sem, S["an"].at(n))
                    dve.wait_ge(S["x4"].sem, S["x4"].before(n))
                    nc.vector.tensor_tensor(ag[:, u], a[:, u], everywhere("g1"), ALU.mult).then_inc(S["ag"].sem, 1)
                for u in range(2):
                    n = 2 * i + u
                    dve.wait_ge(S["ag"].sem, S["ag"].at(n))
                    dve.wait_ge(S["xb"].sem, S["xb"].at(n))
                    nc.vector.tensor_tensor(x[:, u], x[:, u], ag[:, u], ALU.add).then_inc(S["x4"].sem, 1)
                for u in range(2):
                    n = 2 * i + u
                    dve.wait_ge(S["gl"].sem, S["gl"].at(n))
                    nc.vector.tensor_tensor(logit[:, u * NT:(u + 1) * NT],
                                            banks[u](1)[0:R, D:D + NT * E].rearrange("p (t e) -> p t e", e=E),
                                            bg[:].unsqueeze(1).to_broadcast([R, NT, E]), ALU.add)\
                        .then_inc(S["logit"].sem, 1)
                dve.wait_ge(S["logit"].sem, S["logit"].at(2 * i + 1))
                nc.vector.reduce_max(top[:], logit[:], AX.X).then_inc(G["top"].sem, 1)
                dve.wait_ge(G["top"].sem, G["top"].at(i))
                nc.vector.tensor_tensor(shifted[:], logit[:], top[:].unsqueeze(2).to_broadcast([R, 2 * NT, E]),
                                        ALU.subtract).then_inc(G["shifted"].sem, 1)
                every = [R, 2 * NT, E, E]
                other, own = logit[:].unsqueeze(2).to_broadcast(every), logit[:].unsqueeze(3).to_broadcast(every)
                nc.vector.tensor_tensor(equal[:], other, own, ALU.is_equal).then_inc(G["equal"].sem, 1)
                nc.vector.tensor_tensor(greater[:], other, own, ALU.is_gt).then_inc(G["greater"].sem, 1)
                dve.wait_ge(G["equal"].sem, G["equal"].at(i))
                nc.vector.tensor_tensor(equal[:], equal[:], lower[:].unsqueeze(1).to_broadcast(every), ALU.mult)\
                    .then_inc(G["lower"].sem, 1)
                dve.wait_ge(G["greater"].sem, G["greater"].at(i))
                dve.wait_ge(G["lower"].sem, G["lower"].at(i))
                nc.vector.tensor_tensor(equal[:], equal[:], greater[:], ALU.add).then_inc(G["above"].sem, 1)
                dve.wait_ge(G["above"].sem, G["above"].at(i))
                nc.vector.reduce_sum(rank[:], equal[:], AX.X).then_inc(G["rank"].sem, 1)
                dve.wait_ge(G["exp"].sem, G["exp"].at(i))
                nc.vector.reduce_sum(total[:], expl[:], AX.X).then_inc(G["total"].sem, 1)
                dve.wait_ge(G["rank"].sem, G["rank"].at(i))
                nc.vector.scalar_tensor_tensor(out=chosen[:], in0=rank[:], scalar=2.0, in1=expl[:],
                                               op0=ALU.is_lt, op1=ALU.mult).then_inc(G["chosen"].sem, 1)
                dve.wait_ge(G["total"].sem, G["total"].at(i))
                nc.vector.reciprocal(total[:], total[:]).then_inc(G["inv"].sem, 1)
                dve.wait_ge(G["inv"].sem, G["inv"].at(i))
                dve.wait_ge(G["chosen"].sem, G["chosen"].at(i))
                nc.vector.tensor_tensor(weight[:], chosen[:], total[:].unsqueeze(2).to_broadcast([R, 2 * NT, E]),
                                        ALU.mult).then_inc(G["weight"].sem, 1)
                dve.wait_ge(G["weight"].sem, G["weight"].at(i))
                for u in range(2):
                    n, B = 2 * i + u, banks[u]
                    dve.wait_ge(S["acc0"].sem, S["acc0"].at(n))
                    for m in range(M):
                        p, t = divmod(m, NT)
                        if m < EARLY:
                            dve.wait_ge(S["early"].sem, S["early"].at(n, m + 1))
                        else:
                            dve.wait_ge(S["me"].sem, S["me"].at(n, m + 1 - EARLY))
                        for j in range(2):
                            if m >= NT or j:
                                dve.wait_ge(S["acc"].sem, S["acc"].at(n, 2 * m + 1 if j else 2 * (m - NT) + 2))
                            nc.vector.scalar_tensor_tensor(out=acc[:, u, t], in0=B(2 + m % 2)[0:R, j * D:(j + 1) * D],
                                                           scalar=weight[:, u * NT + t, 2 * p + j:2 * p + j + 1],
                                                           in1=acc[:, u, t], op0=ALU.mult, op1=ALU.add)\
                                .then_inc(S["acc"].sem, 1)
                for u in range(2):
                    n = 2 * i + u
                    dve.wait_ge(S["acc"].sem, S["acc"].at(n))
                    ln_stats(nc, dve, acc[:, u], stats[:, u], mv[:, u], (S["bn2"].sem, S["bn2"].at(n)), S["mv2"])
                for u in range(2):
                    n = 2 * i + u
                    dve.wait_ge(S["rstd2"].sem, S["rstd2"].at(n))
                    ln_apply(nc, acc[:, u], acc[:, u], mv[:, u], rstd[:, u], S["accn"])
                for u in range(2):
                    n = 2 * i + u
                    dve.wait_ge(S["accn"].sem, S["accn"].at(n))
                    dve.wait_ge(S["out"].sem, S["out"].before(n))
                    nc.vector.tensor_tensor(accg[:, u], acc[:, u], everywhere("g2"), ALU.mult)\
                        .then_inc(S["accg"].sem, 1)
                for u in range(2):
                    n = 2 * i + u
                    dve.wait_ge(S["accg"].sem, S["accg"].at(n))
                    dve.wait_ge(S["hx"].sem, S["hx"].at(n))
                    nc.vector.tensor_tensor(h[:, u], h[:, u], accg[:, u], ALU.add).then_inc(S["out"].sem, 1)

        @block.tensor
        def _(pe):
            for k in ("cT", "y", "xT", "gl", "early", "me", "wT", "bias"):
                S[k].give(pe)
            pe.wait_ge(w_loaded, WEIGHTS)

            def experts(n, u, ms):
                B = banks[u]
                for m in ms:
                    p, t = divmod(m, NT)
                    if m >= 2:
                        pe.wait_ge(S["acc"].sem, S["acc"].at(n, 2 * (m - 2) + 2))
                    for k in range(CT):
                        last = nc.tensor.matmul(B(2 + m % 2)[0:R, :], xT[:, u, k, t * R:(t + 1) * R],
                                                we[:, k, 2 * p:2 * p + 2, :].rearrange("p e d -> p (e d)"),
                                                start=(k == 0), stop=(k == CT - 1))
                    last.then_inc(S["early" if m < EARLY else "me"].sem, 1)

            with pe.Fori(0, NB // 2) as i:
                for u in range(2):
                    n, B = 2 * i + u, banks[u]
                    pe.wait_ge(c_loaded[u], 16 * i + 16)
                    pe.wait_ge(S["acc"].sem, S["acc"].before(n))
                    transpose_tokens(nc, pe, c, cx[:, u], lambda k: B(2 + k)).then_inc(S["cT"].sem, 1)
                for u in range(2):
                    n, B = 2 * i + u, banks[u]
                    pe.wait_ge(S["cT_out"].sem, S["cT_out"].at(n))
                    pe.wait_ge(S["acc0"].sem, S["acc0"].before(n))
                    for t in range(NT):
                        for k in range(CT):
                            last = nc.tensor.matmul(B(t // 2)[0:R, (t % 2) * D:(t % 2 + 1) * D],
                                                    cT[:, u, k, t * R:(t + 1) * R], wo[:, k, :],
                                                    start=(k == 0), stop=(k == CT - 1))
                    last.then_inc(S["y"].sem, 1)
                for u in range(2):
                    n, B = 2 * i + u, banks[u]
                    pe.wait_ge(S["x4"].sem, S["x4"].at(n))
                    transpose_tokens(nc, pe, c, x[:, u], lambda k: B(2 + k)).then_inc(S["xT"].sem, 1)
                for u in range(2):
                    n, B = 2 * i + u, banks[u]
                    pe.wait_ge(S["xT_out"].sem, S["xT_out"].at(n))
                    for t in range(NT):
                        for k in range(CT):
                            last = nc.tensor.matmul(B(1)[0:R, D + t * E:D + (t + 1) * E],
                                                    xT[:, u, k, t * R:(t + 1) * R], wg[:, k, :],
                                                    start=(k == 0), stop=(k == CT - 1))
                    last.then_inc(S["gl"].sem, 1)
                for u in range(2):
                    experts(2 * i + u, u, range(EARLY))
                for u in range(2):
                    n, B = 2 * i + u, banks[u]
                    pe.wait_ge(G["weight"].sem, G["weight"].at(i))
                    for t in range(NT):
                        last = nc.tensor.transpose(B(1)[0:E, t * R:(t + 1) * R], weight[:, u * NT + t, :],
                                                   c["ident"][0:R, 0:R])
                    last.then_inc(S["wT"].sem, 1)
                for u in range(2):
                    n, B = 2 * i + u, banks[u]
                    pe.wait_ge(S["wT_out"].sem, S["wT_out"].at(n))
                    for t in range(NT):
                        last = nc.tensor.matmul(B(t // 2)[0:R, (t % 2) * D:(t % 2 + 1) * D],
                                                weightT[:, u, t * R:(t + 1) * R], bexp[:], start=True, stop=True)
                    last.then_inc(S["bias"].sem, 1)
                for u in range(2):
                    experts(2 * i + u, u, range(EARLY, M))


def program(nc, NB, patches, txt, rot, wtok, a_wq, a_wk, a_wv, a_wo, gate_w, up_w, down_w,
            wqkv, curv, proj, projb, f_wq, f_bq, f_wk, f_bk, f_wv, f_bv, f_wo, f_bo, g1, be1, g2, be2,
            wg, bg, we, bexp, out):
    def scratch(name, shape, dt=F32):
        return nc.dram_tensor("s_" + name, shape, dt, kind="Internal").ap()

    tokens = [NB, T, D]
    h1, h2, h3, x3, ctx1, ctx2 = (scratch(n, tokens) for n in ("h1", "h2", "h3", "x3", "ctx1", "ctx2"))
    x0 = scratch("x0", [NB, D, T])
    gate, up, gated, o = (scratch(n, [NB, 128, FT * T]) for n in ("gate", "up", "gated", "o"))
    parts1 = scratch("parts1", [NB, 2, H * HD1, PARTS, T], BF16)
    parts2 = scratch("parts2", [NB, 2, H * HD, PARTS, T], BF16)
    v1, v2 = (scratch(n, [NB, R, NT * H * VW]) for n in ("v1", "v2"))
    ctx = ExitStack()
    with ctx:
        ps = ctx.enter_context(nc.psum_tensor("ps", [128, 8, 512], F32))

        def run(stage, *args):
            with nc.cleanup_on_exit():
                stage(nc, *args)

        c = setup_constants(nc, ctx, rot)
        with ExitStack() as ffn:
            def sb(name, shape):
                return ffn.enter_context(nc.sbuf_tensor("k_" + name, shape, F32))

            gateT, upT, downT = sb("gateT", [128, CT, FF]), sb("upT", [128, CT, FF]), sb("downT", [128, FT, D])
            quantised = ("x", "gate", "up", "gated", "o")
            amax = {k: sb("amax_" + k, [128, 2]) for k in quantised}
            scale = {k: sb("scale_" + k, [128, 1]) for k in quantised}
            inv = {k: sb("inv_" + k, [128, 1]) for k in quantised}
            magic = sb("magic", [128, 1])
            with nc.Block() as block:
                @block.vector
                def _(dve):
                    nc.vector.memset(magic[:], MAGIC)
                    for k in quantised:
                        nc.vector.memset(amax[k][:], 0.0)

            def fix_scale(k):
                run(set_scale, "z_" + k, amax[k][:], scale[k][:], inv[k][:])

            run(quantise_weights, c, ps, gate_w, up_w, down_w, gateT, upT, downT)
            run(phase_a, c, ps, NB, patches, txt, wtok, a_wq, a_wk, a_wv, a_wo, h1, x0, amax["x"][0:R])
            fix_scale("x")
            run(phase_b, ps, NB, magic[:], x0, gateT, upT, scale["x"][:], inv["x"][:], gate, up,
                    amax["gate"], amax["up"])
            fix_scale("gate")
            fix_scale("up")
            run(phase_c, NB, magic[:], gate, scale["gate"][:], inv["gate"][:], gated, amax["gated"])
            fix_scale("gated")
            run(phase_d, NB, magic[:], gated, up, scale["gated"][:], inv["gated"][:], scale["up"][:], inv["up"][:],
                    o, amax["o"])
            fix_scale("o")
            run(phase_f1, c, ps, NB, magic[:], o, h1, downT, scale["o"][:], inv["o"][:], wqkv, curv, h2, parts1, v1)
        run(attention_core, c, ps, NB, "g", KINDS, True, HD1, parts1, v1, ctx1, curv)
        run(phase_g1, c, ps, NB, ctx1, h2, proj, projb, f_wq, f_wk, f_wv, f_bq, f_bk, f_bv, h3, x3, parts2, v2)
        run(attention_core, c, ps, NB, "e", [SDPA] * H, False, HD, parts2, v2, ctx2)
        run(phase_g3, c, ps, NB, ctx2, x3, h3, f_wo, f_bo, g1, be1, wg, bg, we, bexp, g2, be2, out)


def kernel(**inputs):
    import concourse.bacc as bacc
    from concourse.bass_utils import run_bass_kernel_spmd

    a = {k: np.asarray(v) for k, v in inputs.items()}
    NB = a["x"].shape[0]
    P = 16
    side = a["x"].shape[-1] // P
    patches = a["x"].reshape(NB, 3, side, P, side, P).transpose(0, 1, 3, 5, 2, 4).reshape(NB, 3 * P * P, side * side)
    frequencies = 1.0 / 10000.0 ** (np.arange(0, HD, 2, dtype=np.float32) / HD)
    angles = np.outer(np.arange(T, dtype=np.float32), frequencies).astype(np.float32)
    cos, sin = np.cos(angles), np.sin(angles)
    rot = np.stack([np.concatenate([cos, cos], 1), np.concatenate([sin, -sin], 1)]).astype(np.float32)

    def ffn(*names):
        return [a["L1_ffn_" + k] for k in names]

    arrays = [patches, a["txt"], rot, a["L0_tok_W"].T] + [a["L0_attn_W" + k] for k in "qkvo"]
    arrays += [a["L0_ffn_w_" + k] for k in ("gate", "up", "down")]
    arrays += [a["L1_attn_qkv_w"].T, a["L1_attn_curvature"].reshape(4), a["L1_attn_proj_w"].T, a["L1_attn_proj_b"]]
    arrays += ffn("Wq", "bq", "Wk", "bk", "Wv", "bv", "Wo", "bo", "g1", "be1", "g2", "be2", "Wg", "bg", "We", "bexp")
    nc = bacc.Bacc("TRN2", target_bir_lowering=False, num_devices=1)
    named, args = {}, []
    for i, x in enumerate(arrays):
        x = np.ascontiguousarray(x)
        named[f"in_{i}"] = x
        args.append(nc.dram_tensor(f"in_{i}", x.shape, mybir.dt.from_np(x.dtype), kind="ExternalInput").ap())
    args.append(nc.dram_tensor("out_0", [NB, T, D], F32, kind="ExternalOutput").ap())
    program(nc, NB, *args)
    return run_bass_kernel_spmd(nc, [named], core_ids=[0]).results[0]["out_0"]
```

```python
import numpy as np
import concourse.bass as bass
from concourse import mybir
from contextlib import ExitStack

F32 = mybir.dt.float32
BF16 = mybir.dt.bfloat16
ALU = mybir.AluOpType
ACT = mybir.ActivationFunctionType
AX = mybir.AxisListType

D = 256
CT = D // 128
PATCHES, TEXT = 196, 77
T = PATCHES + TEXT
R = 91
NT = T // R
P_LAST = PATCHES - (NT - 1) * R
KP = 768 // 128
FF = 768
FT = FF // 128
QBLOCK = 32
H, HD = 16, 16
EXPERTS = 8
EPS = 1e-5
NEG = -1e30
MAGIC = 12582912.0
QMAX = 32767.0


class Signal:

    def __init__(self, nc, name, per, skew):
        self.sem, self.per, self.start = nc.alloc_semaphore(name), per, 2 * per + skew

    def give(self, engine):
        engine.sem_inc(self.sem, self.start)

    def at(self, n, count=None):
        done = self.start + (self.per if count is None else count)
        if isinstance(n, tuple):
            return n[0] * (2 * self.per) + (n[1] * self.per + done)
        return n * self.per + done

    def before(self, n):
        return self.at(n, -self.per)


def signals(ctx, nc, prefix, **pers):
    return {k: Signal(nc, f"{prefix}_{k}", per, skew) for skew, (k, per) in enumerate(pers.items())}


def setup_constants(nc, ctx, rot_dram):
    c = {}
    for name, shape, dt in (("ident", [128, 128], F32), ("identb", [128, 128], BF16),
                            ("mask_qk", [R, R], BF16), ("mask_kq", [R, R], BF16),
                            ("minus_half", [R, 64], F32), ("eps", [R, NT], F32),
                            ("cos", [R, NT, HD], F32), ("sin", [R, NT, HD], F32)):
        c[name] = ctx.enter_context(nc.sbuf_tensor("c_" + name, shape, dt))
    filled = nc.alloc_semaphore("const_filled")
    loaded = nc.alloc_semaphore("const_loaded")
    with nc.Block() as block:
        @block.gpsimd
        def _(pool):
            fills = (("ident", 0.0), ("identb", 0.0), ("mask_qk", 0.0), ("mask_kq", 0.0),
                     ("minus_half", -0.5), ("eps", EPS))
            for name, value in fills:
                nc.gpsimd.memset(c[name][:], value).then_inc(filled, 1)
            pool.wait_ge(filled, len(fills))
            for name in ("ident", "identb"):
                nc.gpsimd.affine_select(out=c[name][:], in_=c[name][:], compare_op=ALU.not_equal,
                                        fill=1.0, base=0, pattern=[[-1, 128]], channel_multiplier=1)
            nc.gpsimd.affine_select(out=c["mask_qk"][:], in_=c["mask_qk"][:], compare_op=ALU.is_ge,
                                    fill=NEG, base=0, pattern=[[-1, R]], channel_multiplier=1)
            nc.gpsimd.affine_select(out=c["mask_kq"][:], in_=c["mask_kq"][:], compare_op=ALU.is_ge,
                                    fill=NEG, base=0, pattern=[[1, R]], channel_multiplier=-1)

        @block.sync
        def _(sp):
            for k, name in enumerate(("cos", "sin")):
                sp.dma_start(c[name][:], rot_dram[k].rearrange("(t p) d -> p t d", p=R)).then_inc(loaded, 16)
            sp.wait_ge(loaded, 32)
    return c


def ln_stats(nc, dve, x, stats, mv, bn, s_mv):
    for t in range(NT):
        nc.vector.bn_stats(stats[:, t, :], x[:, t, :]).then_inc(bn[0], 1)
    dve.wait_ge(bn[0], bn[1] - 1)
    dve.sem_inc(bn[0], 1)
    for t in range(NT):
        last = nc.vector.bn_aggr(mv[:, t, :], stats[:, t, :])
    last.then_inc(s_mv.sem, 1)


def ln_apply(nc, out, x, mv, rstd, done):
    for t in range(NT):
        nc.vector.tensor_scalar(out[:, t, :], x[:, t, :], mv[:, t, 0:1], rstd[:, t:t + 1],
                                ALU.subtract, ALU.mult).then_inc(done.sem, 1)


def ln_rstd(nc, pool, c, mv, var_eps, rstd, s_mv, s_eps, s_rstd, n):
    pool.wait_ge(s_mv.sem, s_mv.at(n))
    pool.wait_ge(s_rstd.sem, s_rstd.before(n))
    nc.gpsimd.tensor_tensor(var_eps[:], mv[:, :, 1], c["eps"][:, 0:NT], ALU.add).then_inc(s_eps.sem, 1)
    pool.wait_ge(s_eps.sem, s_eps.at(n))
    nc.gpsimd.tensor_tensor(rstd[:], var_eps[:], c["minus_half"][:, 0:NT], ALU.pow).then_inc(s_rstd.sem, 1)


def transpose_tokens(nc, pe, c, x, banks):
    for ct in range(CT):
        for t in range(NT):
            last = nc.tensor.transpose(banks(ct)[:, t * R:(t + 1) * R],
                                       x[:, t, ct * 128:(ct + 1) * 128], c["ident"][0:R, 0:R])
    return last


def phase_a(nc, c, ps, NB, patches_dram, txt_dram, wtok_dram, wq_dram, wk_dram, wv_dram, wo_dram,
            h1_dram, x0_dram, amax_x):
    ctx = ExitStack()
    with ctx:
        def sb(name, shape, dt=F32):
            return ctx.enter_context(nc.sbuf_tensor("a_" + name, shape, dt))

        def sem(name):
            return nc.alloc_semaphore("a_" + name)

        wtok = sb("wtok", [128, KP, D])
        wq, wk, wv, wo = (sb(n, [128, CT, D]) for n in ("wq", "wk", "wv", "wo"))
        patches = sb("patches", [128, 2, KP, PATCHES])
        h = sb("h", [R, 2, NT, D])
        h1 = sb("h1", [R, 2, NT, D])
        stats, stats1 = (sb(k, [R, 2, NT, 6]) for k in ("stats", "stats1"))
        mv, mv1 = (sb(k, [R, 2, NT, 2]) for k in ("mv", "mv1"))
        var_eps, var_eps1 = (sb(k, [R, 2, NT]) for k in ("var_eps", "var_eps1"))
        rstd, rstd1 = (sb(k, [R, 2, NT]) for k in ("rstd", "rstd1"))
        xn, x0 = (sb(k, [R, 2, NT, D]) for k in ("xn", "x0"))
        xT = sb("xT", [128, 2, CT, T])
        qT = sb("qT", [128, 2, CT, T])
        kT = sb("kT", [128, 2, CT, T])
        v = sb("v", [R, 2, NT, D])
        mx = sb("mx", [R, 2, NT])
        nb = sb("nb", [R, 2, NT])
        prob = sb("prob", [R, 2, NT, T])
        den = sb("den", [R, 2, NT])
        rden = sb("rden", [R, 2, NT])
        probT = sb("probT", [R, 2, 2, T])
        aT = sb("aT", [128, 2, CT, T])
        x0T = sb("x0T", [128, 2, CT, T])
        amax_new = sb("amax_new", [R, 2, 1])

        w_loaded = sem("w_loaded")
        patches_loaded = [sem(f"patches_loaded{u}") for u in range(2)]
        txt_loaded = [sem(f"txt_loaded{u}") for u in range(2)]
        h1_stored = [sem(f"h1_stored{u}") for u in range(2)]
        x0_stored = [sem(f"x0_stored{u}") for u in range(2)]
        amax_step, passed = sem("amax_step"), sem("passed")
        S = signals(ctx, nc, "a", tok=2, tok_out=2, bn=NT + 1, mv=1, eps=1, rstd=1, xn=NT, xT=1, xT_out=1,
                    qk=CT, qk_out=2, v=1, v_out=1, s=NT, mx=NT, nb=1, p=NT, pT=1, pT_out=1, a=1,
                    a_out=1, rden=1, y=1, h1=1, bn1=NT + 1, mv1=1, eps1=1, rstd1=1, x0=NT, x0T=1, x0T_out=1,
                    amr=1, amax=1)
        causal = {0: (5, 182), 1: (5, 0), 2: (4, 0)}
        scale = float(D) ** -0.5

        block = ctx.enter_context(nc.Block())

        @block.sync
        def _(sp):
            def load_patches(n, u):
                sp.dma_start(patches[:, u], patches_dram[batch_of(n)].rearrange("(k p) n -> p k n", p=128))\
                    .then_inc(patches_loaded[u], 16)

            def load_text(n, u):
                sp.dma_start(h[P_LAST:R, u, NT - 1, :], txt_dram[batch_of(n)]).then_inc(txt_loaded[u], 16)

            def next_patches(n, u, i):
                if following(n, NB):
                    sp.wait_ge(S["tok"].sem, S["tok"].at(n))
                    sp.sem_inc(passed, 1)
                    load_patches((n[0], n[1] + 2), u)

            def store_h1(n, u, i):
                sp.wait_ge(S["h1"].sem, S["h1"].at(n))
                sp.sem_inc(passed, 1)
                sp.dma_start(h1_dram[batch_of(n)].rearrange("(t p) d -> p t d", p=R), h1[:, u])\
                    .then_inc(h1_stored[u], 16)
                if following(n, NB):
                    load_text((n[0], n[1] + 2), u)

            def store_x0(n, u, i):
                sp.wait_ge(S["x0T_out"].sem, S["x0T_out"].at(n))
                sp.sem_inc(passed, 1)
                sp.dma_start(x0_dram[batch_of(n)].rearrange("(c p) t -> p c t", p=128), x0T[:, u])\
                    .then_inc(x0_stored[u], 16)

            sp.dma_start(wtok[:], wtok_dram.rearrange("(k p) n -> p k n", p=128)).then_inc(w_loaded, 16)
            for u in range(2):
                load_patches((0, u), u)
                load_text((0, u), u)
            for w, dram in ((wq, wq_dram), (wk, wk_dram), (wv, wv_dram), (wo, wo_dram)):
                sp.dma_start(w[:], dram.rearrange("(k p) n -> p k n", p=128)).then_inc(w_loaded, 16)
            pipeline(sp, NB, ((store_h1, -1), (next_patches, 1), (store_x0, -1)))
            for u in range(2):
                sp.wait_ge(h1_stored[u], 16 * (NB // 2))
                sp.wait_ge(x0_stored[u], 16 * (NB // 2))

        @block.gpsimd
        def _(pool):
            for k in ("eps", "rstd", "eps1", "rstd1"):
                S[k].give(pool)

            def deviation_h(n, u, i):
                ln_rstd(nc, pool, c, mv[:, u], var_eps[:, u], rstd[:, u], S["mv"], S["eps"], S["rstd"], n)

            def deviation_h1(n, u, i):
                ln_rstd(nc, pool, c, mv1[:, u], var_eps1[:, u], rstd1[:, u], S["mv1"], S["eps1"], S["rstd1"], n)

            pipeline(pool, NB, ((deviation_h1, -1), (deviation_h, 1)))

        @block.scalar
        def _(act):
            for k in ("tok_out", "xT_out", "v_out", "p", "a_out", "x0T_out"):
                S[k].give(act)

            def copy_tok(n, u, i):
                act.wait_ge(S["h1"].sem, S["h1"].before(n))
                act.wait_ge(S["tok"].sem, S["tok"].at(n, 1))
                nc.scalar.copy(h[:, u, 0:2, :], ps[0:R, 0, :].rearrange("p (t d) -> p t d", t=2))\
                    .then_inc(S["tok_out"].sem, 1)
                act.wait_ge(S["tok"].sem, S["tok"].at(n))
                nc.scalar.copy(h[0:P_LAST, u, 2, :], ps[0:P_LAST, 1, 0:D]).then_inc(S["tok_out"].sem, 1)

            def copy_x(n, u, i):
                act.wait_ge(S["xT"].sem, S["xT"].at(n))
                act.wait_ge(S["v"].sem, S["v"].before(n))
                nc.scalar.copy(xT[:, u], ps[:, 2:4, 0:T]).then_inc(S["xT_out"].sem, 1)

            def copy_v(n, u, i):
                act.wait_ge(S["v"].sem, S["v"].at(n))
                act.wait_ge(S["a"].sem, S["a"].before(n))
                nc.scalar.copy(v[:, u, 0:2, :], ps[0:R, 2, :].rearrange("p (t d) -> p t d", t=2))
                nc.scalar.copy(v[:, u, 2, :], ps[0:R, 3, 0:D]).then_inc(S["v_out"].sem, 1)

            def exponentials(n, u, i):
                act.wait_ge(S["nb"].sem, S["nb"].at(n))
                act.wait_ge(S["pT"].sem, S["pT"].before(n))
                act.wait_ge(S["rden"].sem, S["rden"].before(n))
                for t in range(NT):
                    bank, col = causal[t]
                    w = (t + 1) * R
                    nc.scalar.activation(prob[:, u, t, 0:w], ps[0:R, bank, col:col + w], ACT.Exp,
                                         bias=nb[:, u, t:t + 1], scale=scale,
                                         accum_out=den[:, u, t:t + 1]).then_inc(S["p"].sem, 1)

            def copy_a(n, u, i):
                act.wait_ge(S["a"].sem, S["a"].at(n))
                act.wait_ge(S["y"].sem, S["y"].before(n))
                nc.scalar.copy(aT[:, u], ps[:, 2:4, 0:T]).then_inc(S["a_out"].sem, 1)

            def copy_x0(n, u, i):
                act.wait_ge(S["x0T"].sem, S["x0T"].at(n))
                act.wait_ge(x0_stored[u], 16 * i)
                nc.scalar.copy(x0T[:, u], ps[:, 4:6, 0:T]).then_inc(S["x0T_out"].sem, 1)

            pipeline(act, NB, ((copy_x, 0), (copy_v, 0), (exponentials, 0), (copy_tok, 1), (copy_x0, -1),
                               (copy_a, 0)))

        @block.vector
        def _(dve):
            for k in ("bn", "mv", "xn", "qk_out", "mx", "nb", "pT_out", "rden", "h1", "bn1", "mv1", "x0",
                      "amr", "amax"):
                S[k].give(dve)
            nc.vector.memset(amax_x[:], 0.0).then_inc(amax_step, 1)
            dve.wait_ge(amax_step, 1)

            def statistics(n, u, i):
                dve.wait_ge(S["tok_out"].sem, S["tok_out"].at(n))
                dve.wait_ge(txt_loaded[u], 16 * (i + 1))
                dve.wait_ge(S["xn"].sem, S["xn"].before(n))
                ln_stats(nc, dve, h[:, u], stats[:, u], mv[:, u], (S["bn"].sem, S["bn"].at(n)), S["mv"])

            def normalise_h(n, u, i):
                dve.wait_ge(S["rstd"].sem, S["rstd"].at(n))
                dve.wait_ge(S["xT"].sem, S["xT"].before(n))
                ln_apply(nc, xn[:, u], h[:, u], mv[:, u], rstd[:, u], S["xn"])

            def copy_qk(n, u, i):
                dve.wait_ge(S["s"].sem, S["s"].before(n))
                for j, to in enumerate((qT, kT)):
                    dve.wait_ge(S["qk"].sem, S["qk"].at(n, j + 1))
                    nc.vector.tensor_copy(to[:, u], ps[:, 4 + 2 * j:6 + 2 * j, 0:T]).then_inc(S["qk_out"].sem, 1)

            def maxima(n, u, i):
                for t in range(NT):
                    dve.wait_ge(S["s"].sem, S["s"].at(n, max(t + 1, 2)))
                    bank, col = causal[t]
                    nc.vector.reduce_max(mx[:, u, t:t + 1], ps[0:R, bank, col:col + (t + 1) * R], AX.X)\
                        .then_inc(S["mx"].sem, 1)
                dve.wait_ge(S["mx"].sem, S["mx"].at(n))
                dve.wait_ge(S["p"].sem, S["p"].before(n))
                nc.vector.tensor_scalar(nb[:, u], mx[:, u], -scale, None, ALU.mult).then_inc(S["nb"].sem, 1)

            def copy_p(n, u, i):
                dve.wait_ge(S["pT"].sem, S["pT"].at(n))
                dve.wait_ge(S["a"].sem, S["a"].before(n))
                nc.vector.tensor_copy(probT[:, u], ps[0:R, 6:8, 0:T]).then_inc(S["pT_out"].sem, 1)
                dve.wait_ge(S["p"].sem, S["p"].at(n))
                dve.wait_ge(S["h1"].sem, S["h1"].before(n))
                nc.vector.reciprocal(rden[:, u], den[:, u]).then_inc(S["rden"].sem, 1)

            def residual(n, u, i):
                dve.wait_ge(S["y"].sem, S["y"].at(n))
                dve.wait_ge(S["rden"].sem, S["rden"].at(n))
                dve.wait_ge(S["x0"].sem, S["x0"].before(n))
                dve.wait_ge(h1_stored[u], 16 * i)
                for t in range(NT):
                    y = ps[0:R, 6 + t // 2, (t % 2) * D:(t % 2 + 1) * D]
                    last = nc.vector.scalar_tensor_tensor(out=h1[:, u, t, :], in0=y, scalar=rden[:, u, t:t + 1],
                                                          in1=h[:, u, t, :], op0=ALU.mult, op1=ALU.add)
                last.then_inc(S["h1"].sem, 1)
                dve.wait_ge(S["h1"].sem, S["h1"].at(n))
                ln_stats(nc, dve, h1[:, u], stats1[:, u], mv1[:, u], (S["bn1"].sem, S["bn1"].at(n)), S["mv1"])

            def normalise_h1(n, u, i):
                dve.wait_ge(S["rstd1"].sem, S["rstd1"].at(n))
                dve.wait_ge(S["x0T"].sem, S["x0T"].before(n))
                dve.wait_ge(S["amr"].sem, S["amr"].before(n))
                ln_apply(nc, x0[:, u], h1[:, u], mv1[:, u], rstd1[:, u], S["x0"])

            def maximum(n, u, i):
                dve.wait_ge(S["x0"].sem, S["x0"].at(n))
                dve.wait_ge(S["amax"].sem, S["amax"].before(n))
                nc.vector.tensor_reduce(amax_new[:, u], x0[:, u].rearrange("p t d -> p (t d)"), AX.X, ALU.max,
                                        apply_absolute_value=True).then_inc(S["amr"].sem, 1)
                dve.wait_ge(S["amr"].sem, S["amr"].at(n))
                nc.vector.tensor_tensor(amax_x[:, u:u + 1], amax_x[:, u:u + 1], amax_new[:, u], ALU.max)\
                    .then_inc(S["amax"].sem, 1)

            pipeline(dve, NB, ((residual, -1), (copy_qk, 0), (normalise_h1, -1), (maxima, 0), (maximum, -1),
                               (copy_p, 0), (statistics, 1), (normalise_h, 1)))

        @block.tensor
        def _(pe):
            for k in ("tok", "xT", "qk", "v", "s", "pT", "a", "y", "x0T"):
                S[k].give(pe)
            pe.wait_ge(w_loaded, 16 * 5)

            def patch_tile(n, u, t):
                m = R if t < NT - 1 else P_LAST
                for k in range(KP):
                    last = nc.tensor.matmul(ps[0:m, t // 2, (t % 2) * D:(t % 2 + 1) * D],
                                            patches[:, u, k, t * R:t * R + m], wtok[:, k, :],
                                            start=(k == 0), stop=(k == KP - 1))
                return last

            def patches_first(n, u, i):
                pe.wait_ge(patches_loaded[u], 16 * (i + 1))
                pe.wait_ge(S["tok_out"].sem, S["tok_out"].at((n[0], n[1] - 1)))
                patch_tile(n, u, 0)

            def patches_rest(n, u, i):
                for t in range(1, NT):
                    patch_tile(n, u, t).then_inc(S["tok"].sem, 1)

            def turn_x(n, u, i):
                pe.wait_ge(S["xn"].sem, S["xn"].at(n))
                pe.wait_ge(S["a_out"].sem, S["a_out"].at((n[0], n[1] - 1)))
                transpose_tokens(nc, pe, c, xn[:, u], lambda k: ps[:, 2 + k, :]).then_inc(S["xT"].sem, 1)

            def queries_and_keys(n, u, i):
                pe.wait_ge(S["xT_out"].sem, S["xT_out"].at(n))
                pe.wait_ge(S["x0T_out"].sem, S["x0T_out"].at((n[0], n[1] - 2)))
                for j, w in enumerate((wq, wk)):
                    if j:
                        pe.wait_ge(S["h1"].sem, S["h1"].at((n[0], n[1] - 1)))
                    for m in range(CT):
                        for k in range(CT):
                            last = nc.tensor.matmul(ps[:, 4 + 2 * j + m, 0:T], w[:, k, m * 128:(m + 1) * 128],
                                                    xT[:, u, k, :], start=(k == 0), stop=(k == CT - 1))
                    last.then_inc(S["qk"].sem, 1)

            def values(n, u, i):
                for t in range(NT):
                    for k in range(CT):
                        last = nc.tensor.matmul(ps[0:R, 2 + t // 2, (t % 2) * D:(t % 2 + 1) * D],
                                                xT[:, u, k, t * R:(t + 1) * R], wv[:, k, :],
                                                start=(k == 0), stop=(k == CT - 1))
                last.then_inc(S["v"].sem, 1)

            def scores(n, u, i):
                pe.wait_ge(S["qk_out"].sem, S["qk_out"].at(n))
                for t in range(NT):
                    bank, col = causal[t]
                    w = (t + 1) * R
                    for k in range(CT):
                        last = nc.tensor.matmul(ps[0:R, bank, col:col + w], qT[:, u, k, t * R:(t + 1) * R],
                                                kT[:, u, k, 0:w], start=(k == 0), stop=(k == CT - 1))
                        if k == 0:
                            nc.tensor.matmul(ps[0:R, bank, col + t * R:col + w], c["identb"][0:R, 0:R],
                                             c["mask_qk"][:], start=False, stop=False, skip_group_check=True)
                    last.then_inc(S["s"].sem, 1)

            def turn_p(n, u, i):
                pe.wait_ge(S["p"].sem, S["p"].at(n))
                for k in range(NT):
                    for t in range(k, NT):
                        out = ps[0:R, 6, t * R:(t + 1) * R] if k == 0 else \
                            ps[0:R, 7, ((k - 1) * 2 + t - k) * R:((k - 1) * 2 + t - k + 1) * R]
                        last = nc.tensor.transpose(out, prob[:, u, t, k * R:(k + 1) * R], c["ident"][0:R, 0:R])
                last.then_inc(S["pT"].sem, 1)

            def turn_x0(n, u, i):
                pe.wait_ge(S["x0"].sem, S["x0"].at(n))
                transpose_tokens(nc, pe, c, x0[:, u], lambda k: ps[:, 4 + k, :]).then_inc(S["x0T"].sem, 1)

            def attend(n, u, i):
                pe.wait_ge(S["v_out"].sem, S["v_out"].at(n))
                pe.wait_ge(S["pT_out"].sem, S["pT_out"].at(n))
                for m in range(CT):
                    for k in range(NT):
                        moving = probT[:, u, 0, :] if k == 0 else \
                            probT[:, u, 1, (k - 1) * 2 * R:(k - 1) * 2 * R + (NT - k) * R]
                        last = nc.tensor.matmul(ps[:, 2 + m, k * R:T], v[:, u, k, m * 128:(m + 1) * 128],
                                                moving, start=(k == 0), stop=(k == NT - 1))
                last.then_inc(S["a"].sem, 1)

            def project(n, u, i):
                pe.wait_ge(S["a_out"].sem, S["a_out"].at(n))
                for t in range(NT):
                    for k in range(CT):
                        last = nc.tensor.matmul(ps[0:R, 6 + t // 2, (t % 2) * D:(t % 2 + 1) * D],
                                                aT[:, u, k, t * R:(t + 1) * R], wo[:, k, :],
                                                start=(k == 0), stop=(k == CT - 1))
                last.then_inc(S["y"].sem, 1)

            pipeline(pe, NB, ((turn_x, 0), (patches_first, 1), (queries_and_keys, 0), (values, 0), (scores, 0),
                              (patches_rest, 1), (turn_p, 0), (turn_x0, -1), (attend, 0), (project, 0)))


def quantise_weights(nc, c, ps, gate_dram, up_dram, down_dram, gateT, upT, downT):
    ctx = ExitStack()
    NBLK = FT * D // QBLOCK
    srcs = ((gate_dram, gateT, FT, CT), (up_dram, upT, FT, CT), (down_dram, downT, CT, FT))
    with ctx:
        w = ctx.enter_context(nc.sbuf_tensor("q_w", [128, 3, NBLK, QBLOCK], F32))
        step = ctx.enter_context(nc.sbuf_tensor("q_step", [128, 3, NBLK], F32))
        inv = ctx.enter_context(nc.sbuf_tensor("q_inv", [128, 3, NBLK], F32))
        loaded = [nc.alloc_semaphore(f"q_loaded{k}") for k in range(3)]
        chain = nc.alloc_semaphore("q_chain")
        done = nc.alloc_semaphore("q_done")
        turned = nc.alloc_semaphore("q_turned")
        out = nc.alloc_semaphore("q_out")
        block = ctx.enter_context(nc.Block())

        @block.sync
        def _(sp):
            for k, (dram, _, ot, _) in enumerate(srcs):
                sp.dma_start(w[:, k].rearrange("p b q -> p (b q)").rearrange("p (o i) -> p o i", o=ot),
                             dram.rearrange("(o p) i -> p o i", p=128)).then_inc(loaded[k], 16)

        @block.vector
        def _(dve):
            for k in range(3):
                def wide(a):
                    return a[:, k, :].unsqueeze(2).to_broadcast([128, NBLK, QBLOCK])

                dve.wait_ge(loaded[k], 16)
                nc.vector.tensor_reduce(step[:, k], w[:, k], AX.X, ALU.max, apply_absolute_value=True)\
                    .then_inc(chain, 1)
                dve.wait_ge(chain, 6 * k + 1)
                nc.vector.tensor_scalar(step[:, k], step[:, k], 1.0 / 7.0, 1e-12, ALU.mult, ALU.max)\
                    .then_inc(chain, 1)
                dve.wait_ge(chain, 6 * k + 2)
                nc.vector.reciprocal(inv[:, k], step[:, k]).then_inc(chain, 1)
                dve.wait_ge(chain, 6 * k + 3)
                nc.vector.tensor_tensor(w[:, k], w[:, k], wide(inv), ALU.mult).then_inc(chain, 1)
                dve.wait_ge(chain, 6 * k + 4)
                nc.vector.tensor_scalar(w[:, k], w[:, k], MAGIC, MAGIC, ALU.add, ALU.subtract).then_inc(chain, 1)
                dve.wait_ge(chain, 6 * k + 5)
                nc.vector.tensor_tensor(w[:, k], w[:, k], wide(step), ALU.mult).then_inc(chain, 1)
                dve.wait_ge(chain, 6 * k + 6)
                dve.sem_inc(done, 1)

        @block.tensor
        def _(pe):
            turn = 0
            for k, (_, dst, ot, it) in enumerate(srcs):
                pe.wait_ge(done, k + 1)
                src = w[:, k].rearrange("p b q -> p (b q)")
                for i in range(it):
                    for o0 in range(0, ot, 2):
                        if turn >= 8:
                            pe.wait_ge(out, turn - 7)
                        for o in (o0, o0 + 1):
                            last = nc.tensor.transpose(ps[:, turn % 8, (o - o0) * 128:(o - o0 + 1) * 128],
                                                       src[:, (o * it + i) * 128:(o * it + i + 1) * 128],
                                                       c["ident"][:])
                        last.then_inc(turned, 1)
                        turn += 1

        @block.scalar
        def _(act):
            turn = 0
            for k, (_, dst, ot, it) in enumerate(srcs):
                for i in range(it):
                    for o0 in range(0, ot, 2):
                        act.wait_ge(turned, turn + 1)
                        nc.scalar.copy(dst[:, i, o0 * 128:(o0 + 2) * 128], ps[:, turn % 8, 0:256])\
                            .then_inc(out, 1)
                        turn += 1


def set_scale(nc, name, amax, scale, inv):
    ctx = ExitStack()
    with ctx:
        k = amax.shape[1]
        every = ctx.enter_context(nc.sbuf_tensor(name + "_every", [128, k], F32))
        reduced = nc.alloc_semaphore(name + "_reduced")
        chain = nc.alloc_semaphore(name + "_chain")
        block = ctx.enter_context(nc.Block())

        @block.gpsimd
        def _(pool):
            nc.gpsimd.partition_all_reduce(every[:], amax, 128, bass.bass_isa.ReduceOp.max).then_inc(reduced, 1)

        @block.vector
        def _(dve):
            dve.wait_ge(reduced, 1)
            nc.vector.reduce_max(scale, every[:], AX.X).then_inc(chain, 1)
            dve.wait_ge(chain, 1)
            nc.vector.tensor_scalar(scale, scale, 1.0 / QMAX, 1e-12, ALU.mult, ALU.max).then_inc(chain, 1)
            dve.wait_ge(chain, 2)
            nc.vector.reciprocal(inv, scale).then_inc(chain, 1)
            dve.wait_ge(chain, 3)


def running_max(nc, dve, new, total, x, s_new, s_total, n):
    dve.wait_ge(s_total.sem, s_total.before(n))
    nc.vector.tensor_reduce(new, x, AX.X, ALU.max, apply_absolute_value=True).then_inc(s_new.sem, 1)
    dve.wait_ge(s_new.sem, s_new.at(n))
    nc.vector.tensor_tensor(total, total, new, ALU.max).then_inc(s_total.sem, 1)


def phase_b(nc, ps, NB, magic, x0_dram, gateT, upT, scale, inv, gate_dram, up_dram, amax_gate, amax_up):
    ctx = ExitStack()
    with ctx:
        def sb(name, shape, dt=F32):
            return ctx.enter_context(nc.sbuf_tensor("b_" + name, shape, dt))

        def sem(name):
            return nc.alloc_semaphore("b_" + name)

        x = sb("x", [128, 2, CT, T])
        xm = sb("xm", [128, 2, CT, T])
        gu = sb("gu", [128, 2, 2, FT, T])
        new = sb("new", [128, 2, 2])
        x_loaded = [sem(f"x_loaded{u}") for u in range(2)]
        gu_stored = [sem(f"gu_stored{u}") for u in range(2)]
        S = signals(ctx, nc, "b", xm=1, xq=1, mm=2 * FT, out=2 * FT, newg=1, maxg=1, newu=1, maxu=1)
        block = ctx.enter_context(nc.Block())

        @block.sync
        def _(sp):
            def load(n, u):
                sp.dma_start(x[:, u], x0_dram[n].rearrange("(c p) t -> p c t", p=128)).then_inc(x_loaded[u], 16)

            def pair(i, more):
                for u in range(2):
                    n = 2 * i + u
                    if more:
                        sp.wait_ge(S["mm"].sem, S["mm"].at(n))
                        load(n + 2, u)
                    for j, dram in enumerate((gate_dram, up_dram)):
                        sp.wait_ge(S["out"].sem, S["out"].at(n, (j + 1) * FT))
                        sp.dma_start(dram[n], gu[:, u, j].rearrange("p f t -> p (f t)")).then_inc(gu_stored[u], 16)

            for u in range(2):
                load(u, u)
            with sp.Fori(0, NB // 2 - 1) as i:
                pair(i, True)
            pair(NB // 2 - 1, False)
            for u in range(2):
                sp.wait_ge(gu_stored[u], 32 * (NB // 2))

        @block.scalar
        def _(act):
            for k in ("xm", "out"):
                S[k].give(act)
            with act.Fori(0, NB // 2) as i:
                for u in range(2):
                    n = 2 * i + u
                    act.wait_ge(x_loaded[u], 16 * i + 16)
                    act.wait_ge(S["xq"].sem, S["xq"].before(n))
                    nc.scalar.activation(xm[:, u], x[:, u], ACT.Identity, scale=inv, bias=magic)\
                        .then_inc(S["xm"].sem, 1)
                for u in range(2):
                    n = 2 * i + u
                    act.wait_ge(gu_stored[u], 32 * i)
                    act.wait_ge(S["maxu"].sem, S["maxu"].before(n))
                    for m in range(2 * FT):
                        act.wait_ge(S["mm"].sem, S["mm"].at(n, m + 1))
                        nc.scalar.copy(gu[:, u, m // FT, m % FT, :], ps[:, 4 * u + m % 4, 0:T])\
                            .then_inc(S["out"].sem, 1)

        @block.vector
        def _(dve):
            for k in ("xq", "newg", "maxg", "newu", "maxu"):
                S[k].give(dve)
            with dve.Fori(0, NB // 2) as i:
                for u in range(2):
                    n = 2 * i + u
                    dve.wait_ge(S["xm"].sem, S["xm"].at(n))
                    dve.wait_ge(S["mm"].sem, S["mm"].before(n))
                    nc.vector.tensor_scalar(x[:, u], xm[:, u], MAGIC, scale, ALU.subtract, ALU.mult)\
                        .then_inc(S["xq"].sem, 1)
                for u in range(2):
                    n = 2 * i + u
                    for j, (k, amax) in enumerate((("g", amax_gate), ("u", amax_up))):
                        dve.wait_ge(S["out"].sem, S["out"].at(n, (j + 1) * FT))
                        running_max(nc, dve, new[:, u, j:j + 1], amax[:, u:u + 1],
                                    gu[:, u, j].rearrange("p f t -> p (f t)"), S["new" + k], S["max" + k], n)

        @block.tensor
        def _(pe):
            S["mm"].give(pe)
            with pe.Fori(0, NB // 2) as i:
                for u in range(2):
                    n = 2 * i + u
                    pe.wait_ge(S["xq"].sem, S["xq"].at(n))
                    for m in range(2 * FT):
                        if m < 4:
                            pe.wait_ge(S["out"].sem, S["out"].before(n))
                        else:
                            pe.wait_ge(S["out"].sem, S["out"].at(n, m - 3))
                        w = (gateT, upT)[m // FT]
                        for k in range(CT):
                            last = nc.tensor.matmul(ps[:, 4 * u + m % 4, 0:T],
                                                    w[:, k, (m % FT) * 128:(m % FT + 1) * 128],
                                                    x[:, u, k, :], start=(k == 0), stop=(k == CT - 1))
                        last.then_inc(S["mm"].sem, 1)


def phase_c(nc, NB, magic, gate_dram, scale, inv, g2_dram, amax_g2):
    ctx = ExitStack()
    N = FT * T
    with ctx:
        def sb(name):
            return ctx.enter_context(nc.sbuf_tensor("c_" + name, [128, 2, N], F32))

        def sem(name):
            return nc.alloc_semaphore("c_" + name)

        g, gm, gq, sg, sm, g2 = (sb(n) for n in ("g", "gm", "gq", "sg", "sm", "g2"))
        new = ctx.enter_context(nc.sbuf_tensor("c_new", [128, 2], F32))
        loaded = [sem(f"loaded{u}") for u in range(2)]
        stored = [sem(f"stored{u}") for u in range(2)]
        passed = sem("passed")
        S = signals(ctx, nc, "c", gm=1, gq=1, sg=1, sm=1, sr=1, g2=1, new=1, max=1)
        block = ctx.enter_context(nc.Block())

        @block.sync
        def _(sp):
            def load(n, u):
                sp.dma_start(g[:, u], gate_dram[batch_of(n)]).then_inc(loaded[u], 16)

            def next_gate(n, u, i):
                if following(n, NB):
                    sp.wait_ge(S["gm"].sem, S["gm"].at(n))
                    sp.sem_inc(passed, 1)
                    load((n[0], n[1] + 2), u)

            def store(n, u, i):
                sp.wait_ge(S["g2"].sem, S["g2"].at(n))
                sp.sem_inc(passed, 1)
                sp.dma_start(g2_dram[batch_of(n)], g2[:, u]).then_inc(stored[u], 16)

            for u in range(2):
                load((0, u), u)
            pipeline(sp, NB, ((next_gate, 2), (store, 0)))
            for u in range(2):
                sp.wait_ge(stored[u], 16 * (NB // 2))

        @block.scalar
        def _(act):
            for k in ("gm", "sg", "sm"):
                S[k].give(act)

            def divide(n, u, i):
                act.wait_ge(loaded[u], 16 * (i + 1))
                act.wait_ge(S["gq"].sem, S["gq"].before(n))
                nc.scalar.activation(gm[:, u], g[:, u], ACT.Identity, scale=inv, bias=magic)\
                    .then_inc(S["gm"].sem, 1)

            def sigmoid(n, u, i):
                act.wait_ge(S["gq"].sem, S["gq"].at(n))
                act.wait_ge(S["sm"].sem, S["sm"].before(n))
                nc.scalar.activation(sg[:, u], gq[:, u], ACT.Sigmoid).then_inc(S["sg"].sem, 1)
                act.wait_ge(S["sg"].sem, S["sg"].at(n))
                act.wait_ge(S["g2"].sem, S["g2"].before(n))
                nc.scalar.activation(sm[:, u], sg[:, u], ACT.Identity, scale=65536.0, bias=magic)\
                    .then_inc(S["sm"].sem, 1)

            pipeline(act, NB, ((sigmoid, 1), (divide, 2)))

        @block.vector
        def _(dve):
            for k in ("gq", "sr", "g2", "new", "max"):
                S[k].give(dve)

            def quantise(n, u, i):
                dve.wait_ge(S["gm"].sem, S["gm"].at(n))
                dve.wait_ge(S["g2"].sem, S["g2"].before(n))
                nc.vector.tensor_scalar(gq[:, u], gm[:, u], MAGIC, scale, ALU.subtract, ALU.mult)\
                    .then_inc(S["gq"].sem, 1)

            def product(n, u, i):
                dve.wait_ge(S["sm"].sem, S["sm"].at(n))
                nc.vector.tensor_scalar(sm[:, u], sm[:, u], MAGIC + 65535.0, MAGIC, ALU.min, ALU.subtract)\
                    .then_inc(S["sr"].sem, 1)
                dve.wait_ge(S["sr"].sem, S["sr"].at(n))
                dve.wait_ge(stored[u], 16 * i)
                dve.wait_ge(S["new"].sem, S["new"].before(n))
                nc.vector.scalar_tensor_tensor(out=g2[:, u], in0=sm[:, u], scalar=1.0 / 65536.0,
                                               in1=gq[:, u], op0=ALU.mult, op1=ALU.mult)\
                    .then_inc(S["g2"].sem, 1)

            def maximum(n, u, i):
                dve.wait_ge(S["g2"].sem, S["g2"].at(n))
                running_max(nc, dve, new[:, u:u + 1], amax_g2[:, u:u + 1], g2[:, u], S["new"], S["max"], n)

            pipeline(dve, NB, ((quantise, 1), (product, 0), (maximum, 0)))


def phase_d(nc, NB, magic, g2_dram, up_dram, scale_g, inv_g, scale_u, inv_u, o_dram, amax_o):
    ctx = ExitStack()
    N = FT * T
    with ctx:
        def sb(name):
            return ctx.enter_context(nc.sbuf_tensor("d_" + name, [128, 2, N], F32))

        def sem(name):
            return nc.alloc_semaphore("d_" + name)

        src = {k: sb(k) for k in "gu"}
        rounded = {k: sb(k + "m") for k in "gu"}
        quant = {k: sb(k + "q") for k in "gu"}
        o = sb("o")
        new = ctx.enter_context(nc.sbuf_tensor("d_new", [128, 2], F32))
        dram = {"g": g2_dram, "u": up_dram}
        scale, inv = {"g": scale_g, "u": scale_u}, {"g": inv_g, "u": inv_u}
        loaded = {k: [sem(f"loaded_{k}{u}") for u in range(2)] for k in "gu"}
        stored = [sem(f"stored{u}") for u in range(2)]
        S = signals(ctx, nc, "d", gm=1, um=1, gq=1, uq=1, o=1, new=1, max=1)
        block = ctx.enter_context(nc.Block())

        @block.sync
        def _(sp):
            def load(k, n, u):
                sp.dma_start(src[k][:, u], dram[k][n]).then_inc(loaded[k][u], 16)

            def pair(i, more):
                for u in range(2):
                    n = 2 * i + u
                    for k in "gu":
                        if more:
                            sp.wait_ge(S[k + "m"].sem, S[k + "m"].at(n))
                            load(k, n + 2, u)
                for u in range(2):
                    n = 2 * i + u
                    sp.wait_ge(S["o"].sem, S["o"].at(n))
                    sp.dma_start(o_dram[n], o[:, u]).then_inc(stored[u], 16)

            for u in range(2):
                for k in "gu":
                    load(k, u, u)
            with sp.Fori(0, NB // 2 - 1) as i:
                pair(i, True)
            pair(NB // 2 - 1, False)
            for u in range(2):
                sp.wait_ge(stored[u], 16 * (NB // 2))

        @block.scalar
        def _(act):
            for k in ("gm", "um"):
                S[k].give(act)
            with act.Fori(0, NB // 2) as i:
                for u in range(2):
                    n = 2 * i + u
                    for k in "gu":
                        act.wait_ge(loaded[k][u], 16 * i + 16)
                        act.wait_ge(S[k + "q"].sem, S[k + "q"].before(n))
                        nc.scalar.activation(rounded[k][:, u], src[k][:, u], ACT.Identity, scale=inv[k],
                                             bias=magic).then_inc(S[k + "m"].sem, 1)

        @block.vector
        def _(dve):
            for k in ("gq", "uq", "o", "new", "max"):
                S[k].give(dve)
            with dve.Fori(0, NB // 2) as i:
                for u in range(2):
                    n = 2 * i + u
                    for k in "gu":
                        dve.wait_ge(S[k + "m"].sem, S[k + "m"].at(n))
                        dve.wait_ge(S["o"].sem, S["o"].before(n))
                        nc.vector.tensor_scalar(quant[k][:, u], rounded[k][:, u], MAGIC, scale[k],
                                                ALU.subtract, ALU.mult).then_inc(S[k + "q"].sem, 1)
                for u in range(2):
                    n = 2 * i + u
                    dve.wait_ge(S["uq"].sem, S["uq"].at(n))
                    dve.wait_ge(S["gq"].sem, S["gq"].at(n))
                    dve.wait_ge(stored[u], 16 * i)
                    dve.wait_ge(S["new"].sem, S["new"].before(n))
                    nc.vector.tensor_tensor(o[:, u], quant["g"][:, u], quant["u"][:, u], ALU.mult)\
                        .then_inc(S["o"].sem, 1)
                for u in range(2):
                    n = 2 * i + u
                    dve.wait_ge(S["o"].sem, S["o"].at(n))
                    running_max(nc, dve, new[:, u:u + 1], amax_o[:, u:u + 1], o[:, u], S["new"], S["max"], n)


PARTS = 3
Q_PART = (0, 0, 0, 1, 1, 2)
K_PART = (0, 1, 2, 0, 1, 0)
SLOTS = len(Q_PART)
SDPA, HYP, COS = range(3)
KINDS = [SDPA] * 6 + [HYP] * 4 + [COS] * 6
NSCALED = 10
HD1 = HD + 1
VW = 2 * HD
RP = 128


def pipeline(eng, NB, stages):
    def turn(i, b):
        for stage, lead in stages:
            k = b + lead
            if not isinstance(i, int) or 0 <= 2 * i + k < NB:
                stage((i, k), k % 2, i + k // 2)

    for b in range(-3, 2):
        turn(0, b)
    with eng.Fori(1, NB // 2 - 2) as i:
        for b in range(2):
            turn(i, b)
    for b in range(5):
        turn(NB // 2 - 2, b)


def batch_of(n):
    return 2 * n[0] + n[1]


def following(n, NB):
    return not isinstance(n[0], int) or 2 * n[0] + n[1] + 2 < NB


def phase_f1(nc, c, ps, NB, magic, o_dram, h1_dram, downT, scale, inv, wqkv_dram, curv_dram,
             h2_dram, parts_dram, v_dram):
    ctx = ExitStack()
    with ctx:
        def sb(name, shape, dt=F32):
            return ctx.enter_context(nc.sbuf_tensor("f_" + name, shape, dt))

        def sem(name):
            return nc.alloc_semaphore("f_" + name)

        GH = 6
        GROUPS = [(0, 6), (6, 6), (12, 4)]
        TURN = (2, 3, 1)
        wqkv = sb("wqkv", [128, CT, 3 * D])
        icurv = sb("icurv", [R, 4])
        o = sb("o", [128, 2, FT, T])
        om = sb("om", [128, 2, FT, T])
        h = sb("h", [R, 2, NT, D])
        stats = sb("stats", [R, 2, NT, 6])
        mv = sb("mv", [R, 2, NT, 2])
        var_eps = sb("var_eps", [R, 2, NT])
        rstd = sb("rstd", [R, 2, NT])
        xn = sb("xn", [R, 2, NT, D])
        xT = sb("xT", [128, 2, CT, T])
        rc = sb("rc", [R, 2, 2 * H, HD])
        rs = sb("rs", [R, 2, 2 * H, HD])
        qk = sb("qk", [R, 2, NT, 2 * H, HD1])
        sq = sb("sq", [R, 2, 2, NSCALED, HD])
        ss = sb("ss", [R, 2, NT * 2, NSCALED])
        norm = sb("norm", [R, 2, NT * 2, NSCALED])
        parts = sb("parts", [GH * HD1, 2, 6, PARTS, T], BF16)
        rest = sb("rest", [GH * HD1, 2, 2, T])
        vp = sb("vp", [R, 2, NT, H, VW])
        w_loaded = sem("w_loaded")
        filled = sem("filled")
        passed = sem("passed")
        o_loaded = [sem(f"o_loaded{u}") for u in range(2)]
        h_loaded = [sem(f"h_loaded{u}") for u in range(2)]
        h_stored = [sem(f"h_stored{u}") for u in range(2)]
        p_stored = [sem(f"p_stored{u}") for u in range(2)]
        v_stored = [sem(f"v_stored{u}") for u in range(2)]
        S = signals(ctx, nc, "f", om=1, oq=1, y=1, h2=1, bn=NT + 1, mv=1, eps=1, rstd=1, xn=NT, xT=1, xT_out=1,
                    qk=NT, v=2, v_out=2, rc=2 * NT, rot=NT, sq=NT, ss=NT, cap=2, norm=1, inv=1, tq=2, scaled=NT,
                    turn=6, hi=6, rest=6, mid=6, lo=6)
        block = ctx.enter_context(nc.Block())

        def tokens(dram, n):
            return dram[batch_of(n)].rearrange("(t p) d -> p t d", p=R)

        @block.sync
        def _(sp):
            def load_o(n, u):
                sp.dma_start(o[:, u].rearrange("p f t -> p (f t)"), o_dram[batch_of(n)]).then_inc(o_loaded[u], 16)

            def load_h(n, u):
                sp.dma_start(h[:, u], tokens(h1_dram, n)).then_inc(h_loaded[u], 16)

            def next_o(n, u, i):
                if following(n, NB):
                    sp.wait_ge(S["y"].sem, S["y"].at(n))
                    sp.sem_inc(passed, 1)
                    load_o((n[0], n[1] + 2), u)

            def store_h(n, u, i):
                sp.wait_ge(S["h2"].sem, S["h2"].at(n))
                sp.sem_inc(passed, 1)
                sp.dma_start(tokens(h2_dram, n), h[:, u]).then_inc(h_stored[u], 16)

            def next_h(n, u, i):
                if following(n, NB):
                    sp.wait_ge(S["xn"].sem, S["xn"].at(n))
                    sp.sem_inc(passed, 1)
                    sp.wait_ge(h_stored[u], 16 * (i + 1))
                    sp.sem_inc(passed, 1)
                    load_h((n[0], n[1] + 2), u)

            def store_v(n, u, i):
                sp.wait_ge(S["v_out"].sem, S["v_out"].at(n))
                sp.sem_inc(passed, 1)
                sp.dma_start(v_dram[batch_of(n)], vp[:, u].rearrange("p t h w -> p (t h w)")).then_inc(v_stored[u], 16)

            def store_parts(n, u, i):
                for j in range(6):
                    h0, nh = GROUPS[j % 3]
                    sp.wait_ge(S["lo"].sem, S["lo"].at(n, j + 1))
                    sp.sem_inc(passed, 1)
                    sp.dma_start(parts_dram[batch_of(n), j // 3, h0 * HD1:(h0 + nh) * HD1]
                                 .rearrange("r k t -> r (k t)"),
                                 parts[0:nh * HD1, u, j].rearrange("p k t -> p (k t)")).then_inc(p_stored[u], 16)

            sp.dma_start(wqkv[:], wqkv_dram.rearrange("(k p) n -> p k n", p=128)).then_inc(w_loaded, 16)
            sp.dma_start(icurv[:], curv_dram.rearrange("(a h) -> a h", a=1).broadcast_to([R, 4])).then_inc(w_loaded, 16)
            for u in range(2):
                load_o((0, u), u)
                load_h((0, u), u)
            pipeline(sp, NB, ((next_o, 1), (store_h, 1), (store_parts, -1), (next_h, 1), (store_v, 0)))
            for u in range(2):
                sp.wait_ge(h_stored[u], 16 * (NB // 2))
                sp.wait_ge(p_stored[u], 96 * (NB // 2))
                sp.wait_ge(v_stored[u], 16 * (NB // 2))

        @block.gpsimd
        def _(pool):
            for k in ("eps", "rstd", "cap"):
                S[k].give(pool)
            pool.wait_ge(filled, 1)

            def inverse_deviation(n, u, i):
                ln_rstd(nc, pool, c, mv[:, u], var_eps[:, u], rstd[:, u], S["mv"], S["eps"], S["rstd"], n)

            def guard(n, u, i):
                pool.wait_ge(S["ss"].sem, S["ss"].at(n))
                nc.gpsimd.tensor_tensor(ss[:, u, :, 0:4], ss[:, u, :, 0:4],
                                        icurv[:].unsqueeze(1).to_broadcast([R, NT * 2, 4]), ALU.add)\
                    .then_inc(S["cap"].sem, 1)
                nc.gpsimd.tensor_scalar(ss[:, u, :, 4:NSCALED], ss[:, u, :, 4:NSCALED], 1e-24, None, ALU.max)\
                    .then_inc(S["cap"].sem, 1)

            pipeline(pool, NB, ((inverse_deviation, 1), (guard, 0)))

        @block.scalar
        def _(act):
            for k in ("om", "xT_out", "v_out", "sq", "norm", "hi", "mid"):
                S[k].give(act)

            def round_o(n, u, i):
                act.wait_ge(o_loaded[u], 16 * (i + 1))
                act.wait_ge(S["oq"].sem, S["oq"].before(n))
                nc.scalar.activation(om[:, u], o[:, u], ACT.Identity, scale=inv, bias=magic)\
                    .then_inc(S["om"].sem, 1)

            def copy_x(n, u, i):
                act.wait_ge(S["xT"].sem, S["xT"].at(n))
                act.wait_ge(S["v"].sem, S["v"].before(n))
                nc.scalar.copy(xT[:, u], ps[:, 2:4, 0:T]).then_inc(S["xT_out"].sem, 1)

            def values_and_squares(n, u, i):
                act.wait_ge(v_stored[u], 16 * i)
                act.wait_ge(S["v"].sem, S["v"].at(n, 1))
                nc.scalar.copy(vp[:, u, 0:2, :, 0:HD], ps[0:R, 7, :].rearrange("p (t h w) -> p t h w", t=2, w=HD))\
                    .then_inc(S["v_out"].sem, 1)
                act.wait_ge(S["v"].sem, S["v"].at(n, 2))
                nc.scalar.copy(vp[:, u, 2, :, 0:HD], ps[0:R, 0, 0:D].rearrange("p (h w) -> p h w", w=HD))\
                    .then_inc(S["v_out"].sem, 1)
                for t in range(NT):
                    act.wait_ge(S["rot"].sem, S["rot"].at(n, t + 1))
                    if t:
                        act.wait_ge(S["ss"].sem, S["ss"].at(n, t))
                    else:
                        act.wait_ge(S["ss"].sem, S["ss"].before(n))
                    heads = qk[:, u, t].rearrange("p (a h) w -> p a h w", a=2)[:, :, 6:16, 0:HD]
                    nc.scalar.activation(sq[:, u], heads, ACT.Square).then_inc(S["sq"].sem, 1)

            def norms(n, u, i):
                act.wait_ge(S["cap"].sem, S["cap"].at(n))
                act.wait_ge(S["scaled"].sem, S["scaled"].before(n))
                nc.scalar.activation(norm[:, u], ss[:, u], ACT.Sqrt).then_inc(S["norm"].sem, 1)

            def upper_parts(n, u, i):
                act.wait_ge(p_stored[u], 96 * i)
                for j in range(6):
                    rows = GROUPS[j % 3][1] * HD1
                    act.wait_ge(S["turn"].sem, S["turn"].at(n, j + 1))
                    nc.scalar.copy(parts[0:rows, u, j, 0, :], ps[0:rows, TURN[j % 3], 0:T]).then_inc(S["hi"].sem, 1)
                    if j:
                        second_part(n, u, j - 1)
                second_part(n, u, 5)

            def second_part(n, u, j):
                rows = GROUPS[j % 3][1] * HD1
                act.wait_ge(S["rest"].sem, S["rest"].at(n, j + 1))
                nc.scalar.copy(parts[0:rows, u, j, 1, :], rest[0:rows, u, j % 2]).then_inc(S["mid"].sem, 1)

            pipeline(act, NB, ((copy_x, 0), (round_o, 2), (upper_parts, -1), (values_and_squares, 0), (norms, 0)))

        @block.vector
        def _(dve):
            for k in ("oq", "h2", "bn", "mv", "xn", "rc", "rot", "ss", "inv", "tq", "scaled", "rest", "lo"):
                S[k].give(dve)
            dve.wait_ge(w_loaded, 32)
            nc.vector.reciprocal(icurv[:], icurv[:]).then_inc(filled, 1)
            nc.vector.tensor_scalar(wqkv[:, :, 0:6 * HD], wqkv[:, :, 0:6 * HD], float(HD) ** -0.5, None, ALU.mult)\
                .then_inc(filled, 1)
            nc.vector.memset(vp[:], 1.0)
            nc.vector.memset(qk[:], 0.0).then_inc(filled, 1)
            dve.wait_ge(filled, 3)

            def quantise_o(n, u, i):
                dve.wait_ge(S["om"].sem, S["om"].at(n))
                nc.vector.tensor_scalar(o[:, u], om[:, u], MAGIC, scale, ALU.subtract, ALU.mult)\
                    .then_inc(S["oq"].sem, 1)

            def residual(n, u, i):
                dve.wait_ge(S["y"].sem, S["y"].at(n))
                dve.wait_ge(h_loaded[u], 16 * (i + 1))
                nc.vector.tensor_tensor(h[:, u, 0:2, :], ps[0:R, 0, :].rearrange("p (t d) -> p t d", t=2),
                                        h[:, u, 0:2, :], ALU.add)
                nc.vector.tensor_tensor(h[:, u, 2, :], ps[0:R, 1, 0:D], h[:, u, 2, :], ALU.add)\
                    .then_inc(S["h2"].sem, 1)
                dve.wait_ge(S["h2"].sem, S["h2"].at(n))
                dve.wait_ge(S["xn"].sem, S["xn"].before(n))
                ln_stats(nc, dve, h[:, u], stats[:, u], mv[:, u], (S["bn"].sem, S["bn"].at(n)), S["mv"])

            def normalise(n, u, i):
                dve.wait_ge(S["rstd"].sem, S["rstd"].at(n))
                dve.wait_ge(S["xT"].sem, S["xT"].before(n))
                ln_apply(nc, xn[:, u], h[:, u], mv[:, u], rstd[:, u], S["xn"])

            def rotate(n, u, i):
                dve.wait_ge(S["turn"].sem, S["turn"].before(n))
                for t in range(NT):
                    x = ps[0:R, 4 + t, :].rearrange("p (h w) -> p h w", w=HD)
                    cos = c["cos"][:, t].unsqueeze(1).to_broadcast([R, 2 * H, HD])
                    sin = c["sin"][:, t].unsqueeze(1)
                    half = HD // 2
                    dve.wait_ge(S["qk"].sem, S["qk"].at(n, t + 1))
                    if t:
                        dve.wait_ge(S["rot"].sem, S["rot"].at(n, t))
                    nc.vector.tensor_tensor(rc[:, u], x, cos, ALU.mult)
                    nc.vector.tensor_tensor(rs[:, u, :, 0:half], x[:, :, half:HD],
                                            sin[:, :, 0:half].to_broadcast([R, 2 * H, half]), ALU.mult)\
                        .then_inc(S["rc"].sem, 1)
                    nc.vector.tensor_tensor(rs[:, u, :, half:HD], x[:, :, 0:half],
                                            sin[:, :, half:HD].to_broadcast([R, 2 * H, half]), ALU.mult)\
                        .then_inc(S["rc"].sem, 1)
                    dve.wait_ge(S["rc"].sem, S["rc"].at(n, 2 * t + 2))
                    nc.vector.tensor_tensor(qk[:, u, t, :, 0:HD], rc[:, u], rs[:, u], ALU.add)\
                        .then_inc(S["rot"].sem, 1)
                for t in range(NT):
                    dve.wait_ge(S["sq"].sem, S["sq"].at(n, t + 1))
                    if t == 0:
                        dve.wait_ge(S["norm"].sem, S["norm"].before(n))
                    nc.vector.reduce_sum(ss[:, u, 2 * t:2 * t + 2, :], sq[:, u], AX.X).then_inc(S["ss"].sem, 1)

            def scale_heads(n, u, i):
                dve.wait_ge(S["norm"].sem, S["norm"].at(n))
                split = norm[:, u].rearrange("p (t a) h -> p t a h", a=2)
                nc.vector.reciprocal(norm[:, u, :, 4:NSCALED], norm[:, u, :, 4:NSCALED]).then_inc(S["inv"].sem, 1)
                nc.vector.tensor_copy(qk[:, u, :, 6:10, HD], split[:, :, 0, 0:4]).then_inc(S["tq"].sem, 1)
                nc.vector.tensor_scalar(qk[:, u, :, H + 6:H + 10, HD], split[:, :, 1, 0:4], -1.0, None, ALU.mult)\
                    .then_inc(S["tq"].sem, 1)
                dve.wait_ge(S["inv"].sem, S["inv"].at(n))
                for t in range(NT):
                    heads = qk[:, u, t].rearrange("p (a h) w -> p a h w", a=2)[:, :, 10:16, 0:HD]
                    nc.vector.tensor_tensor(heads, heads, split[:, t, :, 4:NSCALED].unsqueeze(3)
                                            .to_broadcast([R, 2, 6, HD]), ALU.mult).then_inc(S["scaled"].sem, 1)

            def lower_parts(n, u, i):
                for j in range(6):
                    rows = GROUPS[j % 3][1] * HD1
                    dve.wait_ge(S["hi"].sem, S["hi"].at(n, j + 1))
                    if j >= 2:
                        dve.wait_ge(S["lo"].sem, S["lo"].at(n, j - 1))
                    nc.vector.tensor_tensor(rest[0:rows, u, j % 2], ps[0:rows, TURN[j % 3], 0:T],
                                            parts[0:rows, u, j, 0, :], ALU.subtract).then_inc(S["rest"].sem, 1)
                    if j:
                        third_part(n, u, j - 1)
                third_part(n, u, 5)

            def third_part(n, u, j):
                rows = GROUPS[j % 3][1] * HD1
                dve.wait_ge(S["mid"].sem, S["mid"].at(n, j + 1))
                nc.vector.tensor_tensor(parts[0:rows, u, j, 2, :], rest[0:rows, u, j % 2],
                                        parts[0:rows, u, j, 1, :], ALU.subtract).then_inc(S["lo"].sem, 1)

            pipeline(dve, NB, ((scale_heads, -1), (quantise_o, 2), (residual, 1), (lower_parts, -1), (normalise, 1),
                               (rotate, 0)))

        @block.tensor
        def _(pe):
            for k in ("y", "xT", "qk", "v", "turn"):
                S[k].give(pe)
            pe.wait_ge(filled, 2)

            def down(n, u, i):
                pe.wait_ge(S["oq"].sem, S["oq"].at(n))
                pe.wait_ge(S["v_out"].sem, S["v_out"].at((n[0], n[1] - 1), 0))
                pe.wait_ge(S["rest"].sem, S["rest"].at((n[0], n[1] - 2), 0))
                for t in range(NT):
                    for k in range(FT):
                        last = nc.tensor.matmul(ps[0:R, t // 2, (t % 2) * D:(t % 2 + 1) * D],
                                                o[:, u, k, t * R:(t + 1) * R], downT[:, k, :],
                                                start=(k == 0), stop=(k == FT - 1))
                last.then_inc(S["y"].sem, 1)

            def turn_x(n, u, i):
                pe.wait_ge(S["xn"].sem, S["xn"].at(n))
                pe.wait_ge(S["rest"].sem, S["rest"].at((n[0], n[1] - 1), 0))
                transpose_tokens(nc, pe, c, xn[:, u], lambda k: ps[:, 2 + k, :]).then_inc(S["xT"].sem, 1)

            def project(n, u, i):
                pe.wait_ge(S["xT_out"].sem, S["xT_out"].at(n))
                pe.wait_ge(S["rot"].sem, S["rot"].at((n[0], n[1] - 1)))
                for t in range(NT):
                    for k in range(CT):
                        last = nc.tensor.matmul(ps[0:R, 4 + t, :], xT[:, u, k, t * R:(t + 1) * R],
                                                wqkv[:, k, 0:2 * D], start=(k == 0), stop=(k == CT - 1))
                    last.then_inc(S["qk"].sem, 1)
                pe.wait_ge(S["v_out"].sem, S["v_out"].at(n, 0))
                if not isinstance(n[0], int) or 2 * n[0] + n[1] + 1 < NB:
                    pe.wait_ge(S["h2"].sem, S["h2"].at((n[0], n[1] + 1)))
                for t in range(NT):
                    if t == 2:
                        last.then_inc(S["v"].sem, 1)
                    for k in range(CT):
                        last = nc.tensor.matmul(ps[0:R, 0 if t == 2 else 7, (t % 2) * D:(t % 2 + 1) * D],
                                                xT[:, u, k, t * R:(t + 1) * R], wqkv[:, k, 2 * D:3 * D],
                                                start=(k == 0), stop=(k == CT - 1))
                last.then_inc(S["v"].sem, 1)

            def turn_heads(n, u, i):
                pe.wait_ge(S["tq"].sem, S["tq"].at(n))
                pe.wait_ge(S["scaled"].sem, S["scaled"].at(n))
                if not isinstance(n[0], int) or 2 * n[0] + n[1] + 1 < NB:
                    pe.wait_ge(S["xT_out"].sem, S["xT_out"].at((n[0], n[1] + 1)))
                if not isinstance(n[0], int) or 2 * n[0] + n[1] + 2 < NB:
                    pe.wait_ge(S["h2"].sem, S["h2"].at((n[0], n[1] + 2)))
                for j in range(6):
                    h0, nh = GROUPS[j % 3]
                    if j >= 3:
                        pe.wait_ge(S["rest"].sem, S["rest"].at(n, j - 2))
                    x = qk[:, u].rearrange("p t h w -> p t (h w)")
                    first = (H * (j // 3) + h0) * HD1
                    for t in range(NT):
                        last = nc.tensor.transpose(ps[0:nh * HD1, TURN[j % 3], t * R:(t + 1) * R],
                                                   x[:, t, first:first + nh * HD1], c["ident"][0:R, 0:R])
                    last.then_inc(S["turn"].sem, 1)

            pipeline(pe, NB, ((turn_x, 0), (down, 1), (turn_heads, -1), (project, 0)))


def attention_core(nc, c, ps, NB, name, kinds, causal, hd, parts_dram, v_dram, ctx_dram, curv_dram=None):
    ctx = ExitStack()
    with ctx:
        def sb(n_, shape, dt=F32):
            return ctx.enter_context(nc.sbuf_tensor(f"{name}_{n_}", shape, dt))

        def sem(n_):
            return nc.alloc_semaphore(f"{name}_{n_}")

        rows, SHIFT = SLOTS * hd, PARTS
        full = 128
        if causal:
            UNITS = 2
            QTILE = {2: (0, 0), 1: (1, 0), 0: (1, 2 * R)}
            KTILE = {0: (0, 0), 1: (1, 0), 2: (1, 2 * R)}
            ORDER = [12, 13, 14, 15, 10, 11, 8, 9, 4, 6, 5, 7, 0, 1, 2, 3]
        else:
            UNITS = 3
            QTILE = {t: (t, 0) for t in range(NT)}
            KTILE = QTILE
            ORDER = list(range(H))
        HYPS = [h for h in range(H) if kinds[h] == HYP]
        hyp_slot = [[h for h in ORDER if h in HYPS].index(h) for h in HYPS]
        SDPAS = [h for h in range(H) if kinds[h] == SDPA]
        NHYP = len(HYPS)
        MAXED = NHYP + len(SDPAS)

        def place(step):
            return (("pre", step + H) if step < 0 else ("main", step) if step < H else ("post", step - H))

        first = -11 if NHYP else -13
        look_order = [h for pair in zip(HYPS, SDPAS) for h in pair] + SDPAS[NHYP:]
        look_step = {h: first + x for x, h in enumerate(look_order)}
        look = {place(step): h for h, step in look_step.items()}
        if NHYP:
            ROOT, SUM, SCORE = 1, 2, 4
            NEGATE = place(look_step[HYPS[-1]] + SCORE + 1)
            shifts = [(look_step[HYPS[-1]] + SCORE + 2, 0, MAXED)]
        else:
            shifts = [(-7, 0, 6), (-3, 6, 10), (5, 10, H)]
        NSH = len(shifts)
        product = {place(4 * g + 4 + kt): (g, kt) for g in range(4) for kt in range(NT)}
        back_step = {g: 4 * g + 8 for g in range(4)}
        back = {place(step): g for g, step in back_step.items()}
        uses = {}
        for h in look_order:
            for which in (("max", "raw") if kinds[h] == HYP else ("max",)):
                for b in range(UNITS):
                    uses[(h, which, b)] = len(uses)
        RING1, RING2 = (0, 1, 2), (3, 4, 5)

        def shifts_at(when, p, later=0):
            return [(x, lo, hi) for x, (step, lo, hi) in enumerate(shifts) if place(step + later) == (when, p)]

        q = sb("q", [full, 2, H, T], BF16)
        k = sb("k", [full, 2, H, T], BF16)
        vp = sb("vp", [RP, 2, NT, H, VW])
        neg = sb("neg", [R, 2, NT, MAXED])
        shift = sb("shift", [H, 2, PARTS, T], BF16)
        rest = sb("rest", [H, 2, T])
        probT = sb("probT", [RP, 8, UNITS, T])
        oT = sb("oT", [128, 2, T])
        rec = sb("rec", [R, 2, NT, 4])
        out = sb("out", [R, 2, NT, H, HD])
        ones_set, zeros_set = sem("ones_set"), sem("zeros_set")
        qk_loaded = [sem(f"qk_loaded{u}") for u in range(2)]
        v_loaded = [sem(f"v_loaded{u}") for u in range(2)]
        stored = [sem(f"stored{u}") for u in range(2)]
        laid = [sem(f"laid{u}") for u in range(2)]
        passed, sp_passed = sem("passed"), sem("sp_passed")
        sigs = dict(look=len(uses), looked=len(uses), turn=NSH, hi=NSH, rest=NSH, mid=NSH, lo=NSH,
                    s=H * UNITS, exp=H * UNITS, pv=4, oT=4, back=4, rec=4, out=4)
        if NHYP:
            W = 2 * T + NT
            negc = sb("negc", [R, 4])
            root_ic = sb("root_ic", [R, 4])
            one = sb("one", [R, 1])
            eps6 = sb("eps6", [R, 1])
            only_shift = sb("only_shift", [full, R], BF16)
            top = sb("top", [R, 2, NHYP, NT])
            hw = sb("hw", [R, 2, NHYP, W])
            hu = sb("hu", [R, NHYP, W])
            curv_loaded, ready = sem("curv_loaded"), sem("ready")
            sigs |= dict(top=NHYP * NT, w=NHYP, wc=NHYP, hu=NHYP, hl=NHYP, root=NHYP, z=NHYP, l1=NHYP, l2=NHYP,
                         score=NHYP, hneg=1, shifted=NHYP * UNITS)
        S = signals(ctx, nc, name, **sigs)
        block = ctx.enter_context(nc.Block())

        def is_last(u, i):
            return isinstance(i, int) and i == NB // 2 - 1 and u == 1

        def program(eng, step):
            def body(i, b, posts=True, mains=True, pres=True):
                for p in range(H):
                    for when, k, there in (("post", b - 1, posts), ("main", b, mains), ("pre", b + 1, pres)):
                        if there:
                            step(when, p, (i, k), k % 2, i + k // 2)

            body(0, -1, posts=False, mains=False)
            body(0, 0, posts=False)
            body(0, 1)
            with eng.Fori(1, NB // 2 - 1) as i:
                body(i, 0)
                body(i, 1)
            body(NB // 2 - 1, 0)
            body(NB // 2 - 1, 1, pres=False)
            body(NB // 2 - 1, 2, mains=False, pres=False)

        @block.sync
        def _(sp):
            def load_qk(n, u):
                for x, which, dst in ((0, Q_PART, q), (1, K_PART, k)):
                    rowsd = parts_dram[n, x].rearrange("(h d) k t -> d h k t", d=hd)
                    for s, part in enumerate(which):
                        sp.dma_start(dst[s * hd:(s + 1) * hd, u], rowsd[:, :, part, :]).then_inc(qk_loaded[u], 16)

            def load_v(n, u):
                sp.dma_start(vp[0:R, u].rearrange("p t h w -> p (t h w)"), v_dram[n]).then_inc(v_loaded[u], 16)

            def batch(i, u, more):
                n = 2 * i + u
                if more:
                    sp.wait_ge(S["s"].sem, S["s"].at(n))
                    sp.sem_inc(sp_passed, 1)
                    load_qk(n + 2, u)
                    sp.wait_ge(S["pv"].sem, S["pv"].at(n))
                    sp.sem_inc(sp_passed, 1)
                    load_v(n + 2, u)
                sp.wait_ge(S["out"].sem, S["out"].at(n))
                sp.dma_start(ctx_dram[n].rearrange("(t p) d -> p t d", p=R),
                             out[:, u].rearrange("p t h w -> p t (h w)")).then_inc(stored[u], 16)

            sp.wait_ge(ones_set, 1)
            sp.wait_ge(zeros_set, 2)
            for u in range(2):
                load_qk(u, u)
                load_v(u, u)
            with sp.Fori(0, NB // 2 - 1) as i:
                for u in range(2):
                    batch(i, u, True)
            for u in range(2):
                batch(NB // 2 - 1, u, False)
            for u in range(2):
                sp.wait_ge(stored[u], 16 * (NB // 2))

        @block.gpsimd
        def _(pool):
            nc.gpsimd.memset(k[96:full], 1.0).then_inc(ones_set, 1)
            pool.wait_ge(ones_set, 1)
            if NHYP:
                pool.dma_start(negc[:], curv_dram.rearrange("(a h) -> a h", a=1).broadcast_to([R, 4]))\
                    .then_inc(curv_loaded, 16)
                nc.gpsimd.memset(one[:], 1.0).then_inc(ready, 1)
                nc.gpsimd.memset(eps6[:], 1e-6).then_inc(ready, 1)
                nc.gpsimd.memset(only_shift[0:96], 0.0).then_inc(ready, 1)
                nc.gpsimd.memset(only_shift[96:full], 1.0).then_inc(ready, 1)
                pool.wait_ge(curv_loaded, 16)
                pool.wait_ge(ready, 4)
                nc.gpsimd.affine_select(out=only_shift[96:full], in_=only_shift[96:full], compare_op=ALU.is_ge,
                                        fill=0.0, base=96 - rows, pattern=[[0, R]], channel_multiplier=1)\
                    .then_inc(ready, 1)
                nc.gpsimd.tensor_tensor(root_ic[:], negc[:], c["minus_half"][:, 0:4], ALU.pow).then_inc(ready, 1)
                pool.wait_ge(ready, 6)
                nc.gpsimd.tensor_scalar(negc[:], negc[:], -1.0, None, ALU.mult).then_inc(ready, 1)

            def step(when, p, n, u, i):
                for x, lo, hi in shifts_at(when, p, 2):
                    pool.wait_ge(S["lo"].sem, S["lo"].at(n, x + 1))
                    pool.sem_inc(passed, 1)
                    for part in range(PARTS):
                        pool.dma_start(q[rows + part:rows + part + 1, u, lo:hi, :],
                                       shift[0:hi - lo, u, part, :]).then_inc(laid[u], 16)

            program(pool, step)

        @block.tensor
        def _(pe):
            for x in ("look", "s", "turn", "pv", "back"):
                S[x].give(pe)
            if NHYP:
                pe.wait_ge(ready, 7)

            def tile(bank, col, w, mask, stationary, moving, col_of_mask):
                out_ = ps[0:R, bank, col:col + w]
                if mask is not None:
                    nc.tensor.matmul(ps[0:R, bank, col + col_of_mask:col + col_of_mask + R], c["identb"][0:R, 0:R],
                                     c[mask][:], start=True, stop=False, skip_group_check=True)
                return nc.tensor.matmul(out_, stationary, moving, start=mask is None, stop=True,
                                        skip_group_check=mask is not None)

            def by_query(u, h, b, bank):
                for t, (unit, col) in sorted(QTILE.items(), key=lambda x: x[1]):
                    if unit == b:
                        w = (t + 1) * R if causal else T
                        last = tile(bank, col, w, "mask_qk" if causal else None,
                                    q[0:rows, u, h, t * R:(t + 1) * R], k[0:rows, u, h, 0:w], t * R)
                return last

            def by_key(u, h, b, bank, kind):
                for t, (unit, col) in sorted(KTILE.items(), key=lambda x: x[1]):
                    if unit == b:
                        q0 = t * R if causal else 0
                        size = full if kind in ("shifted", "shift only") else rows
                        stationary = only_shift[:] if kind == "shift only" else k[0:size, u, h, t * R:(t + 1) * R]
                        masked = causal and kind != "raw"
                        last = tile(bank, col, T - q0, "mask_kq" if masked else None,
                                    stationary, q[0:size, u, h, q0:T], 0)
                return last

            def step(when, p, n, u, i):
                if when == "main":
                    h = ORDER[p]
                    if kinds[h] != COS:
                        x = [lo <= h < hi for _, lo, hi in shifts].index(True)
                        pe.wait_ge(laid[u], 16 * PARTS * (NSH * i + x + 1))
                    for b in range(UNITS):
                        y = p * UNITS + b
                        pe.wait_ge(S["exp"].sem, S["exp"].at(n, y - 2))
                        by_key(u, h, b, RING2[y % 3], {SDPA: "shifted", HYP: "shift only", COS: "plain"}[kinds[h]])\
                            .then_inc(S["s"].sem, 1)
                if (when, p) in look:
                    h = look[when, p]
                    if h == look_order[0]:
                        pe.wait_ge(qk_loaded[u], 16 * 2 * SLOTS * (i + 1))
                    for which in (("max", "raw") if kinds[h] == HYP else ("max",)):
                        for b in range(UNITS):
                            y = uses[(h, which, b)]
                            pe.wait_ge(S["looked"].sem, S["looked"].at(n, y - 2))
                            bank = RING1[y % 3]
                            last = by_query(u, h, b, bank) if which == "max" else by_key(u, h, b, bank, "raw")
                            last.then_inc(S["look"].sem, 1)
                for x, lo, hi in shifts_at(when, p):
                    done = [y for (h, _, _), y in uses.items() if lo <= h < hi]
                    pe.wait_ge(S["looked"].sem, S["looked"].at(n, max(done) + 1))
                    if NHYP:
                        pe.wait_ge(S["hneg"].sem, S["hneg"].at(n))
                    ways = 4 + max([g for g in back_step if back_step[g] - H < shifts[x][0]], default=-1)
                    pe.wait_ge(S["out"].sem, S["out"].at((n[0], n[1] - 1), ways - 3))
                    pe.wait_ge(S["rest"].sem, S["rest"].at(n, x))
                    for t in range(NT):
                        last = nc.tensor.transpose(ps[0:hi - lo, 7, t * R:(t + 1) * R], neg[:, u, t, lo:hi],
                                                   c["ident"][0:R, 0:R])
                    last.then_inc(S["turn"].sem, 1)
                if (when, p) in product:
                    g, kt = product[when, p]
                    if g == 0 and kt == 0:
                        pe.wait_ge(v_loaded[u], 16 * (i + 1))
                    if kt == 0:
                        pe.wait_ge(S["exp"].sem, S["exp"].at(n, (4 * g + 4) * UNITS))
                        pe.wait_ge(S["oT"].sem, S["oT"].at(n, g))
                    b, col = KTILE[kt]
                    q0 = kt * R if causal else 0
                    for j in range(4 * g, 4 * g + 4):
                        a = ORDER[j] % 4
                        last = nc.tensor.matmul(ps[32 * a:32 * a + VW, 6, q0:T], vp[:, u, kt, ORDER[j], :],
                                                probT[:, j % 8, b, col:col + T - q0],
                                                start=(kt == 0), stop=(kt == NT - 1), tile_position=(0, 32 * a))
                    if kt == NT - 1:
                        last.then_inc(S["pv"].sem, 1)
                if (when, p) in back:
                    g = back[when, p]
                    pe.wait_ge(S["oT"].sem, S["oT"].at(n, g + 1))
                    pe.wait_ge(S["out"].sem, S["out"].at(n, g))
                    for x, (at, _, _) in enumerate(shifts):
                        for b in (-1, 0) if is_last(u, i) else (-1, 0, 1):
                            if back_step[g] - 4 <= at + b * H < back_step[g]:
                                pe.wait_ge(S["rest"].sem, S["rest"].at((n[0], n[1] + b), x + 1))
                    for t in range(NT):
                        last = nc.tensor.transpose(ps[0:R, 7, t * 128:(t + 1) * 128],
                                                   oT[:, g % 2, t * R:(t + 1) * R], c["ident"][:])
                    last.then_inc(S["back"].sem, 1)

            program(pe, step)

        @block.scalar
        def _(act):
            for x in ("exp", "oT", "hi", "mid") + (("hl", "root", "l1", "l2", "score") if NHYP else ()):
                S[x].give(act)
            act.wait_ge(zeros_set, 3)
            if NHYP:
                nc.scalar.preload_act_table_set("natural_log_exp_and_others")
                act.wait_ge(ready, 7)

            def step(when, p, n, u, i):
                if when == "main":
                    h = ORDER[p]
                    act.wait_ge(S["pv"].sem, S["pv"].at(n, p // 4 - 1))
                    for b in range(UNITS):
                        y = p * UNITS + b
                        if kinds[h] == HYP:
                            a = HYPS.index(h)
                            act.wait_ge(S["shifted"].sem, S["shifted"].at(n, hyp_slot[a] * UNITS + b + 1))
                            src = hw[:, u, a, b * T:(b + 1) * T]
                        else:
                            act.wait_ge(S["s"].sem, S["s"].at(n, y + 1))
                            src = ps[0:R, RING2[y % 3], 0:T]
                        nc.scalar.activation(probT[0:R, p % 8, b, :], src, ACT.Exp,
                                             scale=float(HD) ** 0.5 if kinds[h] == COS else 1.0)\
                            .then_inc(S["exp"].sem, 1)
                if product.get((when, p), (0, 0))[1] == NT - 1:
                    g = product[when, p][0]
                    act.wait_ge(S["pv"].sem, S["pv"].at(n, g + 1))
                    act.wait_ge(S["back"].sem, S["back"].at(n, g - 1))
                    nc.scalar.copy(oT[:, g % 2], ps[:, 6, 0:T]).then_inc(S["oT"].sem, 1)
                for a, h in enumerate(HYPS):
                    if (when, p) == place(look_step[h] + ROOT):
                        act.wait_ge(S["hu"].sem, S["hu"].at(n, a + 1))
                        nc.scalar.activation(hu[:, a], hu[:, a], ACT.Ln).then_inc(S["hl"].sem, 1)
                        act.wait_ge(S["hl"].sem, S["hl"].at(n, a + 1))
                        nc.scalar.activation(hu[:, a], hu[:, a], ACT.Exp, scale=0.5).then_inc(S["root"].sem, 1)
                    if (when, p) == place(look_step[h] + SCORE):
                        act.wait_ge(S["z"].sem, S["z"].at(n, a + 1))
                        nc.scalar.activation(hw[:, u, a], hw[:, u, a], ACT.Ln, bias=one[:]).then_inc(S["l1"].sem, 1)
                        act.wait_ge(S["l1"].sem, S["l1"].at(n, a + 1))
                        nc.scalar.activation(hw[:, u, a], hw[:, u, a], ACT.Ln, bias=eps6[:],
                                             scale=root_ic[:, a:a + 1]).then_inc(S["l2"].sem, 1)
                        act.wait_ge(S["l2"].sem, S["l2"].at(n, a + 1))
                        nc.scalar.activation(hw[:, u, a], hw[:, u, a], ACT.Exp, scale=-1.0)\
                            .then_inc(S["score"].sem, 1)
                for x, lo, hi in shifts_at(when, p, 1):
                    act.wait_ge(S["turn"].sem, S["turn"].at(n, x + 1))
                    act.wait_ge(laid[u], 16 * PARTS * (NSH * i + x))
                    nc.scalar.copy(shift[0:hi - lo, u, 0], ps[0:hi - lo, 7, 0:T]).then_inc(S["hi"].sem, 1)
                for x, lo, hi in shifts_at(when, p, 2):
                    act.wait_ge(S["rest"].sem, S["rest"].at(n, x + 1))
                    nc.scalar.copy(shift[0:hi - lo, u, 1], rest[0:hi - lo, u]).then_inc(S["mid"].sem, 1)

            program(act, step)

        @block.vector
        def _(dve):
            for x in ("looked", "rest", "lo", "rec", "out") + (("top", "w", "wc", "hu", "z", "hneg", "shifted") if NHYP else ()):
                S[x].give(dve)
            nc.vector.memset(q[96:full], 0.0).then_inc(zeros_set, 1)
            nc.vector.memset(vp[64:RP], 0.0).then_inc(zeros_set, 1)
            nc.vector.memset(probT[64:RP], 0.0).then_inc(zeros_set, 1)
            if NHYP:
                dve.wait_ge(ready, 7)

            def step(when, p, n, u, i):
                if when == "main" and kinds[ORDER[p]] == HYP:
                    a = HYPS.index(ORDER[p])
                    for b in range(UNITS):
                        y = p * UNITS + b
                        dve.wait_ge(S["s"].sem, S["s"].at(n, y + 1))
                        dve.wait_ge(S["score"].sem, S["score"].at(n, a + 1))
                        d = hw[:, u, a, b * T:(b + 1) * T]
                        nc.vector.tensor_tensor(d, d, ps[0:R, RING2[y % 3], 0:T], ALU.add)\
                            .then_inc(S["shifted"].sem, 1)
                if (when, p) in look:
                    h = look[when, p]
                    a = HYPS.index(h) if kinds[h] == HYP else None
                    if a is not None:
                        dve.wait_ge(S["exp"].sem, S["exp"].at((n[0], n[1] - 1), 0))
                    for b in range(UNITS):
                        y = uses[(h, "max", b)]
                        dve.wait_ge(S["look"].sem, S["look"].at(n, y + 1))
                        for t, (unit, col) in sorted(QTILE.items(), key=lambda x: x[1]):
                            if unit == b:
                                src = ps[0:R, RING1[y % 3], col:col + ((t + 1) * R if causal else T)]
                                if a is not None:
                                    nc.vector.reduce_max(top[:, u, a, t:t + 1], src, AX.X).then_inc(S["top"].sem, 1)
                                else:
                                    last = nc.vector.tensor_reduce(neg[:, u, t, h:h + 1], src, AX.X, ALU.max,
                                                                   negate=True)
                        if a is None:
                            last.then_inc(S["looked"].sem, 1)
                        else:
                            dve.wait_ge(S["top"].sem, S["top"].at(n, a * NT + (1 if b == 0 else NT)))
                            dve.sem_inc(S["looked"].sem, 1)
                    if a is not None:
                        nc.vector.tensor_scalar(hw[:, u, a, 2 * T:W], top[:, u, a], negc[:, a:a + 1], -1.0,
                                                ALU.mult, ALU.add).then_inc(S["w"].sem, 1)
                        for b in range(UNITS):
                            y = uses[(h, "raw", b)]
                            dve.wait_ge(S["look"].sem, S["look"].at(n, y + 1))
                            nc.vector.tensor_scalar(hw[:, u, a, b * T:(b + 1) * T], ps[0:R, RING1[y % 3], 0:T],
                                                    negc[:, a:a + 1], -1.0, ALU.mult, ALU.add)\
                                .then_inc(S["looked"].sem, 1)
                        dve.wait_ge(S["w"].sem, S["w"].at(n, a + 1))
                        dve.wait_ge(S["looked"].sem, S["looked"].at(n, y + 1))
                        nc.vector.tensor_scalar(hw[:, u, a], hw[:, u, a], 2.0 ** -23, None, ALU.max)\
                            .then_inc(S["wc"].sem, 1)
                        dve.wait_ge(S["z"].sem, S["z"].at(n, a + 1 - NHYP))
                        dve.wait_ge(S["wc"].sem, S["wc"].at(n, a + 1))
                        nc.vector.scalar_tensor_tensor(out=hu[:, a], in0=hw[:, u, a], scalar=2.0,
                                                       in1=hw[:, u, a], op0=ALU.add, op1=ALU.mult)\
                            .then_inc(S["hu"].sem, 1)
                for a, h in enumerate(HYPS):
                    if (when, p) == place(look_step[h] + SUM):
                        dve.wait_ge(S["root"].sem, S["root"].at(n, a + 1))
                        nc.vector.tensor_tensor(hw[:, u, a], hw[:, u, a], hu[:, a], ALU.add).then_inc(S["z"].sem, 1)
                if NHYP and (when, p) == NEGATE:
                    dve.wait_ge(S["score"].sem, S["score"].at(n))
                    nc.vector.tensor_scalar(neg[:, u, :, HYPS[0]:HYPS[0] + NHYP].rearrange("p t a -> p a t"),
                                            hw[:, u, :, 2 * T:W], -1.0, None, ALU.mult).then_inc(S["hneg"].sem, 1)
                for x, lo, hi in shifts_at(when, p, 1):
                    dve.wait_ge(S["hi"].sem, S["hi"].at(n, x + 1))
                    dve.wait_ge(S["lo"].sem, S["lo"].at(n, x))
                    nc.vector.tensor_tensor(rest[0:hi - lo, u], ps[0:hi - lo, 7, 0:T], shift[0:hi - lo, u, 0],
                                            ALU.subtract).then_inc(S["rest"].sem, 1)
                for x, lo, hi in shifts_at(when, p, 2):
                    dve.wait_ge(S["mid"].sem, S["mid"].at(n, x + 1))
                    nc.vector.tensor_tensor(shift[0:hi - lo, u, 2], rest[0:hi - lo, u], shift[0:hi - lo, u, 1],
                                            ALU.subtract).then_inc(S["lo"].sem, 1)
                if (when, p) in back:
                    g = back[when, p]
                    if g == 0:
                        dve.wait_ge(stored[u], 16 * i)
                    dve.wait_ge(S["back"].sem, S["back"].at(n, g + 1))
                    dve.wait_ge(S["out"].sem, S["out"].at(n, g - 1))
                    x = ps[0:R, 7, 0:NT * 128].rearrange("p (t a w) -> p t a w", t=NT, a=4)
                    nc.vector.reciprocal(rec[:, g % 2], x[:, :, :, HD]).then_inc(S["rec"].sem, 1)
                    dve.wait_ge(S["rec"].sem, S["rec"].at(n, g + 1))
                    h0 = min(ORDER[4 * g:4 * g + 4])
                    nc.vector.tensor_tensor(out[:, u, :, h0:h0 + 4, :], x[:, :, :, 0:HD],
                                            rec[:, g % 2].unsqueeze(3).to_broadcast([R, NT, 4, HD]), ALU.mult)\
                        .then_inc(S["out"].sem, 1)

            program(dve, step)


def row(dram):
    return dram.rearrange("(a d) -> a d", a=1)


def phase_g1(nc, c, ps, NB, ctx_dram, h2_dram, proj_dram, projb_dram, wq_dram, wk_dram, wv_dram,
             bq_dram, bk_dram, bv_dram, h3_dram, x3_dram, parts_dram, v_dram):
    ctx = ExitStack()
    with ctx:
        def sb(name, shape, dt=F32):
            return ctx.enter_context(nc.sbuf_tensor("p_" + name, shape, dt))

        def sem(name):
            return nc.alloc_semaphore("p_" + name)

        proj, wv = sb("proj", [128, CT, D]), sb("wv", [128, CT, D])
        wqk = sb("wqk", [128, CT, 2, D])
        bqk = sb("bqk", [128, 2, CT])
        projb, bv = sb("projb", [R, D]), sb("bv", [R, D])
        cx = sb("cx", [R, 2, NT, D])
        cT = sb("cT", [128, 2, CT, T])
        h = sb("h", [R, 2, NT, D])
        stats = sb("stats", [R, 2, NT, 6])
        mv = sb("mv", [R, 2, NT, 2])
        var_eps = sb("var_eps", [R, 2, NT])
        rstd = sb("rstd", [R, 2, NT])
        xn = sb("xn", [R, 2, NT, D])
        xT = sb("xT", [128, 2, CT, T])
        parts = sb("parts", [128, 2, 2 * CT, PARTS, T], BF16)
        rest = sb("rest", [128, 2, 2, T])
        vp = sb("vp", [R, 2, NT, H, VW])
        w_loaded, scaled, filled, passed = (sem(k) for k in ("w_loaded", "scaled", "filled", "passed"))
        c_loaded = [sem(f"c_loaded{u}") for u in range(2)]
        h_loaded = [sem(f"h_loaded{u}") for u in range(2)]
        h_stored = [sem(f"h_stored{u}") for u in range(2)]
        x_stored = [sem(f"x_stored{u}") for u in range(2)]
        p_stored = [sem(f"p_stored{u}") for u in range(2)]
        v_stored = [sem(f"v_stored{u}") for u in range(2)]
        S = signals(ctx, nc, "p", cT=1, cT_out=1, y=1, hb=1, h3=1, bn=NT + 1, mv=1, eps=1, rstd=1, xn=NT, xT=1,
                    xT_out=1, v=1, v_out=1, qk=2 * CT, hi=2 * CT, rest=2 * CT, mid=2 * CT, lo=2 * CT)
        banks = [lambda k, u=u: ps[:, 4 * u + k, :] for u in range(2)]
        QK_BANK = (4, 5, 2, 3)
        WEIGHTS = 16 * (4 + 2 * CT + 2)
        block = ctx.enter_context(nc.Block())

        def tokens(dram, n):
            return dram[batch_of(n)].rearrange("(t p) d -> p t d", p=R)

        @block.sync
        def _(sp):
            def load_c(n, u):
                sp.dma_start(cx[:, u], tokens(ctx_dram, n)).then_inc(c_loaded[u], 16)

            def load_h(n, u):
                sp.dma_start(h[:, u], tokens(h2_dram, n)).then_inc(h_loaded[u], 16)

            def next_c(n, u, i):
                if following(n, NB):
                    sp.wait_ge(S["cT"].sem, S["cT"].at(n))
                    sp.sem_inc(passed, 1)
                    load_c((n[0], n[1] + 2), u)

            def store_h(n, u, i):
                sp.wait_ge(S["h3"].sem, S["h3"].at(n))
                sp.sem_inc(passed, 1)
                sp.dma_start(tokens(h3_dram, n), h[:, u]).then_inc(h_stored[u], 16)

            def store_x(n, u, i):
                sp.wait_ge(S["xn"].sem, S["xn"].at(n))
                sp.sem_inc(passed, 1)
                sp.dma_start(tokens(x3_dram, n), xn[:, u]).then_inc(x_stored[u], 16)
                if following(n, NB):
                    sp.wait_ge(h_stored[u], 16 * (i + 1))
                    sp.sem_inc(passed, 1)
                    load_h((n[0], n[1] + 2), u)

            def store_v(n, u, i):
                sp.wait_ge(S["v_out"].sem, S["v_out"].at(n))
                sp.sem_inc(passed, 1)
                sp.dma_start(v_dram[batch_of(n)], vp[:, u].rearrange("p t h w -> p (t h w)")).then_inc(v_stored[u], 16)

            def store_parts(n, u, i):
                for j in range(2 * CT):
                    sp.wait_ge(S["lo"].sem, S["lo"].at(n, j + 1))
                    sp.sem_inc(passed, 1)
                    sp.dma_start(parts_dram[batch_of(n), j // CT, (j % CT) * 128:(j % CT + 1) * 128]
                                 .rearrange("r k t -> r (k t)"),
                                 parts[:, u, j].rearrange("p k t -> p (k t)")).then_inc(p_stored[u], 16)

            sp.dma_start(wqk[:, :, 0], wq_dram.rearrange("(k p) n -> p k n", p=128)).then_inc(w_loaded, 16)
            sp.dma_start(wqk[:, :, 1], wk_dram.rearrange("(k p) n -> p k n", p=128)).then_inc(w_loaded, 16)
            sp.dma_start(proj[:], proj_dram.rearrange("(k p) n -> p k n", p=128)).then_inc(w_loaded, 16)
            sp.dma_start(wv[:], wv_dram.rearrange("(k p) n -> p k n", p=128)).then_inc(w_loaded, 16)
            for j, dram in enumerate((bq_dram, bk_dram)):
                for k in range(CT):
                    sp.dma_start(bqk[:, j, k:k + 1], dram[k * 128:(k + 1) * 128].rearrange("(p a) -> p a", a=1))\
                        .then_inc(w_loaded, 16)
            sp.dma_start(projb[:], row(projb_dram).broadcast_to([R, D])).then_inc(w_loaded, 16)
            sp.dma_start(bv[:], row(bv_dram).broadcast_to([R, D])).then_inc(w_loaded, 16)
            for u in range(2):
                load_c((0, u), u)
                load_h((0, u), u)
            pipeline(sp, NB, ((next_c, 1), (store_v, 0), (store_h, 1), (store_parts, 0), (store_x, 1)))
            for u in range(2):
                for s, times in ((h_stored, 1), (x_stored, 1), (p_stored, 2 * CT), (v_stored, 1)):
                    sp.wait_ge(s[u], 16 * times * (NB // 2))

        @block.gpsimd
        def _(pool):
            for k in ("hb", "eps", "rstd"):
                S[k].give(pool)
            pool.wait_ge(w_loaded, WEIGHTS)

            def add_bias(n, u, i):
                pool.wait_ge(h_loaded[u], 16 * (i + 1))
                nc.gpsimd.tensor_tensor(h[:, u], h[:, u], projb[:].unsqueeze(1).to_broadcast([R, NT, D]), ALU.add)\
                    .then_inc(S["hb"].sem, 1)

            def deviation(n, u, i):
                ln_rstd(nc, pool, c, mv[:, u], var_eps[:, u], rstd[:, u], S["mv"], S["eps"], S["rstd"], n)

            pipeline(pool, NB, ((add_bias, 1), (deviation, 1)))

        @block.scalar
        def _(act):
            for k in ("cT_out", "xT_out", "hi", "mid"):
                S[k].give(act)
            act.wait_ge(scaled, 2)

            def copy_c(n, u, i):
                act.wait_ge(S["cT"].sem, S["cT"].at(n))
                act.wait_ge(S["y"].sem, S["y"].before(n))
                nc.scalar.copy(cT[:, u], ps[:, 2:4, 0:T]).then_inc(S["cT_out"].sem, 1)

            def copy_x(n, u, i):
                act.wait_ge(S["xT"].sem, S["xT"].at(n))
                act.wait_ge(S["qk"].sem, S["qk"].before(n))
                nc.scalar.copy(xT[:, u], ps[:, 4:6, 0:T]).then_inc(S["xT_out"].sem, 1)

            def upper_parts(n, u, i):
                act.wait_ge(p_stored[u], 16 * 2 * CT * i)
                for j in range(2 * CT):
                    act.wait_ge(S["qk"].sem, S["qk"].at(n, j + 1))
                    nc.scalar.activation(parts[:, u, j, 0, :], ps[:, QK_BANK[j], 0:T], ACT.Identity,
                                         bias=bqk[:, j // CT, j % CT:j % CT + 1]).then_inc(S["hi"].sem, 1)
                    if j:
                        second_part(n, u, j - 1)
                second_part(n, u, 2 * CT - 1)

            def second_part(n, u, j):
                act.wait_ge(S["rest"].sem, S["rest"].at(n, j + 1))
                nc.scalar.copy(parts[:, u, j, 1, :], rest[:, u, j % 2]).then_inc(S["mid"].sem, 1)

            pipeline(act, NB, ((copy_x, 0), (copy_c, 1), (upper_parts, 0)))

        @block.vector
        def _(dve):
            for k in ("h3", "bn", "mv", "xn", "v_out", "rest", "lo"):
                S[k].give(dve)
            dve.wait_ge(w_loaded, WEIGHTS)
            nc.vector.tensor_scalar(wqk[:, :, 0], wqk[:, :, 0], float(HD) ** -0.5, None, ALU.mult).then_inc(scaled, 1)
            nc.vector.tensor_scalar(bqk[:, 0], bqk[:, 0], float(HD) ** -0.5, None, ALU.mult).then_inc(scaled, 1)
            nc.vector.memset(vp[:], 1.0).then_inc(filled, 1)
            dve.wait_ge(filled, 1)
            dve.wait_ge(scaled, 2)

            def residual(n, u, i):
                dve.wait_ge(S["y"].sem, S["y"].at(n))
                dve.wait_ge(S["hb"].sem, S["hb"].at(n))
                nc.vector.tensor_tensor(h[:, u, 0:2, :], ps[0:R, 0, :].rearrange("p (t d) -> p t d", t=2),
                                        h[:, u, 0:2, :], ALU.add)
                nc.vector.tensor_tensor(h[:, u, 2, :], ps[0:R, 1, 0:D], h[:, u, 2, :], ALU.add)\
                    .then_inc(S["h3"].sem, 1)
                dve.wait_ge(S["h3"].sem, S["h3"].at(n))
                ln_stats(nc, dve, h[:, u], stats[:, u], mv[:, u], (S["bn"].sem, S["bn"].at(n)), S["mv"])

            def normalise(n, u, i):
                dve.wait_ge(S["rstd"].sem, S["rstd"].at(n))
                dve.wait_ge(S["xT"].sem, S["xT"].before(n))
                dve.wait_ge(x_stored[u], 16 * i)
                ln_apply(nc, xn[:, u], h[:, u], mv[:, u], rstd[:, u], S["xn"])

            def values(n, u, i):
                dve.wait_ge(S["v"].sem, S["v"].at(n))
                dve.wait_ge(v_stored[u], 16 * i)
                bias = bv[:].rearrange("p (h w) -> p h w", w=HD)
                for t in range(NT):
                    x = ps[0:R, 6 + t // 2, (t % 2) * D:(t % 2 + 1) * D].rearrange("p (h w) -> p h w", w=HD)
                    last = nc.vector.tensor_tensor(vp[:, u, t, :, 0:HD], x, bias, ALU.add)
                last.then_inc(S["v_out"].sem, 1)

            def lower_parts(n, u, i, tiles):
                for j in tiles:
                    dve.wait_ge(S["hi"].sem, S["hi"].at(n, j + 1))
                    if j >= 2:
                        dve.wait_ge(S["lo"].sem, S["lo"].at(n, j - 1))
                    nc.vector.scalar_tensor_tensor(out=rest[:, u, j % 2], in0=ps[:, QK_BANK[j], 0:T],
                                                   scalar=bqk[:, j // CT, j % CT:j % CT + 1],
                                                   in1=parts[:, u, j, 0, :], op0=ALU.add, op1=ALU.subtract)\
                        .then_inc(S["rest"].sem, 1)
                    if j > tiles[0]:
                        third_part(n, u, j - 1)
                third_part(n, u, tiles[-1])

            def lower_parts_q(n, u, i):
                lower_parts(n, u, i, range(CT))

            def lower_parts_k(n, u, i):
                lower_parts(n, u, i, range(CT, 2 * CT))

            def third_part(n, u, j):
                dve.wait_ge(S["mid"].sem, S["mid"].at(n, j + 1))
                nc.vector.tensor_tensor(parts[:, u, j, 2, :], rest[:, u, j % 2], parts[:, u, j, 1, :],
                                        ALU.subtract).then_inc(S["lo"].sem, 1)

            pipeline(dve, NB, ((values, 0), (residual, 1), (lower_parts_q, 0), (normalise, 1),
                               (lower_parts_k, 0)))

        @block.tensor
        def _(pe):
            for k in ("cT", "y", "xT", "v", "qk"):
                S[k].give(pe)
            pe.wait_ge(w_loaded, WEIGHTS)
            pe.wait_ge(scaled, 1)

            def turn_x(n, u, i):
                pe.wait_ge(S["xn"].sem, S["xn"].at(n))
                pe.wait_ge(S["rest"].sem, S["rest"].at((n[0], n[1] - 1), 2))
                transpose_tokens(nc, pe, c, xn[:, u], lambda k: ps[:, 4 + k, :]).then_inc(S["xT"].sem, 1)

            def turn_c(n, u, i):
                pe.wait_ge(c_loaded[u], 16 * (i + 1))
                pe.wait_ge(S["rest"].sem, S["rest"].at((n[0], n[1] - 2)))
                transpose_tokens(nc, pe, c, cx[:, u], lambda k: ps[:, 2 + k, :]).then_inc(S["cT"].sem, 1)

            def values(n, u, i):
                pe.wait_ge(S["xT_out"].sem, S["xT_out"].at(n))
                pe.wait_ge(S["v_out"].sem, S["v_out"].at((n[0], n[1] - 1)))
                for t in range(NT):
                    for k in range(CT):
                        last = nc.tensor.matmul(ps[0:R, 6 + t // 2, (t % 2) * D:(t % 2 + 1) * D],
                                                xT[:, u, k, t * R:(t + 1) * R], wv[:, k, :],
                                                start=(k == 0), stop=(k == CT - 1))
                last.then_inc(S["v"].sem, 1)

            def project(n, u, i):
                pe.wait_ge(S["cT_out"].sem, S["cT_out"].at(n))
                pe.wait_ge(S["h3"].sem, S["h3"].at((n[0], n[1] - 1)))
                for t in range(NT):
                    for k in range(CT):
                        last = nc.tensor.matmul(ps[0:R, t // 2, (t % 2) * D:(t % 2 + 1) * D],
                                                cT[:, u, k, t * R:(t + 1) * R], proj[:, k, :],
                                                start=(k == 0), stop=(k == CT - 1))
                last.then_inc(S["y"].sem, 1)

            def queries_and_keys(n, u, i):
                for j in range(2 * CT):
                    if j == 2 and (not isinstance(n[0], int) or 2 * n[0] + n[1] + 1 < NB):
                        pe.wait_ge(S["cT_out"].sem, S["cT_out"].at((n[0], n[1] + 1)))
                    for k in range(CT):
                        last = nc.tensor.matmul(ps[:, QK_BANK[j], 0:T],
                                                wqk[:, k, j // CT, (j % CT) * 128:(j % CT + 1) * 128],
                                                xT[:, u, k, :], start=(k == 0), stop=(k == CT - 1))
                    last.then_inc(S["qk"].sem, 1)

            pipeline(pe, NB, ((turn_x, 0), (turn_c, 1), (values, 0), (project, 1), (queries_and_keys, 0)))


def phase_g3(nc, c, ps, NB, ctx_dram, x3_dram, h3_dram, wo_dram, bo_dram, g1_dram, be1_dram, wg_dram, bg_dram,
             we_dram, bexp_dram, g2_dram, be2_dram, out_dram):
    ctx = ExitStack()
    E, PAIRS = EXPERTS, EXPERTS // 2
    M = PAIRS * NT
    EBANK = (4, 5, 6, 7)
    with ctx:
        def sb(name, shape, dt=F32):
            return ctx.enter_context(nc.sbuf_tensor("m_" + name, shape, dt))

        def sem(name):
            return nc.alloc_semaphore("m_" + name)

        wo, wg = sb("wo", [128, CT, D]), sb("wg", [128, CT, E])
        we = sb("we", [128, CT, E, D])
        bexp = sb("bexp", [E, D])
        rows = {k: sb(k, [R, D]) for k in ("bo", "g1", "be1", "g2", "be2")}
        bg = sb("bg", [R, E])
        lower = sb("lower", [R, E, E])
        cx = sb("cx", [R, 2, NT, D])
        x = sb("x", [R, 2, NT, D])
        h = sb("h", [R, 2, NT, D])
        cT = sb("cT", [128, 2, CT, T])
        xT = sb("xT", [128, 2, CT, T])
        a = sb("a", [R, 2, NT, D])
        ag = sb("ag", [R, 2, NT, D])
        acc = sb("acc", [R, 2, NT, D])
        accg = sb("accg", [R, 2, NT, D])
        stats = sb("stats", [R, 2, NT, 6])
        mv = sb("mv", [R, 2, NT, 2])
        var_eps = sb("var_eps", [R, 2, NT])
        rstd = sb("rstd", [R, 2, NT])
        logit = sb("logit", [R, NT, E])
        top = sb("top", [R, NT])
        shifted = sb("shifted", [R, NT, E])
        expl = sb("expl", [R, NT, E])
        total = sb("total", [R, NT])
        greater = sb("greater", [R, NT, E, E])
        equal = sb("equal", [R, NT, E, E])
        rank = sb("rank", [R, NT, E])
        chosen = sb("chosen", [R, NT, E])
        weight = sb("weight", [R, 2, NT, E])
        weightT = sb("weightT", [E, 2, T])
        w_loaded, filled, passed = sem("w_loaded"), sem("filled"), sem("passed")
        c_loaded = [sem(f"c_loaded{u}") for u in range(2)]
        x_loaded = [sem(f"x_loaded{u}") for u in range(2)]
        h_loaded = [sem(f"h_loaded{u}") for u in range(2)]
        stored = [sem(f"stored{u}") for u in range(2)]
        S = signals(ctx, nc, "m", cT=1, cT_out=1, y=1, xb=1, hb=1, a=1, bn=NT + 1, mv=1, eps=1, rstd=1, an=NT,
                    ag=1, x4=1, xT=1, xT_out=1, gl=1, logit=1, wT=1, wT_out=1, bias=1, acc0=1, me=M, acc=2 * M,
                    hx=1, bn2=NT + 1, mv2=1, eps2=1, rstd2=1, accn=NT, accg=1, out=1,
                    top=1, shifted=1, exp=1, greater=1, equal=1, lower=1, above=1, rank=1,
                    total=1, inv=1, chosen=1, weight=1)
        block = ctx.enter_context(nc.Block())

        def tokens(dram, n):
            return dram[batch_of(n)].rearrange("(t p) d -> p t d", p=R)

        def banks01(t):
            return ps[0:R, t // 2, (t % 2) * D:(t % 2 + 1) * D]

        @block.sync
        def _(sp):
            def load(dst, dram, n, u, loaded):
                sp.dma_start(dst[:, u], tokens(dram, n)).then_inc(loaded[u], 16)

            def next_c(n, u, i):
                if following(n, NB):
                    sp.wait_ge(S["cT"].sem, S["cT"].at(n))
                    sp.sem_inc(passed, 1)
                    load(cx, ctx_dram, (n[0], n[1] + 2), u, c_loaded)

            def next_x(n, u, i):
                if following(n, NB):
                    sp.wait_ge(S["xT"].sem, S["xT"].at(n))
                    sp.sem_inc(passed, 1)
                    sp.wait_ge(S["hx"].sem, S["hx"].at(n))
                    sp.sem_inc(passed, 1)
                    load(x, x3_dram, (n[0], n[1] + 2), u, x_loaded)

            def store(n, u, i):
                sp.wait_ge(S["out"].sem, S["out"].at(n))
                sp.sem_inc(passed, 1)
                sp.dma_start(tokens(out_dram, n), h[:, u]).then_inc(stored[u], 16)
                if following(n, NB):
                    sp.wait_ge(stored[u], 16 * (i + 1))
                    sp.sem_inc(passed, 1)
                    load(h, h3_dram, (n[0], n[1] + 2), u, h_loaded)

            sp.dma_start(wo[:], wo_dram.rearrange("(k p) n -> p k n", p=128)).then_inc(w_loaded, 16)
            sp.dma_start(wg[:], wg_dram.rearrange("(k p) n -> p k n", p=128)).then_inc(w_loaded, 16)
            for e in range(E):
                sp.dma_start(we[:, :, e], we_dram[e].rearrange("(k p) n -> p k n", p=128)).then_inc(w_loaded, 16)
            sp.dma_start(bexp[:], bexp_dram).then_inc(w_loaded, 16)
            for k, dram in (("bo", bo_dram), ("g1", g1_dram), ("be1", be1_dram), ("g2", g2_dram), ("be2", be2_dram)):
                sp.dma_start(rows[k][:], row(dram).broadcast_to([R, D])).then_inc(w_loaded, 16)
            sp.dma_start(bg[:], row(bg_dram).broadcast_to([R, E])).then_inc(w_loaded, 16)
            for u in range(2):
                load(cx, ctx_dram, (0, u), u, c_loaded)
                load(x, x3_dram, (0, u), u, x_loaded)
                load(h, h3_dram, (0, u), u, h_loaded)
            pipeline(sp, NB, ((next_c, 1), (store, -1), (next_x, 1)))
            for u in range(2):
                sp.wait_ge(stored[u], 16 * (NB // 2))

        WEIGHTS = 16 * (2 + E + 1 + 5 + 1)

        def everywhere(k):
            return rows[k][:].unsqueeze(1).to_broadcast([R, NT, D])

        @block.gpsimd
        def _(pool):
            for k in ("xb", "hb", "eps", "rstd", "hx", "eps2", "rstd2"):
                S[k].give(pool)
            nc.gpsimd.memset(lower[:], 1.0).then_inc(filled, 1)
            pool.wait_ge(filled, 1)
            nc.gpsimd.affine_select(out=lower[:], in_=lower[:], compare_op=ALU.is_gt, fill=0.0, base=0,
                                    pattern=[[1, E], [-1, E]], channel_multiplier=0).then_inc(filled, 1)
            pool.wait_ge(w_loaded, WEIGHTS)

            def add_be1(n, u, i):
                pool.wait_ge(x_loaded[u], 16 * (i + 1))
                nc.gpsimd.tensor_tensor(x[:, u], x[:, u], everywhere("be1"), ALU.add).then_inc(S["xb"].sem, 1)

            def deviation1(n, u, i):
                ln_rstd(nc, pool, c, mv[:, u], var_eps[:, u], rstd[:, u], S["mv"], S["eps"], S["rstd"], n)

            def deviation2(n, u, i):
                ln_rstd(nc, pool, c, mv[:, u], var_eps[:, u], rstd[:, u], S["mv2"], S["eps2"], S["rstd2"], n)

            def add_be2(n, u, i):
                pool.wait_ge(h_loaded[u], 16 * (i + 1))
                nc.gpsimd.tensor_tensor(h[:, u], h[:, u], everywhere("be2"), ALU.add).then_inc(S["hb"].sem, 1)

            def add_x4(n, u, i):
                pool.wait_ge(S["hb"].sem, S["hb"].at(n))
                pool.wait_ge(S["x4"].sem, S["x4"].at(n))
                nc.gpsimd.tensor_tensor(h[:, u], h[:, u], x[:, u], ALU.add).then_inc(S["hx"].sem, 1)

            pipeline(pool, NB, ((deviation2, -1), (add_be1, 1), (deviation1, 1), (add_be2, 1), (add_x4, 1)))

        @block.scalar
        def _(act):
            for k in ("cT_out", "xT_out", "exp", "wT_out", "acc0"):
                S[k].give(act)

            def copy_c(n, u, i):
                act.wait_ge(S["cT"].sem, S["cT"].at(n))
                act.wait_ge(S["y"].sem, S["y"].before(n))
                nc.scalar.copy(cT[:, u], ps[:, 2:4, 0:T]).then_inc(S["cT_out"].sem, 1)

            def copy_x(n, u, i):
                act.wait_ge(S["xT"].sem, S["xT"].at(n))
                act.wait_ge(S["me"].sem, S["me"].before(n))
                nc.scalar.copy(xT[:, u], ps[:, 2:4, 0:T]).then_inc(S["xT_out"].sem, 1)

            def exponentials(n, u, i):
                act.wait_ge(S["shifted"].sem, S["shifted"].at(n))
                act.wait_ge(S["chosen"].sem, S["chosen"].at((n[0], n[1] - 1)))
                nc.scalar.activation(expl[:], shifted[:], ACT.Exp).then_inc(S["exp"].sem, 1)

            def copy_weights(n, u, i):
                act.wait_ge(S["wT"].sem, S["wT"].at(n))
                act.wait_ge(S["bias"].sem, S["bias"].before(n))
                nc.scalar.copy(weightT[:, u], ps[0:E, 1, 0:T]).then_inc(S["wT_out"].sem, 1)

            def start_sum(n, u, i):
                act.wait_ge(S["bias"].sem, S["bias"].at(n))
                act.wait_ge(S["accg"].sem, S["accg"].before(n))
                nc.scalar.copy(acc[:, u, 0:2], ps[0:R, 0, :].rearrange("p (t d) -> p t d", t=2))
                nc.scalar.copy(acc[:, u, 2], ps[0:R, 1, 0:D]).then_inc(S["acc0"].sem, 1)

            pipeline(act, NB, ((copy_c, 1), (copy_x, 1), (exponentials, 1), (copy_weights, 1), (start_sum, 1)))

        @block.vector
        def _(dve):
            for k in ("a", "bn", "mv", "an", "ag", "x4", "logit", "acc", "bn2", "mv2", "accn", "accg", "out",
                      "top", "shifted", "greater", "equal", "lower", "above", "rank", "total", "inv", "chosen",
                      "weight"):
                S[k].give(dve)
            dve.wait_ge(w_loaded, WEIGHTS)
            dve.wait_ge(filled, 2)

            def add_bo(n, u, i):
                dve.wait_ge(S["y"].sem, S["y"].at(n))
                dve.wait_ge(S["ag"].sem, S["ag"].before(n))
                for t in range(NT):
                    last = nc.vector.tensor_tensor(a[:, u, t], banks01(t), rows["bo"][:], ALU.add)
                last.then_inc(S["a"].sem, 1)
                dve.wait_ge(S["a"].sem, S["a"].at(n))
                ln_stats(nc, dve, a[:, u], stats[:, u], mv[:, u], (S["bn"].sem, S["bn"].at(n)), S["mv"])

            def finish_x4(n, u, i):
                dve.wait_ge(S["rstd"].sem, S["rstd"].at(n))
                ln_apply(nc, a[:, u], a[:, u], mv[:, u], rstd[:, u], S["an"])
                dve.wait_ge(S["an"].sem, S["an"].at(n))
                dve.wait_ge(S["x4"].sem, S["x4"].before(n))
                nc.vector.tensor_tensor(ag[:, u], a[:, u], everywhere("g1"), ALU.mult).then_inc(S["ag"].sem, 1)
                dve.wait_ge(S["ag"].sem, S["ag"].at(n))
                dve.wait_ge(S["xb"].sem, S["xb"].at(n))
                nc.vector.tensor_tensor(x[:, u], x[:, u], ag[:, u], ALU.add).then_inc(S["x4"].sem, 1)

            every = [R, NT, E, E]

            def rank_logits(n, u, i):
                other, own = logit[:].unsqueeze(2).to_broadcast(every), logit[:].unsqueeze(3).to_broadcast(every)
                dve.wait_ge(S["gl"].sem, S["gl"].at(n))
                nc.vector.tensor_tensor(logit[:], ps[0:R, 1, D:D + NT * E].rearrange("p (t e) -> p t e", e=E),
                                        bg[:].unsqueeze(1).to_broadcast([R, NT, E]), ALU.add)\
                    .then_inc(S["logit"].sem, 1)
                dve.wait_ge(S["logit"].sem, S["logit"].at(n))
                nc.vector.reduce_max(top[:], logit[:], AX.X).then_inc(S["top"].sem, 1)
                nc.vector.tensor_tensor(equal[:], other, own, ALU.is_equal).then_inc(S["equal"].sem, 1)
                dve.wait_ge(S["top"].sem, S["top"].at(n))
                nc.vector.tensor_tensor(shifted[:], logit[:], top[:].unsqueeze(2).to_broadcast([R, NT, E]),
                                        ALU.subtract).then_inc(S["shifted"].sem, 1)
                nc.vector.tensor_tensor(greater[:], other, own, ALU.is_gt).then_inc(S["greater"].sem, 1)
                dve.wait_ge(S["equal"].sem, S["equal"].at(n))
                nc.vector.tensor_tensor(equal[:], equal[:], lower[:].unsqueeze(1).to_broadcast(every), ALU.mult)\
                    .then_inc(S["lower"].sem, 1)
                dve.wait_ge(S["greater"].sem, S["greater"].at(n))
                dve.wait_ge(S["lower"].sem, S["lower"].at(n))
                nc.vector.tensor_tensor(equal[:], equal[:], greater[:], ALU.add).then_inc(S["above"].sem, 1)
                dve.wait_ge(S["above"].sem, S["above"].at(n))
                nc.vector.reduce_sum(rank[:], equal[:], AX.X).then_inc(S["rank"].sem, 1)

            def weigh(n, u, i):
                dve.wait_ge(S["exp"].sem, S["exp"].at(n))
                nc.vector.reduce_sum(total[:], expl[:], AX.X).then_inc(S["total"].sem, 1)
                dve.wait_ge(S["rank"].sem, S["rank"].at(n))
                nc.vector.scalar_tensor_tensor(out=chosen[:], in0=rank[:], scalar=2.0, in1=expl[:],
                                               op0=ALU.is_lt, op1=ALU.mult).then_inc(S["chosen"].sem, 1)
                dve.wait_ge(S["total"].sem, S["total"].at(n))
                nc.vector.reciprocal(total[:], total[:]).then_inc(S["inv"].sem, 1)
                dve.wait_ge(S["inv"].sem, S["inv"].at(n))
                dve.wait_ge(S["chosen"].sem, S["chosen"].at(n))
                nc.vector.tensor_tensor(weight[:, u], chosen[:], total[:].unsqueeze(2).to_broadcast([R, NT, E]),
                                        ALU.mult).then_inc(S["weight"].sem, 1)

            def add_experts(first, end):
                def stage(n, u, i):
                    if first == 0:
                        dve.wait_ge(S["acc0"].sem, S["acc0"].at(n))
                        dve.wait_ge(S["weight"].sem, S["weight"].at(n))
                    for m in range(first, end):
                        p, t = divmod(m, NT)
                        dve.wait_ge(S["me"].sem, S["me"].at(n, m + 1))
                        for j in range(2):
                            if m >= NT or j:
                                dve.wait_ge(S["acc"].sem, S["acc"].at(n, 2 * m + 1 if j else 2 * (m - NT) + 2))
                            nc.vector.scalar_tensor_tensor(out=acc[:, u, t],
                                                           in0=ps[0:R, EBANK[m % 4], j * D:(j + 1) * D],
                                                           scalar=weight[:, u, t, 2 * p + j:2 * p + j + 1],
                                                           in1=acc[:, u, t], op0=ALU.mult, op1=ALU.add)\
                                .then_inc(S["acc"].sem, 1)
                return stage

            def statistics2(n, u, i):
                dve.wait_ge(S["acc"].sem, S["acc"].at(n))
                dve.wait_ge(S["an"].sem, S["an"].at(n))
                ln_stats(nc, dve, acc[:, u], stats[:, u], mv[:, u], (S["bn2"].sem, S["bn2"].at(n)), S["mv2"])

            def finish(n, u, i):
                dve.wait_ge(S["rstd2"].sem, S["rstd2"].at(n))
                ln_apply(nc, acc[:, u], acc[:, u], mv[:, u], rstd[:, u], S["accn"])
                dve.wait_ge(S["accn"].sem, S["accn"].at(n))
                dve.wait_ge(S["out"].sem, S["out"].before(n))
                nc.vector.tensor_tensor(accg[:, u], acc[:, u], everywhere("g2"), ALU.mult).then_inc(S["accg"].sem, 1)
                dve.wait_ge(S["accg"].sem, S["accg"].at(n))
                dve.wait_ge(S["hx"].sem, S["hx"].at(n))
                nc.vector.tensor_tensor(h[:, u], h[:, u], accg[:, u], ALU.add).then_inc(S["out"].sem, 1)

            pipeline(dve, NB, ((add_experts(0, 2), 0), (finish, -1), (add_bo, 1), (add_experts(2, 4), 0),
                               (finish_x4, 1), (add_experts(4, 7), 0), (rank_logits, 1), (add_experts(7, 9), 0),
                               (weigh, 1), (add_experts(9, M), 0), (statistics2, 0)))

        @block.tensor
        def _(pe):
            for k in ("cT", "y", "xT", "gl", "me", "wT", "bias"):
                S[k].give(pe)
            pe.wait_ge(w_loaded, WEIGHTS)

            def turn_c(n, u, i):
                pe.wait_ge(c_loaded[u], 16 * (i + 1))
                pe.wait_ge(S["xT_out"].sem, S["xT_out"].at((n[0], n[1] - 1)))
                transpose_tokens(nc, pe, c, cx[:, u], lambda k: ps[:, 2 + k, :]).then_inc(S["cT"].sem, 1)

            def project(n, u, i):
                pe.wait_ge(S["cT_out"].sem, S["cT_out"].at(n))
                pe.wait_ge(S["acc0"].sem, S["acc0"].at((n[0], n[1] - 1)))
                for t in range(NT):
                    for k in range(CT):
                        last = nc.tensor.matmul(banks01(t), cT[:, u, k, t * R:(t + 1) * R], wo[:, k, :],
                                                start=(k == 0), stop=(k == CT - 1))
                last.then_inc(S["y"].sem, 1)

            def turn_x4(n, u, i):
                pe.wait_ge(S["x4"].sem, S["x4"].at(n))
                transpose_tokens(nc, pe, c, x[:, u], lambda k: ps[:, 2 + k, :]).then_inc(S["xT"].sem, 1)

            def gate(n, u, i):
                pe.wait_ge(S["xT_out"].sem, S["xT_out"].at(n))
                for t in range(NT):
                    for k in range(CT):
                        last = nc.tensor.matmul(ps[0:R, 1, D + t * E:D + (t + 1) * E],
                                                xT[:, u, k, t * R:(t + 1) * R], wg[:, k, :],
                                                start=(k == 0), stop=(k == CT - 1))
                last.then_inc(S["gl"].sem, 1)

            def experts(first, end):
                def stage(n, u, i):
                    for m in range(first, end):
                        p, t = divmod(m, NT)
                        pe.wait_ge(S["acc"].sem, S["acc"].at(n, 2 * (m - 4) + 2))
                        for k in range(CT):
                            last = nc.tensor.matmul(ps[0:R, EBANK[m % 4], :], xT[:, u, k, t * R:(t + 1) * R],
                                                    we[:, k, 2 * p:2 * p + 2, :].rearrange("p e d -> p (e d)"),
                                                    start=(k == 0), stop=(k == CT - 1))
                        last.then_inc(S["me"].sem, 1)
                return stage

            def turn_weights(n, u, i):
                pe.wait_ge(S["weight"].sem, S["weight"].at(n))
                for t in range(NT):
                    last = nc.tensor.transpose(ps[0:E, 1, t * R:(t + 1) * R], weight[:, u, t, :],
                                               c["ident"][0:R, 0:R])
                last.then_inc(S["wT"].sem, 1)

            def weigh_biases(n, u, i):
                pe.wait_ge(S["wT_out"].sem, S["wT_out"].at(n))
                for t in range(NT):
                    last = nc.tensor.matmul(banks01(t), weightT[:, u, t * R:(t + 1) * R], bexp[:],
                                            start=True, stop=True)
                last.then_inc(S["bias"].sem, 1)

            pipeline(pe, NB, ((turn_c, 1), (experts(0, 2), 0), (project, 1), (experts(2, 6), 0), (turn_x4, 1),
                              (experts(6, 7), 0), (gate, 1), (experts(7, M - 1), 0), (turn_weights, 1),
                              (experts(M - 1, M), 0), (weigh_biases, 1)))


def program(nc, NB, patches, txt, rot, wtok, a_wq, a_wk, a_wv, a_wo, gate_w, up_w, down_w,
            wqkv, curv, proj, projb, f_wq, f_bq, f_wk, f_bk, f_wv, f_bv, f_wo, f_bo, g1, be1, g2, be2,
            wg, bg, we, bexp, out):
    def scratch(name, shape, dt=F32):
        return nc.dram_tensor("s_" + name, shape, dt, kind="Internal").ap()

    tokens = [NB, T, D]
    h1, h2, h3, x3, ctx1, ctx2 = (scratch(n, tokens) for n in ("h1", "h2", "h3", "x3", "ctx1", "ctx2"))
    x0 = scratch("x0", [NB, D, T])
    gate, up, gated, o = (scratch(n, [NB, 128, FT * T]) for n in ("gate", "up", "gated", "o"))
    parts1 = scratch("parts1", [NB, 2, H * HD1, PARTS, T], BF16)
    parts2 = scratch("parts2", [NB, 2, H * HD, PARTS, T], BF16)
    v1, v2 = (scratch(n, [NB, R, NT * H * VW]) for n in ("v1", "v2"))
    ctx = ExitStack()
    with ctx:
        ps = ctx.enter_context(nc.psum_tensor("ps", [128, 8, 512], F32))

        def run(stage, *args):
            with nc.cleanup_on_exit():
                stage(nc, *args)

        c = setup_constants(nc, ctx, rot)
        with ExitStack() as ffn:
            def sb(name, shape):
                return ffn.enter_context(nc.sbuf_tensor("k_" + name, shape, F32))

            gateT, upT, downT = sb("gateT", [128, CT, FF]), sb("upT", [128, CT, FF]), sb("downT", [128, FT, D])
            quantised = ("x", "gate", "up", "gated", "o")
            amax = {k: sb("amax_" + k, [128, 2]) for k in quantised}
            scale = {k: sb("scale_" + k, [128, 1]) for k in quantised}
            inv = {k: sb("inv_" + k, [128, 1]) for k in quantised}
            magic = sb("magic", [128, 1])
            with nc.Block() as block:
                @block.vector
                def _(dve):
                    nc.vector.memset(magic[:], MAGIC)
                    for k in quantised:
                        nc.vector.memset(amax[k][:], 0.0)

            def fix_scale(k):
                run(set_scale, "z_" + k, amax[k][:], scale[k][:], inv[k][:])

            run(quantise_weights, c, ps, gate_w, up_w, down_w, gateT, upT, downT)
            run(phase_a, c, ps, NB, patches, txt, wtok, a_wq, a_wk, a_wv, a_wo, h1, x0, amax["x"][0:R])
            fix_scale("x")
            run(phase_b, ps, NB, magic[:], x0, gateT, upT, scale["x"][:], inv["x"][:], gate, up,
                    amax["gate"], amax["up"])
            fix_scale("gate")
            fix_scale("up")
            run(phase_c, NB, magic[:], gate, scale["gate"][:], inv["gate"][:], gated, amax["gated"])
            fix_scale("gated")
            run(phase_d, NB, magic[:], gated, up, scale["gated"][:], inv["gated"][:], scale["up"][:], inv["up"][:],
                    o, amax["o"])
            fix_scale("o")
            run(phase_f1, c, ps, NB, magic[:], o, h1, downT, scale["o"][:], inv["o"][:], wqkv, curv, h2, parts1, v1)
        run(attention_core, c, ps, NB, "g", KINDS, True, HD1, parts1, v1, ctx1, curv)
        run(phase_g1, c, ps, NB, ctx1, h2, proj, projb, f_wq, f_wk, f_wv, f_bq, f_bk, f_bv, h3, x3, parts2, v2)
        run(attention_core, c, ps, NB, "e", [SDPA] * H, False, HD, parts2, v2, ctx2)
        run(phase_g3, c, ps, NB, ctx2, x3, h3, f_wo, f_bo, g1, be1, wg, bg, we, bexp, g2, be2, out)


def kernel(**inputs):
    import concourse.bacc as bacc
    from concourse.bass_utils import run_bass_kernel_spmd

    a = {k: np.asarray(v) for k, v in inputs.items()}
    NB = a["x"].shape[0]
    P = 16
    side = a["x"].shape[-1] // P
    patches = a["x"].reshape(NB, 3, side, P, side, P).transpose(0, 1, 3, 5, 2, 4).reshape(NB, 3 * P * P, side * side)
    frequencies = 1.0 / 10000.0 ** (np.arange(0, HD, 2, dtype=np.float32) / HD)
    angles = np.outer(np.arange(T, dtype=np.float32), frequencies).astype(np.float32)
    cos, sin = np.cos(angles), np.sin(angles)
    rot = np.stack([np.concatenate([cos, cos], 1), np.concatenate([sin, -sin], 1)]).astype(np.float32)

    def ffn(*names):
        return [a["L1_ffn_" + k] for k in names]

    arrays = [patches, a["txt"], rot, a["L0_tok_W"].T] + [a["L0_attn_W" + k] for k in "qkvo"]
    arrays += [a["L0_ffn_w_" + k] for k in ("gate", "up", "down")]
    arrays += [a["L1_attn_qkv_w"].T, a["L1_attn_curvature"].reshape(4), a["L1_attn_proj_w"].T, a["L1_attn_proj_b"]]
    arrays += ffn("Wq", "bq", "Wk", "bk", "Wv", "bv", "Wo", "bo", "g1", "be1", "g2", "be2", "Wg", "bg", "We", "bexp")
    nc = bacc.Bacc("TRN2", target_bir_lowering=False, num_devices=1)
    named, args = {}, []
    for i, x in enumerate(arrays):
        x = np.ascontiguousarray(x)
        named[f"in_{i}"] = x
        args.append(nc.dram_tensor(f"in_{i}", x.shape, mybir.dt.from_np(x.dtype), kind="ExternalInput").ap())
    args.append(nc.dram_tensor("out_0", [NB, T, D], F32, kind="ExternalOutput").ap())
    program(nc, NB, *args)
    return run_bass_kernel_spmd(nc, [named], core_ids=[0]).results[0]["out_0"]
```
